# Optimizing a Trainium2 kernel written in Bass

```python
import numpy as np
import jax
import jax.numpy as jnp

def _softmax(x, axis=-1):
    return jax.nn.softmax(x, axis=axis)

def _gelu(x):
    return jax.nn.gelu(x, approximate=True)

def _silu(x):
    return jax.nn.silu(x)

def _sigmoid(x):
    return jax.nn.sigmoid(x)

def _layernorm(x, axis=-1, eps=1e-05):
    m = jnp.mean(x, axis=axis, keepdims=True)
    v = jnp.var(x, axis=axis, keepdims=True)
    return (x - m) / jnp.sqrt(v + eps)

def _scatter_add(tgt, idx, src, axis=0):
    return tgt.at[idx].add(src)

def _segment_sum(src, seg, n):
    return jax.ops.segment_sum(src, seg, n)
kernel_name = 'mk_decoder_preln_d1_seqx_r4_daf4ae'

def setup_inputs(seed: int=0):
    np.random.seed(seed)
    _w = jnp.asarray

    def _rec_inputs():
        import jax
        import jax.numpy as jnp
        _rk = jax.random.key(seed)
        x = -0.000125 + 0.9999 * jax.random.normal(jax.random.fold_in(_rk, 1), (2, 512, 1024), jnp.float32)
        _lenS = 512 - jax.random.randint(jax.random.fold_in(_rk, 7), (2,), 0, max(1, 512 // 4) + 1, jnp.int32)
        _lenS2 = 1024 - jax.random.randint(jax.random.fold_in(_rk, 8), (2,), 0, max(1, 1024 // 4) + 1, jnp.int32)
        _ctx_4096P = jax.random.normal(jax.random.fold_in(_rk, 11), (2, 16, 1024), jnp.float32)
        _ctx_4096c = jax.random.dirichlet(jax.random.fold_in(_rk, 511), 0.3 * jnp.ones((16,), jnp.float32), (2, 1024))
        _ctx_4096t = jnp.einsum('bsk,bkd->bsd', _ctx_4096c, _ctx_4096P)
        _ctx_4096t = _ctx_4096t * jax.lax.rsqrt(jnp.mean(jnp.square(_ctx_4096t)) + 1e-12) * 0.953939
        ctx_4096 = -5.72187e-05 + 0.999849 * (_ctx_4096t + 0.3 * jax.random.normal(jax.random.fold_in(_rk, 611), (2, 1024, 1024), jnp.float32))
        return (x, ctx_4096)
    x, ctx_4096 = _rec_inputs()

    def _L0_attn_setup():
        import jax, jax.numpy as jnp
        import numpy as np
        H = 1024
        D = H // 4
        key = jax.random.key(seed)
        k1, k2, k3, k4, k5 = jax.random.split(key, 5)
        x = jax.random.normal(k1, (4, 1024, H), dtype=jnp.float32)
        s_in = 1.0 / np.sqrt(H)
        Wqkv = jax.random.normal(k2, (H, 3 * D), dtype=jnp.float32) * s_in
        bqkv = jax.random.normal(k3, (3 * D,), dtype=jnp.float32) * 0.01
        Wo = jax.random.normal(k4, (D, H), dtype=jnp.float32) * (1.0 / np.sqrt(D))
        bo = jax.random.normal(k5, (H,), dtype=jnp.float32) * 0.01
        return {'x': x, 'Wqkv': Wqkv, 'bqkv': bqkv, 'Wo': Wo, 'bo': bo}
    _L0_attn_all = _L0_attn_setup()
    _L0_attn_in = {k: v for k, v in _L0_attn_all.items() if k in ('Wqkv', 'bqkv', 'Wo', 'bo')}
    del _L0_attn_all

    def _L0_xattn_setup():
        import jax, jax.numpy as jnp
        import numpy as np
        QMIN = 0.0
        QMAX = 255.0

        def fake_quant(x, scale, zp):
            s = scale.reshape(())
            z = zp.reshape(())
            q = jnp.clip(jnp.round(x / s + z), QMIN, QMAX)
            return (q - z) * s
        key = jax.random.key(seed)
        k1, k2 = jax.random.split(key)
        B, M, K, N = (4, 512, 1024, 1024)
        x1 = jax.random.normal(k1, (B, M, K), dtype=jnp.float32)
        x2 = jax.random.normal(k2, (B, K, N), dtype=jnp.float32)
        x1_scale = jnp.full((1,), 8.0 / 255.0, dtype=jnp.float32)
        x1_zp = jnp.full((1,), 128.0, dtype=jnp.float32)
        x2_scale = jnp.full((1,), 8.0 / 255.0, dtype=jnp.float32)
        x2_zp = jnp.full((1,), 128.0, dtype=jnp.float32)
        return {'x1': x1, 'x2': x2, 'x1_scale': x1_scale, 'x1_zp': x1_zp, 'x2_scale': x2_scale, 'x2_zp': x2_zp}
    _L0_xattn_all = _L0_xattn_setup()
    _L0_xattn_in = {k: v for k, v in _L0_xattn_all.items() if k in ('x1_scale', 'x1_zp', 'x2_scale', 'x2_zp')}
    del _L0_xattn_all

    def _L0_ffn_setup():
        import jax, jax.numpy as jnp
        import numpy as np
        DIM = 1024
        INTER = 3584
        SPARSITY = 64
        RANK = 16
        key = jax.random.key(seed)
        ks = jax.random.split(key, 5)
        B, T = (64, 1)
        x = jax.random.normal(ks[0], (B, T, DIM), dtype=jnp.float32)
        c1_w = jax.random.normal(ks[1], (RANK, DIM), dtype=jnp.float32) * (1.0 / np.sqrt(DIM))
        c2_w = jax.random.normal(ks[2], (INTER, RANK), dtype=jnp.float32) * (1.0 / np.sqrt(RANK))
        w1 = jax.random.normal(ks[3], (INTER, DIM), dtype=jnp.float32) * (1.0 / np.sqrt(DIM))
        w2t = jax.random.normal(ks[4], (INTER, DIM), dtype=jnp.float32) * (1.0 / np.sqrt(INTER))
        return {'x': x, 'c1_w': c1_w, 'c2_w': c2_w, 'w1': w1, 'w2t': w2t}
    _L0_ffn_all = _L0_ffn_setup()
    _L0_ffn_in = {k: v for k, v in _L0_ffn_all.items() if k in ('c1_w', 'c2_w', 'w1', 'w2t')}
    del _L0_ffn_all
    return {'x': x, 'ctx_4096': ctx_4096, 'L0_attn_Wqkv': _L0_attn_in['Wqkv'], 'L0_attn_bqkv': _L0_attn_in['bqkv'], 'L0_attn_Wo': _L0_attn_in['Wo'], 'L0_attn_bo': _L0_attn_in['bo'], 'L0_xattn_x1_scale': _L0_xattn_in['x1_scale'], 'L0_xattn_x1_zp': _L0_xattn_in['x1_zp'], 'L0_xattn_x2_scale': _L0_xattn_in['x2_scale'], 'L0_xattn_x2_zp': _L0_xattn_in['x2_zp'], 'L0_ffn_c1_w': _L0_ffn_in['c1_w'], 'L0_ffn_c2_w': _L0_ffn_in['c2_w'], 'L0_ffn_w1': _L0_ffn_in['w1'], 'L0_ffn_w2t': _L0_ffn_in['w2t']}

def reference(x, ctx_4096, L0_attn_Wqkv, L0_attn_bqkv, L0_attn_Wo, L0_attn_bo, L0_xattn_x1_scale, L0_xattn_x1_zp, L0_xattn_x2_scale, L0_xattn_x2_zp, L0_ffn_c1_w, L0_ffn_c2_w, L0_ffn_w1, L0_ffn_w2t):
    import jax
    import jax.numpy as jnp

    def _L0_attn_ref(x, Wqkv, bqkv, Wo, bo):
        import jax, jax.numpy as jnp
        import numpy as np
        H = 1024
        D = H // 4
        B, S, C = x.shape
        d = C // 4
        qkv = jnp.einsum('bsc,cf->bsf', x, Wqkv) + bqkv
        qkv = qkv.reshape(B, S, 3, d)
        q, k, v = (qkv[:, :, 0], qkv[:, :, 1], qkv[:, :, 2])
        scale = 1.0 / jnp.sqrt(jnp.float32(d)).astype(x.dtype)
        attn = jnp.einsum('bqd,bkd->bqk', q, k) * scale
        attn = jax.nn.softmax(attn, axis=-1)
        out = jnp.einsum('bqk,bkd->bqd', attn, v)
        return jnp.einsum('bqd,dc->bqc', out, Wo) + bo

    def _L0_xattn_ref(x1, x2, x1_scale, x1_zp, x2_scale, x2_zp):
        import jax, jax.numpy as jnp
        import numpy as np
        QMIN = 0.0
        QMAX = 255.0

        def fake_quant(x, scale, zp):
            s = scale.reshape(())
            z = zp.reshape(())
            q = jnp.clip(jnp.round(x / s + z), QMIN, QMAX)
            return (q - z) * s
        q1 = fake_quant(x1, x1_scale, x1_zp)
        q2 = fake_quant(x2, x2_scale, x2_zp)
        return jnp.matmul(q1, q2)

    def _L0_ffn_ref(x, c1_w, c2_w, w1, w2t):
        import jax, jax.numpy as jnp
        import numpy as np
        DIM = 1024
        INTER = 3584
        SPARSITY = 64
        RANK = 16
        B, T, M = x.shape
        xf = x.reshape(B * T, M)
        inter = xf @ c1_w.T @ c2_w.T
        n_blocks = INTER // SPARSITY
        blk = inter.reshape(B * T, n_blocks, SPARSITY)
        idx = jnp.argmax(blk, axis=-1) + jnp.arange(0, INTER, SPARSITY)
        w1_g = w1[idx]
        w2_g = w2t[idx]
        h = jax.nn.relu(jnp.einsum('bkm,bm->bk', w1_g, xf))
        out = jnp.einsum('bk,bkm->bm', h, w2_g)
        return out.reshape(B, T, M)
    x = x + _L0_attn_ref(_layernorm(x, axis=-1), L0_attn_Wqkv, L0_attn_bqkv, L0_attn_Wo, L0_attn_bo)
    x = x + _L0_xattn_ref(_layernorm(x, axis=-1), ctx_4096, L0_xattn_x1_scale, L0_xattn_x1_zp, L0_xattn_x2_scale, L0_xattn_x2_zp)
    x = x + _L0_ffn_ref(_layernorm(x, axis=-1), L0_ffn_c1_w, L0_ffn_c2_w, L0_ffn_w1, L0_ffn_w2t)
    return x

_drawn_inputs = setup_inputs


def setup_inputs(seed=0):
    import zlib

    import numpy as np

    out = dict(_drawn_inputs(seed))
    spreads = {}
    factors = {'L0_attn_bqkv': 3.873,
     'L0_attn_bo': 4.13,
     'L0_ffn_c1_w': 8.0,
     'L0_ffn_c2_w': 8.0,
     'L0_ffn_w1': 8.0,
     'L0_ffn_w2t': 8.0}
    for name, (base, spread) in spreads.items():
        noise = np.random.default_rng([zlib.crc32(name.encode()), seed]).standard_normal(out[name].shape)
        drawn = base * np.exp(spread * noise) if base else spread * noise
        out[name] = jnp.asarray(drawn.astype(out[name].dtype))
    for name, factor in factors.items():
        out[name] = (out[name] * factor).astype(out[name].dtype)
    return out
```

```python
from contextlib import ExitStack

import concourse.bass as bass
from concourse import mybir

P = 128
F32 = mybir.dt.float32
F32R = mybir.dt.float32r
BF16 = mybir.dt.bfloat16
ALU = mybir.AluOpType
ACT = mybir.ActivationFunctionType
AX = mybir.AxisListType

KB = 1024
BANK = 512
RING = 6
EPS = 1e-5
ROUND = 12582912.0
QMAX = 255.0
CENTRE = 128.0


def job_order():
    jobs = []
    for t in range(4):
        jobs += [("T1", t, 0), ("T1", t, 1)]
    for c in range(4):
        jobs += [("Q", 0, c), ("T1", 4 + c, 0), ("T1", 4 + c, 1)]
    jobs += [("V", 0, 0), ("V", 0, 1)]
    jobs += [("S", 0, i) for i in range(4)]
    jobs += [("Q", 1, c) for c in range(4)] + [("V", 1, 0), ("V", 1, 1)]
    jobs += [("PT", 0, i) for i in range(4)] + [("O", 0, 0), ("O", 0, 1)]
    jobs += [("S", 1, i) for i in range(4)]
    jobs += [("WO", i, n) for i in range(4) for n in range(2)]
    jobs += [("PT", 1, i) for i in range(4)] + [("O", 1, 0), ("O", 1, 1)]
    jobs += [("WO", i, n) for i in range(4, 8) for n in range(2)]
    jobs += [("CB", 0, 0), ("CB", 0, 1), ("QT", 0), ("QT", 1), ("XA", 0, 0), ("XA", 0, 1), ("QT", 2),
             ("XA", 1, 0), ("XA", 1, 1), ("QT", 3), ("XA", 2, 0), ("XA", 2, 1), ("XA", 3, 0), ("XA", 3, 1)]
    jobs += [("CB", 1, 0), ("CB", 1, 1), ("QT", 4), ("QT", 5), ("XA", 4, 0), ("XA", 4, 1), ("QT", 6),
             ("XA", 5, 0), ("XA", 5, 1), ("QT", 7), ("T3", 0, 0), ("T3", 0, 1), ("XA", 6, 0), ("XA", 6, 1),
             ("T3", 1, 0), ("T3", 1, 1), ("XA", 7, 0), ("XA", 7, 1)]
    jobs += [("T3", 2, 0), ("T3", 2, 1), ("T3", 3, 0), ("T3", 3, 1), ("U", 0)]
    for t in range(4, 8):
        jobs += [("T3", t, 0), ("T3", t, 1)]
    jobs += [("U", 1)]
    return jobs


JOBS = job_order()
NJ = len(JOBS)
HI_KINDS = ("T1", "Q", "V", "PT", "O", "T3")


def nth(*job):
    return JOBS.index(job)


def nth_hi(*job):
    return sum(j[0] in HI_KINDS for j in JOBS[:nth(*job)])


def decoder_layer(nc, x_in, ctx_in, wqkv, bqk, bv, wo, bo, s1, z1, s2, z2, c1, c2, w1, w2, out):
    D = x_in.shape[2]
    NT = x_in.shape[0]
    NB = 2
    TB = NT // NB
    KD = D // P
    HD = wqkv.shape[3]
    DC = HD // P
    RANK = c1.shape[2]
    BLK = 64
    NG = c2.shape[0]
    GH = c2.shape[2]
    GJ = GH // P
    SB = TB * P
    SCALE = 1.0 / 16.0
    assert (D, NT, HD, GH, SB, HD ** 0.5) == (1024, 8, 256, BANK, BANK, 1 / SCALE)

    base = (nc.sbuf_base + 31) // 32 * 32

    def at(name, kb, shape, dt):
        t = nc.alloc_sbuf_tensor_at(name, shape, dt, offset=base + int(kb * KB))
        size = 2 if dt == BF16 else 4
        for d in shape[1:]:
            size *= d
        assert base + int(kb * KB) + size <= nc.sbuf_usable_end, name
        return t

    x = at("x", 0, [P, NT, D], F32)
    xT_hi = [at(f"xT_hi{b}", 32 + 32 * b, [P, KD, SB], F32R) for b in range(NB)]
    xT_lo = [at(f"xT_lo{b}", 48 + 32 * b, [P, KD, SB], F32R) for b in range(NB)]
    W_hi = at("W_hi", 96, [P, 3, KD, HD], F32R)
    W_lo = at("W_lo", 120, [P, 3, KD, HD], F32R)
    W_raw = at("W_raw", 168, [P, 3, KD, HD], F32)
    q_hi, q_lo, k_hi, k_lo, v_hi, v_lo = (
        [at(f"{n}{b}", 144 + 24 * b + 4 * i, [P, TB, HD] if n[0] == "v" else [P, DC, SB], F32R) for b in range(NB)]
        for i, n in enumerate(("q_hi", "q_lo", "k_hi", "k_lo", "v_hi", "v_lo")))
    xn = at("xn", 192, [P, 2, D], F32)
    ctx_raw = at("ctx_raw", 48, [P, 2, D], F32)
    probs = at("probs", 56, [P, TB, SB], F32)
    q2 = [at("q2_0", 32, [P, KD, D], BF16), at("q2_1", 112, [P, KD, D], BF16)]
    pT_hi = at("pT_hi", 64, [P, TB, SB], F32R)
    pT_lo = at("pT_lo", 72, [P, TB, SB], F32R)
    oT_hi = at("oT_hi", 80, [P, DC, SB], F32R)
    oT_lo = at("oT_lo", 84, [P, DC, SB], F32R)
    Wo_raw = at("Wo_raw", 88, [P, DC, D], F32)
    Wo_hi = at("Wo_hi", 96, [P, DC, D], F32R)
    Wo_lo = at("Wo_lo", 104, [P, DC, D], F32R)
    corr = at("corr", 128, [P, NB, D], F32)
    q1 = at("q1", 136, [P, 4, D], BF16)
    q1T = at("q1T", 160, [P, 2, KD, P], BF16)
    xn3 = at("xn3", 96, [P, 2, D], F32)
    c1_raw = at("c1_raw", 104, [P, KD, RANK], F32)
    c1_hi = at("c1_hi", 105, [P, KD, 4, RANK], F32R)
    c1_lo = at("c1_lo", 107, [P, KD, 4, RANK], F32R)
    u_hi = at("u_hi", 109, [4 * RANK, SB], F32)
    u_lo = at("u_lo", 203, [4 * RANK, SB], F32)
    h_hi = at("h_hi", 96, [P, GJ, NT * P], F32R)
    h_lo = at("h_lo", 112, [P, GJ, NT * P], F32R)
    w2_lo = at("w2_lo", 128, [P, GJ, D], F32R)
    w1_hi = at("w1_hi", 144, [P, 2, KD, P], F32R)
    w1_lo = at("w1_lo", 152, [P, 2, KD, P], F32R)
    w2_hi = at("w2_hi", 160, [P, GJ, D], F32R)
    w_raw = at("w_raw", 176, [P, 2, D], F32)
    maskT = at("maskT", 184, [P, GJ, NT * P], BF16)
    u_stack = at("u_stack", 192, [4 * RANK, NT * P], F32R)
    c2_raw = at("c2_raw", 196, [4 * RANK, GH], F32)
    c2_stack = at("c2_stack", 198, [4 * RANK, GH], F32R)
    cand = at("cand", 200, [P, GH], BF16)
    pick = at("pick", 201, [P, GH], BF16)
    order = at("order", 202, [P, GH], BF16)
    bo_b = at("bo_b", 200, [P, D], F32)
    bv_b = at("bv_b", 204, [P, HD], F32)
    smalls = [205.0]

    def small(name, shape, dt):
        t = at(name, smalls[0], shape, dt)
        size = 2 if dt == BF16 else 4
        for d in shape[1:]:
            size *= d
        smalls[0] += (size + 31) // 32 * 32 / KB
        return t

    id_f = small("id_f", [P, P], F32)
    id_b = small("id_b", [P, P], BF16)
    ones_b = small("ones_b", [P, P], BF16)
    bqk_s = small("bqk_s", [P, 2 * DC], F32)
    stats = small("stats", [P, NT, 12], F32)
    mv = small("mv", [P, NT, 2], F32)
    veps = small("veps", [P, NT], F32)
    sdev = small("sdev", [P, NT], F32)
    rinv = small("rinv", [P, NT], F32)
    newt = small("newt", [P, NT], F32)
    rstd = small("rstd", [P, NT], F32)
    nmr = small("nmr", [P, NT], F32)
    qp = small("qp", [P, 4], F32)
    qd = small("qd", [P, 8], F32)
    inv1, inv2, s12, d1, d2, cs, rb_mul, rb_add = (qd[:, i:i + 1] for i in range(8))
    smax = small("smax", [P, NT], F32)
    nbias = small("nbias", [P, NT], F32)
    psum_row = small("psum_row", [P, NT], F32)
    pinv = small("pinv", [P, NT], F32)
    rowsum = small("rowsum", [P, NT], F32)
    rowbias = small("rowbias", [P, NT], F32)
    mslot = small("mslot", [4 * RANK, 2], F32)
    bmax = small("bmax", [P, GH // BLK], F32)
    cmax = small("cmax", [P, GH // BLK], BF16)

    with ExitStack() as ctx:
        bank = [ctx.enter_context(nc.psum_tensor(f"bank{i}", [P, BANK], F32)) for i in range(8)]
        score_bank = bank[6]
        maskT_bank = bank[7][:, 0:BANK // 2].bitcast(BF16)

        def sem(name):
            return ctx.enter_context(nc.semaphore(name))

        x_loaded = [sem(f"x_loaded{t}") for t in range(NT)]
        W_loaded = [sem(f"W_loaded{i}") for i in range(3)]
        bias_loaded = sem("bias_loaded")
        qp_loaded = sem("qp_loaded")
        ctx_loaded = [sem(f"ctx_loaded{i}") for i in range(2)]
        Wo_loaded = sem("Wo_loaded")
        c1_loaded = sem("c1_loaded")
        c2_loaded = sem("c2_loaded")
        w_loaded = [sem(f"w_loaded{i}") for i in range(2)]
        stored = sem("stored")
        ident_zeroed = sem("ident_zeroed")
        ident_ready = sem("ident_ready")
        id_b_ready = sem("id_b_ready")
        order_ready = sem("order_ready")
        qp_ready = sem("qp_ready")
        mm_done = sem("mm_done")
        hi_done = sem("hi_done")
        bank_free = sem("bank_free")
        vec = sem("vec")
        veps_ready = sem("veps_ready")
        sdev_ready = sem("sdev_ready")
        rstd_ready = sem("rstd_ready")
        normed = sem("normed")
        vbias_added = sem("vbias_added")
        W_hi_done = sem("W_hi_done")
        W_lo_done = sem("W_lo_done")
        bo_added = sem("bo_added")
        nbias_ready = sem("nbias_ready")
        exp_done = sem("exp_done")
        Wo_hi_done = sem("Wo_hi_done")
        Wo_lo_done = sem("Wo_lo_done")
        ctx_scaled = sem("ctx_scaled")
        ctx_rounded = sem("ctx_rounded")
        q2_done = sem("q2_done")
        q1_done = sem("q1_done")
        rowsum_done = sem("rowsum_done")
        rowbias_ready = sem("rowbias_ready")
        xa_scaled = sem("xa_scaled")
        corr_added = sem("corr_added")
        c1_done = sem("c1_done")
        w_hi_done = sem("w_hi_done")
        w_lo_done = sem("w_lo_done")
        c2_done = sem("c2_done")
        score_done = sem("score_done")
        score_read = sem("score_read")
        pick_ready = sem("pick_ready")
        maskT_done = sem("maskT_done")
        maskT_copied = sem("maskT_copied")
        relu_masked = sem("relu_masked")
        h_hi_done = sem("h_hi_done")

        def job_bank(*job):
            return bank[nth(*job) % RING]

        PER = 2 * GJ + 2 * NT
        WSEQ = [("w1", 0), ("w1", 1), ("w2", 0), ("w2", 1), ("w1", 2), ("w2", 2), ("w1", 3), ("w2", 3)]
        NW = len(WSEQ)
        UNIT_BANK = [(0, 1, 4, 5, 2, 3)[u % 6] for u in range(2 * NT)]

        def hidden_nth(g, j, half):
            return g * PER + (NJ + 2 * j + half)

        def unit_nth(g, u):
            return g * PER + (NJ + 2 * GJ + u)

        def prev_unit_on(b):
            return max(u for u in range(2 * NT) if UNIT_BANK[u] == b)

        block = ctx.enter_context(nc.Block())

        @block.sync
        def _(sp):
            for t in range(TB):
                sp.dma_start(x[:, t, :], x_in[t]).then_inc(x_loaded[t], 16)
            for i in range(3):
                sp.dma_start(W_raw[:, i, :, :], wqkv[i]).then_inc(W_loaded[i], 16)
            for dst, src in ((bqk_s[:, :], bqk), (bv_b[:, :], bv.partition_broadcast(P)),
                             (bo_b[:, :], bo.partition_broadcast(P))):
                sp.dma_start(dst, src).then_inc(bias_loaded, 16)
            for t in range(TB, NT):
                sp.dma_start(x[:, t, :], x_in[t]).then_inc(x_loaded[t], 16)
            for i, src in enumerate((s1, z1, s2, z2)):
                sp.dma_start(qp[:, i:i + 1], src.partition_broadcast(P)).then_inc(qp_loaded, 16)
            sp.wait_ge(mm_done, nth("V", 0, 1) + 1)
            for i in range(NB * KD):
                if i >= 2:
                    sp.wait_ge(q2_done, i - 1)
                sp.dma_start(ctx_raw[:, i % 2, :], ctx_in[i]).then_inc(ctx_loaded[i % 2], 16)

            def load_w(which, j, g, slot):
                src = w1 if which == "w1" else w2
                sp.dma_start(w_raw[:, slot, :], src[g * GJ + j]).then_inc(w_loaded[slot], 16)

            def load_c2(g):
                for i in range(4):
                    sp.dma_start(c2_raw[RANK * i:RANK * (i + 1), :], c2[g]).then_inc(c2_loaded, 16)

            sp.wait_ge(mm_done, nth("O", 1, 1) + 1)
            load_w(*WSEQ[0], 0, 0)
            load_w(*WSEQ[1], 0, 1)
            sp.wait_ge(mm_done, nth("WO", 7, 1) + 1)
            sp.dma_start(c1_raw[:, :, :], c1).then_inc(c1_loaded, 16)
            sp.wait_ge(q1_done, NT)
            load_c2(0)

            def group(g, last):
                if not last:
                    sp.wait_ge(c2_done, g + 1)
                    load_c2(g + 1)
                for i in range(NW - 2 if last else NW):
                    sp.wait_ge(w_lo_done, g * NW + (i + 1))
                    which, j = WSEQ[(i + 2) % NW]
                    load_w(which, j, g + 1 if i + 2 >= NW else g, i % 2)

            with sp.Fori(0, NG - 1) as g:
                group(g, False)
            group(NG - 1, True)
            for t in range(NT):
                sp.wait_ge(bank_free, unit_nth(NG - 1, 2 * t + 1) + 1)
                sp.dma_start(out[t], x[:, t, :]).then_inc(stored, 16)
            sp.wait_ge(stored, 16 * NT)

        @block.gpsimd
        def _(pool):
            nc.gpsimd.memset(id_f[:, :], 0.0).then_inc(ident_zeroed, 1)
            pool.wait_ge(ident_zeroed, 1)
            nc.gpsimd.affine_select(out=id_f[:, :], in_=id_f[:, :], compare_op=ALU.not_equal, fill=1.0,
                                    base=0, pattern=[[-1, P]], channel_multiplier=1).then_inc(ident_ready, 1)
            for i in range(3):
                pool.wait_ge(W_hi_done, i + 1)
                nc.gpsimd.tensor_tensor(W_lo[:, i, :, :], W_raw[:, i, :, :], W_hi[:, i, :, :].bitcast(F32),
                                        ALU.subtract).then_inc(W_lo_done, 1)
            pool.wait_ge(bias_loaded, 48)
            for t in range(NT):
                pool.wait_ge(normed, t + 1)
                nc.gpsimd.tensor_tensor(x[:, t, :], x[:, t, :], bo_b[:, :], ALU.add).then_inc(bo_added, 1)
            for i in range(NB * KD):
                pool.wait_ge(ctx_rounded, i + 1)
                if i == KD:
                    pool.wait_ge(mm_done, nth("V", 1, 1) + 1)
                nc.gpsimd.tensor_scalar(q2[i // KD][:, i % KD, :], ctx_raw[:, i % 2, :], -(ROUND + CENTRE), 1.0,
                                        ALU.add, ALU.mult).then_inc(q2_done, 1)
            for t in range(NT):
                pool.wait_ge(normed, NT + t + 1)
                pool.wait_ge(bank_free, nth("CB", t // TB, 1) + 1)
                nc.gpsimd.tensor_tensor(x[:, t, :], x[:, t, :], corr[:, t // TB, :], ALU.add).then_inc(corr_added, 1)
            nc.gpsimd.iota(order[:, :].rearrange("p (b w) -> p b w", w=BLK), pattern=[[0, GH // BLK], [-1, BLK]],
                           base=BLK, channel_multiplier=0,
                           allow_small_or_imprecise_dtypes=True).then_inc(order_ready, 1)

            def cut_w(g, i):
                which, j = WSEQ[i % NW]
                pool.wait_ge(w_hi_done, g * NW + (i + 1))
                hi, lo = (w1_hi[:, j % 2], w1_lo[:, j % 2]) if which == "w1" else (w2_hi[:, j], w2_lo[:, j])
                raw = w_raw[:, i % 2, :]
                if which == "w1":
                    raw = raw.rearrange("p (k m) -> p k m", k=KD)
                nc.gpsimd.tensor_tensor(lo, raw, hi.bitcast(F32), ALU.subtract).then_inc(w_lo_done, 1)

            cut_w(0, 0)
            cut_w(0, 1)
            for i in range(2, NW):
                cut_w(0, i)
            with pool.Fori(1, NG) as g:
                for i in range(NW):
                    cut_w(g, i)

        @block.scalar
        def _(act):
            def sqrt_pair(rnd, t):
                act.wait_ge(veps_ready, (rnd * NT + t) // 2 + 1)
                nc.scalar.activation(sdev[:, t:t + 2], veps[:, t:t + 2], ACT.Sqrt).then_inc(sdev_ready, 1)

            def norm(rnd, t):
                act.wait_ge(rstd_ready, (rnd * NT + t) // 2 + 1)
                if rnd == 0 and t >= 2:
                    act.wait_ge(mm_done, nth("T1", t - 2, 1) + 1)
                if rnd == 1 and t < 2:
                    act.wait_ge(mm_done, nth("T1", t + 6, 1) + 1)
                if rnd == 1 and t >= 2:
                    act.wait_ge(q1_done, t - 1)
                if rnd == 2 and t >= 2:
                    act.wait_ge(mm_done, nth("T3", t - 2, 1) + 1)
                dst = (xn3 if rnd == 2 else xn)[:, t % 2, :]
                nc.scalar.activation(dst, x[:, t, :], ACT.Identity, bias=nmr[:, t:t + 1],
                                     scale=rstd[:, t:t + 1]).then_inc(normed, 1)

            def hi_T(rnd, t, h):
                job = ("T1" if rnd == 0 else "T3", t, h)
                act.wait_ge(mm_done, nth(*job) + 1)
                nc.scalar.activation(
                    xT_hi[t // TB][:, 4 * h:4 * h + 4, (t % TB) * P:(t % TB + 1) * P],
                    job_bank(*job)[:, :].rearrange("p (k m) -> p k m", k=4), ACT.Copy).then_inc(hi_done, 1)

            def hi_W(i):
                act.wait_ge(W_loaded[i], 16)
                nc.scalar.activation(W_hi[:, i, :, :], W_raw[:, i, :, :], ACT.Copy).then_inc(W_hi_done, 1)

            def hi_Q(b, c):
                act.wait_ge(mm_done, nth("Q", b, c) + 1)
                if b == 0 and c == 0:
                    act.wait_ge(bias_loaded, 48)
                if b == 1 and c == 0:
                    act.wait_ge(W_lo_done, 3)
                dst = (q_hi if c < DC else k_hi)[b]
                nc.scalar.activation(dst[:, c % DC, :], job_bank("Q", b, c)[:, :], ACT.Identity,
                                     bias=bqk_s[:, c:c + 1], scale=1.0).then_inc(hi_done, 1)

            def hi_V(b, i):
                act.wait_ge(vbias_added, 2 * b + i + 1)
                nc.scalar.activation(v_hi[b][:, 2 * i:2 * i + 2, :],
                                     job_bank("V", b, i)[:, :].rearrange("p (t d) -> p t d", t=2),
                                     ACT.Copy).then_inc(hi_done, 1)

            def exp(b, i):
                n = b * TB + i
                act.wait_ge(nbias_ready, n + 1)
                if b == 0 and i == 0:
                    act.wait_ge(mm_done, nth("V", 0, 1) + 1)
                if b == 1:
                    act.wait_ge(mm_done, nth("PT", 0, i) + 1)
                nc.scalar.activation(probs[:, i, :], job_bank("S", b, i)[:, :], ACT.Exp, bias=nbias[:, n:n + 1],
                                     scale=SCALE, accum_out=psum_row[:, n:n + 1]).then_inc(exp_done, 1)

            def hi_PT(b, i):
                act.wait_ge(mm_done, nth("PT", b, i) + 1)
                nc.scalar.activation(pT_hi[:, :, i * P:(i + 1) * P],
                                     job_bank("PT", b, i)[:, :].rearrange("p (k m) -> p k m", k=TB),
                                     ACT.Copy).then_inc(hi_done, 1)

            def hi_O(b, c):
                act.wait_ge(mm_done, nth("O", b, c) + 1)
                nc.scalar.activation(oT_hi[:, c, :], job_bank("O", b, c)[:, :], ACT.Copy).then_inc(hi_done, 1)

            def scale_ctx(i):
                act.wait_ge(ctx_loaded[i % 2], 16 * (i // 2 + 1))
                nc.scalar.activation(ctx_raw[:, i % 2, :], ctx_raw[:, i % 2, :], ACT.Copy,
                                     scale=inv2).then_inc(ctx_scaled, 1)

            def sum_row(t):
                act.wait_ge(q1_done, t + 1)
                nc.scalar.activation(q1[:, t % 4, :], q1[:, t % 4, :], ACT.Copy,
                                     accum_out=rowsum[:, t:t + 1]).then_inc(rowsum_done, 1)

            def scale_xa(t):
                act.wait_ge(rowbias_ready, t + 1)
                for n in range(2):
                    act.wait_ge(mm_done, nth("XA", t, n) + 1)
                    pb = job_bank("XA", t, n)
                    nc.scalar.activation(pb[:, :], pb[:, :], ACT.Identity, bias=rowbias[:, t:t + 1],
                                         scale=s12).then_inc(xa_scaled, 1)

            def both(f, *a):
                f(*a, 0)
                f(*a, 1)

            sqrt_pair(0, 0)
            norm(0, 0)
            norm(0, 1)
            both(hi_T, 0, 0)
            sqrt_pair(0, 2)
            norm(0, 2)
            both(hi_T, 0, 1)
            hi_W(0)
            norm(0, 3)
            both(hi_T, 0, 2)
            hi_W(1)
            both(hi_T, 0, 3)
            hi_W(2)
            sqrt_pair(0, 4)
            norm(0, 4)
            norm(0, 5)
            hi_Q(0, 0)
            both(hi_T, 0, 4)
            sqrt_pair(0, 6)
            norm(0, 6)
            hi_Q(0, 1)
            both(hi_T, 0, 5)
            norm(0, 7)
            hi_Q(0, 2)
            both(hi_T, 0, 6)
            hi_Q(0, 3)
            both(hi_T, 0, 7)
            hi_V(0, 0)
            hi_V(0, 1)
            for i in range(TB):
                exp(0, i)
            act.wait_ge(qp_ready, 1)
            scale_ctx(0)
            scale_ctx(1)
            for c in range(4):
                hi_Q(1, c)
                scale_ctx(2 * c + 2)
                scale_ctx(2 * c + 3)
            hi_V(1, 0)
            hi_V(1, 1)
            act.wait_ge(mm_done, nth("V", 1, 1) + 1)
            act.dma_start(Wo_raw[:, :, :], wo).then_inc(Wo_loaded, 16)
            for i in range(TB):
                hi_PT(0, i)
            hi_O(0, 0)
            hi_O(0, 1)
            scale_ctx(10)
            for i in range(TB):
                exp(1, i)
            act.wait_ge(Wo_loaded, 16)
            nc.scalar.activation(Wo_hi[:, :, :], Wo_raw[:, :, :], ACT.Copy).then_inc(Wo_hi_done, 1)
            for i in range(11, 16):
                scale_ctx(i)
            sqrt_pair(1, 0)
            hi_PT(1, 0)
            hi_PT(1, 1)
            norm(1, 0)
            norm(1, 1)
            sqrt_pair(1, 2)
            hi_PT(1, 2)
            hi_PT(1, 3)
            norm(1, 2)
            hi_O(1, 0)
            hi_O(1, 1)
            norm(1, 3)
            for t in range(4):
                sum_row(t)
            sqrt_pair(1, 4)
            norm(1, 4)
            norm(1, 5)
            scale_xa(0)
            sum_row(4)
            sum_row(5)
            sqrt_pair(1, 6)
            scale_xa(1)
            norm(1, 6)
            norm(1, 7)
            scale_xa(2)
            sum_row(6)
            scale_xa(3)
            sum_row(7)
            sqrt_pair(2, 0)
            scale_xa(4)
            norm(2, 0)
            scale_xa(5)
            norm(2, 1)
            both(hi_T, 2, 0)
            sqrt_pair(2, 2)
            scale_xa(6)
            both(hi_T, 2, 1)
            norm(2, 2)
            scale_xa(7)
            norm(2, 3)

            def hi_w(g, i):
                which, j = WSEQ[i % NW]
                act.wait_ge(w_loaded[i % 2], g * (16 * NW // 2) + 16 * (i // 2 + 1))
                if which == "w1":
                    gg, jj = (g + i // NW, j - 2) if j >= 2 else (g + i // NW - 1, j + 2)
                    if isinstance(gg, int) and gg < 0:
                        act.wait_ge(mm_done, nth("O", 0, 1) + 1)
                    else:
                        act.wait_ge(mm_done, hidden_nth(gg, jj, 1) + 1)
                    dst = w1_hi[:, j % 2]
                else:
                    act.wait_ge(mm_done, hidden_nth(g, 0, 0))
                    dst = w2_hi[:, j]
                raw = w_raw[:, i % 2, :]
                if which == "w1":
                    raw = raw.rearrange("p (k m) -> p k m", k=KD)
                nc.scalar.activation(dst, raw, ACT.Copy).then_inc(w_hi_done, 1)

            def copy_maskT(g, t):
                act.wait_ge(maskT_done, g * NT + (t + 1))
                if not (isinstance(g, int) and g == 0):
                    act.wait_ge(relu_masked, g * 2 * GJ)
                nc.scalar.activation(maskT[:, :, t * P:(t + 1) * P],
                                     maskT_bank.rearrange("p (j m) -> p j m", j=GJ),
                                     ACT.Copy).then_inc(maskT_copied, 1)

            def hi_h(g, j):
                for half in range(2):
                    act.wait_ge(relu_masked, g * 2 * GJ + (2 * j + half + 1))
                    nc.scalar.activation(h_hi[:, j, half * SB:(half + 1) * SB], bank[2 * (j % 2) + half][:, :],
                                         ACT.Copy).then_inc(h_hi_done, 1)

            both(hi_T, 2, 2)
            both(hi_T, 2, 3)
            sqrt_pair(2, 4)
            norm(2, 4)
            norm(2, 5)
            sqrt_pair(2, 6)
            hi_w(0, 0)
            hi_w(0, 1)
            both(hi_T, 2, 4)
            copy_maskT(0, 0)
            norm(2, 6)
            both(hi_T, 2, 5)
            copy_maskT(0, 1)
            norm(2, 7)
            both(hi_T, 2, 6)
            copy_maskT(0, 2)
            both(hi_T, 2, 7)
            copy_maskT(0, 3)
            hi_w(0, 2)
            hi_w(0, 3)
            copy_maskT(0, 4)
            for half in range(1):
                act.wait_ge(relu_masked, 1)
                nc.scalar.activation(h_hi[:, 0, 0:SB], bank[0][:, :], ACT.Copy).then_inc(h_hi_done, 1)
            copy_maskT(0, 5)
            copy_maskT(0, 6)
            hi_w(0, 4)
            copy_maskT(0, 7)
            act.wait_ge(relu_masked, 2)
            nc.scalar.activation(h_hi[:, 0, SB:2 * SB], bank[1][:, :], ACT.Copy).then_inc(h_hi_done, 1)
            hi_h(0, 1)
            hi_w(0, 5)
            hi_w(0, 6)
            hi_w(0, 7)
            hi_h(0, 2)
            hi_h(0, 3)
            with act.Fori(0, NG - 1) as g:
                for t in range(NT):
                    copy_maskT(g + 1, t)
                    if t == 2:
                        hi_w(g, NW)
                    if t == 4:
                        hi_w(g, NW + 1)
                hi_w(g + 1, 2)
                hi_w(g + 1, 3)
                hi_h(g + 1, 0)
                hi_w(g + 1, 4)
                hi_w(g + 1, 5)
                hi_h(g + 1, 1)
                hi_w(g + 1, 6)
                hi_w(g + 1, 7)
                hi_h(g + 1, 2)
                hi_h(g + 1, 3)

        @block.vector
        def _(dve):
            chained = [0]

            def link(ins, off=0):
                chained[0] += 1
                ins.then_inc(vec, 1)
                dve.wait_ge(vec, chained[0] + off)

            def free(ins):
                ins.then_inc(bank_free, 1)

            def stats_of(t):
                link(nc.vector.bn_stats(stats[:, t, 0:6], x[:, t, 0:BANK]))
                link(nc.vector.bn_stats(stats[:, t, 6:12], x[:, t, BANK:D]))
                link(nc.vector.bn_aggr(mv[:, t, :], stats[:, t, :]))

            def norm_stats(t):
                stats_of(t)
                stats_of(t + 1)
                nc.vector.tensor_scalar(veps[:, t:t + 2], mv[:, t:t + 2, 1], EPS, None,
                                        ALU.add).then_inc(veps_ready, 1)

            def norm_scale(rnd, t):
                s = slice(t, t + 2)
                dve.wait_ge(sdev_ready, (rnd * NT + t) // 2 + 1)
                dve.wait_ge(veps_ready, (rnd * NT + t) // 2 + 1)
                link(nc.vector.reciprocal(rinv[:, s], sdev[:, s]))
                link(nc.vector.tensor_tensor(newt[:, s], veps[:, s], rinv[:, s], ALU.mult))
                link(nc.vector.tensor_tensor(newt[:, s], newt[:, s], rinv[:, s], ALU.mult))
                link(nc.vector.tensor_scalar(newt[:, s], newt[:, s], -0.5, 1.5, ALU.mult, ALU.add))
                link(nc.vector.tensor_tensor(rstd[:, s], newt[:, s], rinv[:, s], ALU.mult))
                nc.vector.scalar_tensor_tensor(nmr[:, s], mv[:, s, 0], -1.0, rstd[:, s], ALU.mult,
                                               ALU.mult).then_inc(rstd_ready, 1)

            def lo_T(rnd, t):
                for h in range(2):
                    job = ("T1" if rnd == 0 else "T3", t, h)
                    dve.wait_ge(hi_done, nth_hi(*job) + 1)
                    k, m = slice(4 * h, 4 * h + 4), slice((t % TB) * P, (t % TB + 1) * P)
                    free(nc.vector.tensor_tensor(
                        xT_lo[t // TB][:, k, m], job_bank(*job)[:, :].rearrange("p (k m) -> p k m", k=4),
                        xT_hi[t // TB][:, k, m].bitcast(F32), ALU.subtract))

            def lo_Q(b, c):
                dve.wait_ge(hi_done, nth_hi("Q", b, c) + 1)
                hi, lo = (q_hi, q_lo) if c < DC else (k_hi, k_lo)
                free(nc.vector.scalar_tensor_tensor(
                    lo[b][:, c % DC, :], job_bank("Q", b, c)[:, :], bqk_s[:, c:c + 1],
                    hi[b][:, c % DC, :].bitcast(F32), ALU.add, ALU.subtract))

            def lo_V(b, i):
                pv = job_bank("V", b, i)[:, :].rearrange("p (t d) -> p t d", t=2)
                dve.wait_ge(mm_done, nth("V", b, i) + 1)
                nc.vector.tensor_tensor(
                    pv, pv, bv_b[:, :].rearrange("p (o d) -> p o d", o=1).to_broadcast([P, 2, HD]),
                    ALU.add).then_inc(vbias_added, 1)
                dve.wait_ge(hi_done, nth_hi("V", b, i) + 1)
                free(nc.vector.tensor_tensor(v_lo[b][:, 2 * i:2 * i + 2, :], pv,
                                             v_hi[b][:, 2 * i:2 * i + 2, :].bitcast(F32), ALU.subtract))

            def softmax(b):
                for i in range(TB):
                    n = b * TB + i
                    dve.wait_ge(mm_done, nth("S", b, i) + 1)
                    link(nc.vector.reduce_max(smax[:, n:n + 1], job_bank("S", b, i)[:, :], AX.X))
                    nc.vector.tensor_scalar(nbias[:, n:n + 1], smax[:, n:n + 1], -SCALE, None,
                                            ALU.mult).then_inc(nbias_ready, 1)
                for i in range(TB):
                    n = b * TB + i
                    dve.wait_ge(exp_done, n + 1)
                    free(nc.vector.reciprocal(pinv[:, n:n + 1], psum_row[:, n:n + 1]))

            def lo_PT(b, i):
                dve.wait_ge(hi_done, nth_hi("PT", b, i) + 1)
                m = slice(i * P, (i + 1) * P)
                free(nc.vector.tensor_tensor(pT_lo[:, :, m],
                                             job_bank("PT", b, i)[:, :].rearrange("p (k m) -> p k m", k=TB),
                                             pT_hi[:, :, m].bitcast(F32), ALU.subtract))

            def lo_O(b, c):
                dve.wait_ge(hi_done, nth_hi("O", b, c) + 1)
                free(nc.vector.tensor_tensor(oT_lo[:, c, :], job_bank("O", b, c)[:, :],
                                             oT_hi[:, c, :].bitcast(F32), ALU.subtract))

            def add_WO(t):
                dve.wait_ge(bo_added, t + 1)
                for n in range(2):
                    dve.wait_ge(mm_done, nth("WO", t, n) + 1)
                    c = slice(n * BANK, (n + 1) * BANK)
                    free(nc.vector.scalar_tensor_tensor(x[:, t, c], job_bank("WO", t, n)[:, :], pinv[:, t:t + 1],
                                                        x[:, t, c], ALU.mult, ALU.add))

            def round_ctx(i):
                r = ctx_raw[:, i % 2, :]
                dve.wait_ge(ctx_scaled, i + 1)
                link(nc.vector.tensor_scalar(r, r, qp[:, 3:4], ROUND, ALU.add, ALU.add))
                nc.vector.tensor_scalar(r, r, ROUND, ROUND + QMAX, ALU.max, ALU.min).then_inc(ctx_rounded, 1)

            def quantise(t):
                r = xn[:, t % 2, :]
                dve.wait_ge(normed, NT + t + 1)
                link(nc.vector.tensor_scalar(r, r, inv1, qp[:, 1:2], ALU.mult, ALU.add))
                link(nc.vector.tensor_scalar(r, r, ROUND, ROUND, ALU.add, ALU.max))
                if t >= 4:
                    dve.wait_ge(mm_done, nth("QT", t - 4) + 1)
                if t == 0:
                    dve.wait_ge(mm_done, nth("V", 1, 1) + 1)
                nc.vector.tensor_scalar(q1[:, t % 4, :], r, ROUND + QMAX, ROUND + CENTRE, ALU.min,
                                        ALU.subtract).then_inc(q1_done, 1)

            def copy_CB(b):
                for n in range(2):
                    dve.wait_ge(mm_done, nth("CB", b, n) + 1)
                    free(nc.vector.tensor_scalar(corr[:, b, n * BANK:(n + 1) * BANK], job_bank("CB", b, n)[:, :],
                                                 cs, None, ALU.mult))

            def copy_QT(t):
                dve.wait_ge(mm_done, nth("QT", t) + 1)
                if t >= 2:
                    dve.wait_ge(mm_done, nth("XA", t - 2, 1) + 1)
                free(nc.vector.tensor_copy(q1T[:, t % 2, :, :],
                                           job_bank("QT", t)[:, :].bitcast(BF16).rearrange("p (k m) -> p k m", k=KD)))
                dve.wait_ge(rowsum_done, t + 1)
                nc.vector.tensor_scalar(rowbias[:, t:t + 1], rowsum[:, t:t + 1], rb_mul, rb_add, ALU.mult,
                                        ALU.add).then_inc(rowbias_ready, 1)

            def add_XA(t):
                dve.wait_ge(corr_added, t + 1)
                for n in range(2):
                    c = slice(n * BANK, (n + 1) * BANK)
                    dve.wait_ge(xa_scaled, 2 * t + n + 1)
                    free(nc.vector.tensor_tensor(x[:, t, c], job_bank("XA", t, n)[:, :], x[:, t, c], ALU.add))

            def stack_u(b):
                pu = job_bank("U", b)[0:4 * RANK, :]
                dve.wait_ge(mm_done, nth("U", b) + 1)
                link(nc.vector.tensor_copy(u_hi[:, :].bitcast(F32R), pu))
                link(nc.vector.tensor_tensor(u_lo[:, :], pu, u_hi[:, :], ALU.subtract))
                link(nc.vector.tensor_scalar(u_hi[:, :], u_hi[:, :], mslot[:, 0:1], None, ALU.mult))
                free(nc.vector.scalar_tensor_tensor(u_stack[:, b * SB:(b + 1) * SB], u_lo[:, :], mslot[:, 1:2],
                                                    u_hi[:, :], ALU.mult, ALU.add))

            def cut_c2(g, off=0):
                dve.wait_ge(c2_loaded, g * 64 + 64)
                half = slice(2 * RANK, 4 * RANK)
                link(nc.vector.tensor_copy(c2_stack[:, :], c2_raw[:, :]), off)
                nc.vector.tensor_tensor(c2_stack[half, :], c2_raw[half, :], c2_stack[half, :].bitcast(F32),
                                        ALU.subtract).then_inc(c2_done, 1)

            def pick_first(g, t, off=0):
                sc = score_bank[:, :].rearrange("p (b w) -> p b w", w=BLK)
                cd = cand[:, :].rearrange("p (b w) -> p b w", w=BLK)
                pk = pick[:, :].rearrange("p (b w) -> p b w", w=BLK)
                wide = [P, GH // BLK, BLK]
                dve.wait_ge(score_done, g * NT + (t + 1))
                link(nc.vector.tensor_reduce(bmax[:, :], sc, AX.X, ALU.max), off)
                ins = nc.vector.tensor_tensor(
                    cd, sc, bmax[:, :].rearrange("p (b o) -> p b o", o=1).to_broadcast(wide), ALU.is_equal)
                ins.then_inc(score_read, 1)
                dve.wait_ge(score_read, g * NT + (t + 1))
                link(nc.vector.tensor_tensor(cand[:, :], cand[:, :], order[:, :], ALU.mult), off)
                link(nc.vector.tensor_reduce(cmax[:, :], cd, AX.X, ALU.max), off)
                if isinstance(g, int) and g == 0:
                    if t > 0:
                        dve.wait_ge(maskT_done, t)
                else:
                    dve.wait_ge(maskT_done, g * NT + t)
                nc.vector.tensor_tensor(pk, cd, cmax[:, :].rearrange("p (b o) -> p b o", o=1).to_broadcast(wide),
                                        ALU.is_equal).then_inc(pick_ready, 1)

            def relu_mask(g, j, half):
                pb = bank[2 * (j % 2) + half]
                dve.wait_ge(mm_done, hidden_nth(g, j, half) + 1)
                dve.wait_ge(maskT_copied, g * NT + TB * (half + 1))
                nc.vector.scalar_tensor_tensor(pb[:, :], pb[:, :], 0.0, maskT[:, j, half * SB:(half + 1) * SB],
                                               ALU.max, ALU.mult).then_inc(relu_masked, 1)

            def lo_h(g, j, half):
                dve.wait_ge(h_hi_done, g * 2 * GJ + (2 * j + half + 1))
                s = slice(half * SB, (half + 1) * SB)
                free(nc.vector.tensor_tensor(h_lo[:, j, s], bank[2 * (j % 2) + half][:, :],
                                             h_hi[:, j, s].bitcast(F32), ALU.subtract))

            def add_unit(g, u):
                t, n = divmod(u, 2)
                c = slice(n * BANK, (n + 1) * BANK)
                dve.wait_ge(mm_done, unit_nth(g, u) + 1)
                free(nc.vector.tensor_tensor(x[:, t, c], bank[UNIT_BANK[u]][:, :], x[:, t, c], ALU.add))

            nc.vector.memset(ones_b[:, :], 1.0)
            for t in (0, 2):
                dve.wait_ge(x_loaded[t], 16)
                dve.wait_ge(x_loaded[t + 1], 16)
                norm_stats(t)
                if t == 0:
                    norm_scale(0, t)
                else:
                    lo_T(0, 0)
                    norm_scale(0, t)
            dve.wait_ge(ident_ready, 1)
            nc.vector.tensor_copy(id_b[:, :], id_f[:, :]).then_inc(id_b_ready, 1)
            slots = id_f[0:4 * RANK, 0:4 * RANK].rearrange("p (a s c) -> p s a c", a=2, s=2)
            for s in range(2):
                link(nc.vector.tensor_reduce(mslot[:, s:s + 1], slots[:, s], AX.XY, ALU.add))
            for t in (1, 2, 3):
                lo_T(0, t)
            dve.wait_ge(x_loaded[4], 16)
            dve.wait_ge(x_loaded[5], 16)
            norm_stats(4)
            norm_scale(0, 4)
            lo_Q(0, 0)
            lo_T(0, 4)
            dve.wait_ge(x_loaded[6], 16)
            dve.wait_ge(x_loaded[7], 16)
            norm_stats(6)
            norm_scale(0, 6)
            lo_Q(0, 1)
            lo_T(0, 5)
            lo_Q(0, 2)
            lo_T(0, 6)
            lo_Q(0, 3)
            lo_T(0, 7)
            dve.wait_ge(qp_loaded, 64)
            nc.vector.reciprocal(inv1, qp[:, 0:1])
            nc.vector.reciprocal(inv2, qp[:, 2:3])
            nc.vector.tensor_tensor(s12, qp[:, 0:1], qp[:, 2:3], ALU.mult)
            nc.vector.tensor_scalar(d1, qp[:, 1:2], -1.0, CENTRE, ALU.mult, ALU.add)
            link(nc.vector.tensor_scalar(d2, qp[:, 3:4], -1.0, CENTRE, ALU.mult, ALU.add))
            nc.vector.tensor_tensor(cs, s12, d1, ALU.mult)
            link(nc.vector.tensor_tensor(rb_mul, s12, d2, ALU.mult))
            nc.vector.scalar_tensor_tensor(rb_add, rb_mul, float(D), d1, ALU.mult, ALU.mult).then_inc(qp_ready, 1)
            dve.wait_ge(bias_loaded, 48)
            lo_V(0, 0)
            lo_V(0, 1)
            softmax(0)
            for c in range(4):
                lo_Q(1, c)
                round_ctx(2 * c)
                round_ctx(2 * c + 1)
            lo_V(1, 0)
            lo_V(1, 1)
            for i in range(TB):
                lo_PT(0, i)
                if i % 2:
                    round_ctx(8 + i // 2)
            lo_O(0, 0)
            lo_O(0, 1)
            softmax(1)
            dve.wait_ge(Wo_hi_done, 1)
            nc.vector.tensor_tensor(Wo_lo[:, :, :], Wo_raw[:, :, :], Wo_hi[:, :, :].bitcast(F32),
                                    ALU.subtract).then_inc(Wo_lo_done, 1)
            round_ctx(10)
            for t in range(TB):
                add_WO(t)
                round_ctx(11 + t)
            round_ctx(15)
            norm_stats(0)
            lo_PT(1, 0)
            lo_PT(1, 1)
            norm_scale(1, 0)
            quantise(0)
            quantise(1)
            norm_stats(2)
            lo_PT(1, 2)
            lo_PT(1, 3)
            norm_scale(1, 2)
            lo_O(1, 0)
            lo_O(1, 1)
            quantise(2)
            quantise(3)
            for t in range(TB, NT):
                add_WO(t)
            norm_stats(4)
            norm_scale(1, 4)
            copy_CB(0)
            copy_QT(0)
            copy_QT(1)
            quantise(4)
            quantise(5)
            add_XA(0)
            copy_QT(2)
            norm_stats(6)
            add_XA(1)
            copy_QT(3)
            norm_scale(1, 6)
            quantise(6)
            add_XA(2)
            quantise(7)
            add_XA(3)
            copy_CB(1)
            copy_QT(4)
            copy_QT(5)
            norm_stats(0)
            add_XA(4)
            copy_QT(6)
            norm_scale(2, 0)
            add_XA(5)
            copy_QT(7)
            lo_T(2, 0)
            norm_stats(2)
            add_XA(6)
            lo_T(2, 1)
            norm_scale(2, 2)
            add_XA(7)
            lo_T(2, 2)
            lo_T(2, 3)
            norm_stats(4)
            norm_scale(2, 4)
            wide = c1_raw[:, :, :].rearrange("p k (o r) -> p k o r", o=1).to_broadcast([P, KD, 4, RANK])
            dve.wait_ge(c1_loaded, 16)
            for k in range(KD):
                last = nc.vector.tensor_copy(c1_hi[:, k], wide[:, k])
            link(last)
            for k in range(KD):
                last = nc.vector.tensor_tensor(c1_lo[:, k], wide[:, k], c1_hi[:, k].bitcast(F32), ALU.subtract)
            last.then_inc(c1_done, 1)
            norm_stats(6)
            norm_scale(2, 6)
            dve.wait_ge(order_ready, 1)
            cut_c2(0)
            stack_u(0)
            for t in range(TB):
                pick_first(0, t)
                lo_T(2, TB + t)
            stack_u(1)
            pick_first(0, 4)
            relu_mask(0, 0, 0)
            lo_h(0, 0, 0)
            for t in range(5, NT):
                pick_first(0, t)
            relu_mask(0, 0, 1)
            lo_h(0, 0, 1)
            for j in range(1, GJ):
                for half in range(2):
                    relu_mask(0, j, half)
                for half in range(2):
                    lo_h(0, j, half)

            before = chained[0]
            links = 1 + 3 * NT
            with dve.Fori(0, NG - 1) as g:
                off = g * links
                dve.wait_ge(score_done, g * NT + NT)
                cut_c2(g + 1, off)
                pick_first(g + 1, 0, off)
                pick_first(g + 1, 1, off)
                for u in range(4):
                    add_unit(g, u)
                for t in range(2, NT):
                    pick_first(g + 1, t, off)
                    add_unit(g, 2 * t)
                    add_unit(g, 2 * t + 1)
                for j in range(GJ):
                    for half in range(2):
                        relu_mask(g + 1, j, half)
                    for half in range(2):
                        lo_h(g + 1, j, half)
            assert chained[0] - before == links
            for u in range(2 * NT):
                add_unit(NG - 1, u)

        @block.tensor
        def _(pe):
            def take_bank(*job):
                n = nth(*job)
                if n >= RING:
                    pe.wait_ge(bank_free, n - RING + 1)

            def made(*job):
                pe.wait_ge(bank_free, nth(*job) + 1)

            def split_mm(dst, pairs):
                for n, ((ah, al), (bh, bl)) in enumerate(pairs):
                    nc.tensor.matmul(dst, ah, bh, start=n == 0, stop=False)
                    nc.tensor.matmul(dst, ah, bl, start=False, stop=False)
                    last = nc.tensor.matmul(dst, al, bh, start=False, stop=n == len(pairs) - 1)
                return last

            def transpose_norm(rnd, t):
                pe.wait_ge(normed, rnd * NT + t + 1)
                for h in range(2):
                    job = ("T1" if rnd == 0 else "T3", t, h)
                    take_bank(*job)
                    for k in range(4):
                        src = (xn3 if rnd == 2 else xn)[:, t % 2, (4 * h + k) * P:(4 * h + k + 1) * P]
                        last = nc.tensor.transpose(job_bank(*job)[:, k * P:(k + 1) * P], src, id_f[:, :])
                    last.then_inc(mm_done, 1)

            def project_qk(b, c):
                take_bank("Q", b, c)
                if b == 0:
                    pe.wait_ge(W_lo_done, c // DC + 1)
                m = slice((c % DC) * P, (c % DC + 1) * P)
                split_mm(job_bank("Q", b, c)[:, :],
                         [((W_hi[:, c // DC, k, m], W_lo[:, c // DC, k, m]), (xT_hi[b][:, k, :], xT_lo[b][:, k, :]))
                          for k in range(KD)]).then_inc(mm_done, 1)

            def project_v(b, i):
                take_bank("V", b, i)
                if b == 0:
                    pe.wait_ge(W_lo_done, 3)
                for s in range(2):
                    m = slice((2 * i + s) * P, (2 * i + s + 1) * P)
                    last = split_mm(job_bank("V", b, i)[:, s * HD:(s + 1) * HD],
                                    [((xT_hi[b][:, k, m], xT_lo[b][:, k, m]), (W_hi[:, 2, k, :], W_lo[:, 2, k, :]))
                                     for k in range(KD)])
                last.then_inc(mm_done, 1)

            def scores(b, i):
                take_bank("S", b, i)
                if i == 0:
                    made("Q", b, 3)
                m = slice(i * P, (i + 1) * P)
                split_mm(job_bank("S", b, i)[:, :],
                         [((q_hi[b][:, c, m], q_lo[b][:, c, m]), (k_hi[b][:, c, :], k_lo[b][:, c, :]))
                          for c in range(DC)]).then_inc(mm_done, 1)

            def transpose_probs(b, i):
                take_bank("PT", b, i)
                pe.wait_ge(exp_done, b * TB + i + 1)
                for k in range(TB):
                    last = nc.tensor.transpose(job_bank("PT", b, i)[:, k * P:(k + 1) * P],
                                               probs[:, i, k * P:(k + 1) * P], id_f[:, :])
                last.then_inc(mm_done, 1)

            def mix_values(b, c):
                take_bank("O", b, c)
                if c == 0:
                    made("PT", b, TB - 1)
                m = slice(c * P, (c + 1) * P)
                split_mm(job_bank("O", b, c)[:, :],
                         [((v_hi[b][:, k, m], v_lo[b][:, k, m]), (pT_hi[:, k, :], pT_lo[:, k, :]))
                          for k in range(TB)]).then_inc(mm_done, 1)

            def project_out(t):
                if t == 0:
                    pe.wait_ge(Wo_lo_done, 1)
                if t % TB == 0:
                    made("O", t // TB, 1)
                m = slice((t % TB) * P, (t % TB + 1) * P)
                for n in range(2):
                    take_bank("WO", t, n)
                    c = slice(n * BANK, (n + 1) * BANK)
                    split_mm(job_bank("WO", t, n)[:, :],
                             [((oT_hi[:, d, m], oT_lo[:, d, m]), (Wo_hi[:, d, c], Wo_lo[:, d, c]))
                              for d in range(DC)]).then_inc(mm_done, 1)

            def column_sums(b):
                pe.wait_ge(q2_done, KD * (b + 1))
                for n in range(2):
                    take_bank("CB", b, n)
                    for k in range(KD):
                        last = nc.tensor.matmul(job_bank("CB", b, n)[:, :], ones_b[:, :],
                                                q2[b][:, k, n * BANK:(n + 1) * BANK], start=k == 0, stop=k == KD - 1)
                    last.then_inc(mm_done, 1)

            def transpose_q1(t):
                take_bank("QT", t)
                pe.wait_ge(rowsum_done, t + 1)
                dst = job_bank("QT", t)[:, :].bitcast(BF16)
                for k in range(KD):
                    last = nc.tensor.transpose(dst[:, k * P:(k + 1) * P], q1[:, t % 4, k * P:(k + 1) * P], id_b[:, :])
                last.then_inc(mm_done, 1)

            def quantised_product(t):
                made("QT", t)
                for n in range(2):
                    take_bank("XA", t, n)
                    for k in range(KD):
                        last = nc.tensor.matmul(job_bank("XA", t, n)[:, :], q1T[:, t % 2, k, :],
                                                q2[t // TB][:, k, n * BANK:(n + 1) * BANK],
                                                start=k == 0, stop=k == KD - 1)
                    last.then_inc(mm_done, 1)

            def rank_projection(b):
                take_bank("U", b)
                made("T3", TB * b + 3, 1)
                if b == 0:
                    pe.wait_ge(c1_done, 1)
                split_mm(job_bank("U", b)[0:4 * RANK, :],
                         [((c1_hi[:, k].rearrange("p s r -> p (s r)"), c1_lo[:, k].rearrange("p s r -> p (s r)")),
                           (xT_hi[b][:, k, :], xT_lo[b][:, k, :])) for k in range(KD)]).then_inc(mm_done, 1)

            def score_tile(g, t):
                if t == 0:
                    pe.wait_ge(c2_done, g + 1)
                if isinstance(g, int) and g == 0:
                    if t == 0:
                        made("U", 0)
                    else:
                        pe.wait_ge(score_read, t)
                    if t == TB:
                        made("U", 1)
                else:
                    pe.wait_ge(score_read, g * NT + t)
                nc.tensor.matmul(score_bank[:, :], u_stack[:, t * P:(t + 1) * P], c2_stack[:, :],
                                 start=True, stop=True).then_inc(score_done, 1)

            def transpose_pick(g, t):
                pe.wait_ge(pick_ready, g * NT + (t + 1))
                if isinstance(g, int) and g == 0:
                    if t > 0:
                        pe.wait_ge(maskT_copied, t)
                else:
                    pe.wait_ge(maskT_copied, g * NT + t)
                for j in range(GJ):
                    last = nc.tensor.transpose(maskT_bank[:, j * P:(j + 1) * P], pick[:, j * P:(j + 1) * P], id_b[:, :])
                last.then_inc(maskT_done, 1)

            def hidden(g, j, half):
                b = 2 * (j % 2) + half
                if half == 0:
                    pe.wait_ge(w_lo_done, g * NW + (WSEQ.index(("w1", j)) + 1))
                if j >= 2:
                    pe.wait_ge(bank_free, hidden_nth(g, j - 2, half) + 1)
                elif isinstance(g, int) and g == 0:
                    pe.wait_ge(bank_free, NJ)
                else:
                    pe.wait_ge(bank_free, unit_nth(g, prev_unit_on(b)) + (1 - PER))
                split_mm(bank[b][:, :],
                         [((w1_hi[:, j % 2, k, :], w1_lo[:, j % 2, k, :]), (xT_hi[half][:, k, :], xT_lo[half][:, k, :]))
                          for k in range(KD)]).then_inc(mm_done, 1)

            def unit_part(u, js):
                t, n = divmod(u, 2)
                m, c = slice(t * P, (t + 1) * P), slice(n * BANK, (n + 1) * BANK)
                dst = bank[UNIT_BANK[u]][:, :]
                for j in js:
                    nc.tensor.matmul(dst, h_hi[:, j, m], w2_hi[:, j, c], start=j == 0, stop=False)
                    nc.tensor.matmul(dst, h_hi[:, j, m], w2_lo[:, j, c], start=False, stop=False)
                    last = nc.tensor.matmul(dst, h_lo[:, j, m], w2_hi[:, j, c], start=False, stop=j == GJ - 1)
                return last

            def take_unit_bank(g, u):
                if u >= 6:
                    pe.wait_ge(bank_free, unit_nth(g, u - 6) + 1)
                elif UNIT_BANK[u] < 4:
                    b = UNIT_BANK[u]
                    pe.wait_ge(bank_free, hidden_nth(g, GJ - 2 + b // 2, b % 2) + 1)

            def outputs(g, last_group):
                if not last_group:
                    score_tile(g + 1, 0)
                pe.wait_ge(w_lo_done, g * NW + (WSEQ.index(("w2", 2)) + 1))
                for u in range(4):
                    take_unit_bank(g, u)
                    for j in range(GJ - 1):
                        if u == 0:
                            pe.wait_ge(bank_free, hidden_nth(g, j, 1) + 1)
                        unit_part(u, [j])
                    if u == 1 and not last_group:
                        score_tile(g + 1, 1)
                if not last_group:
                    transpose_pick(g + 1, 0)
                pe.wait_ge(w_lo_done, g * NW + NW)
                pe.wait_ge(bank_free, hidden_nth(g, GJ - 1, 1) + 1)
                for u in range(4):
                    unit_part(u, [GJ - 1]).then_inc(mm_done, 1)
                for u in range(4, 2 * NT):
                    if u % 2 == 0 and not last_group:
                        score_tile(g + 1, u // 2)
                    take_unit_bank(g, u)
                    unit_part(u, range(GJ)).then_inc(mm_done, 1)
                    if u % 2 == 1 and not last_group:
                        transpose_pick(g + 1, u // 2 - 1)
                if not last_group:
                    transpose_pick(g + 1, NT - 1)

            pe.wait_ge(ident_ready, 1)
            for t in range(TB):
                transpose_norm(0, t)
            made("T1", TB - 1, 1)
            for c in range(4):
                project_qk(0, c)
                transpose_norm(0, TB + c)
            project_v(0, 0)
            project_v(0, 1)
            for i in range(TB):
                scores(0, i)
            made("T1", NT - 1, 1)
            for c in range(4):
                project_qk(1, c)
            project_v(1, 0)
            project_v(1, 1)
            for i in range(TB):
                transpose_probs(0, i)
            made("V", 0, 1)
            mix_values(0, 0)
            mix_values(0, 1)
            for i in range(TB):
                scores(1, i)
            for t in range(TB):
                project_out(t)
            for i in range(TB):
                transpose_probs(1, i)
            made("V", 1, 1)
            mix_values(1, 0)
            mix_values(1, 1)
            for t in range(TB, NT):
                project_out(t)
            pe.wait_ge(id_b_ready, 1)
            column_sums(0)
            transpose_q1(0)
            transpose_q1(1)
            quantised_product(0)
            transpose_q1(2)
            quantised_product(1)
            transpose_q1(3)
            quantised_product(2)
            quantised_product(3)
            column_sums(1)
            transpose_q1(4)
            transpose_q1(5)
            quantised_product(4)
            transpose_q1(6)
            quantised_product(5)
            transpose_q1(7)
            transpose_norm(2, 0)
            quantised_product(6)
            transpose_norm(2, 1)
            quantised_product(7)
            transpose_norm(2, 2)
            transpose_norm(2, 3)
            rank_projection(0)
            score_tile(0, 0)
            for t in range(TB, NT):
                transpose_norm(2, t)
                if t - TB + 1 < TB:
                    score_tile(0, t - TB + 1)
                transpose_pick(0, t - TB)
            rank_projection(1)
            hidden(0, 0, 0)
            score_tile(0, 4)
            hidden(0, 0, 1)
            score_tile(0, 5)
            transpose_pick(0, 4)
            hidden(0, 1, 0)
            score_tile(0, 6)
            transpose_pick(0, 5)
            hidden(0, 1, 1)
            score_tile(0, 7)
            transpose_pick(0, 6)
            hidden(0, 2, 0)
            transpose_pick(0, 7)
            hidden(0, 2, 1)
            hidden(0, 3, 0)
            hidden(0, 3, 1)
            with pe.Fori(0, NG - 1) as g:
                outputs(g, False)
                for j in range(GJ):
                    hidden(g + 1, j, 0)
                    hidden(g + 1, j, 1)
            outputs(NG - 1, True)


def kernel(x, ctx_4096, L0_attn_Wqkv, L0_attn_bqkv, L0_attn_Wo, L0_attn_bo, L0_xattn_x1_scale, L0_xattn_x1_zp,
           L0_xattn_x2_scale, L0_xattn_x2_zp, L0_ffn_c1_w, L0_ffn_c2_w, L0_ffn_w1, L0_ffn_w2t):
    import numpy as np
    import concourse.bacc as bacc
    from concourse.bass_utils import run_bass_kernel_spmd

    x, ctx = np.asarray(x), np.asarray(ctx_4096)
    wqkv, bqkv = np.asarray(L0_attn_Wqkv), np.asarray(L0_attn_bqkv)
    B, S, D = x.shape
    HD = D // 4
    nt, kd, ni = B * S // P, D // P, L0_ffn_w1.shape[0] // P
    c1, c2, w1, w2 = (np.asarray(a) for a in (L0_ffn_c1_w, L0_ffn_c2_w, L0_ffn_w1, L0_ffn_w2t))
    rank = c1.shape[0]
    laid = {
        "x_in": x.reshape(nt, P, D),
        "ctx_in": ctx.reshape(B * kd, P, D),
        "wqkv": wqkv.reshape(kd, P, 3, HD).transpose(2, 1, 0, 3),
        "bqk": bqkv[:2 * HD].reshape(2 * HD // P, P).T,
        "bv": bqkv[2 * HD:],
        "wo": np.asarray(L0_attn_Wo).reshape(HD // P, P, D).transpose(1, 0, 2),
        "bo": np.asarray(L0_attn_bo),
        "s1": np.asarray(L0_xattn_x1_scale), "z1": np.asarray(L0_xattn_x1_zp),
        "s2": np.asarray(L0_xattn_x2_scale), "z2": np.asarray(L0_xattn_x2_zp),
        "c1": c1.T.reshape(kd, P, rank).transpose(1, 0, 2),
        "c2": c2.reshape(-1, BANK, rank).transpose(0, 2, 1),
        "w1": w1.reshape(ni, P, kd, P).transpose(0, 3, 2, 1).reshape(ni, P, D),
        "w2": w2.reshape(ni, P, D),
    }
    arrays = {n: np.ascontiguousarray(a) for n, a in laid.items()}
    nc = bacc.Bacc("TRN2", target_bir_lowering=False, num_devices=1)
    args = [nc.dram_tensor(n, a.shape, mybir.dt.from_np(a.dtype), kind="ExternalInput").ap() for n, a in arrays.items()]
    out = nc.dram_tensor("out", (nt, P, D), F32, kind="ExternalOutput").ap()
    decoder_layer(nc, *args, out)
    r = run_bass_kernel_spmd(nc, [arrays], core_ids=[0])
    return r.results[0]["out"].reshape(B, S, D)
```

```python
from contextlib import ExitStack

import concourse.bass as bass
from concourse import mybir

P = 128
F32 = mybir.dt.float32
F32R = mybir.dt.float32r
BF16 = mybir.dt.bfloat16
ALU = mybir.AluOpType
ACT = mybir.ActivationFunctionType
AX = mybir.AxisListType

KB = 1024
BANK = 512
RING = 6
EPS = 1e-5
ROUND = 12582912.0
QMAX = 255.0
CENTRE = 128.0


def job_order():
    both = lambda kind, a: [(kind, a, 0), (kind, a, 1)]
    jobs = both("T1", 0) + both("T1", 1) + [("V", 0, 0)] + both("T1", 2) + both("T1", 3) + [("V", 0, 1)]
    jobs += [("Q", 0, 0), ("Q", 0, 1)] + both("T1", 4) + [("Q", 0, 2)] + both("T1", 5)
    jobs += [("Q", 0, 3)] + both("T1", 6) + both("T1", 7)
    jobs += [("S", 0, i) for i in range(4)]
    jobs += [("Q", 1, c) for c in range(4)] + both("V", 1)
    jobs += [("PT", 0, i) for i in range(4)] + [("S", 1, i) for i in range(4)] + both("O", 0)
    jobs += [("PT", 1, i) for i in range(4)]
    for t in range(4):
        jobs += both("WO", t)
    jobs += both("O", 1) + both("CB", 0)
    for t in range(4, 8):
        jobs += both("WO", t)
    jobs += both("CB", 1)
    for t in range(6):
        jobs += both("XA", t)
    jobs += both("T3", 0) + both("T3", 1) + both("XA", 6) + both("T3", 2) + both("T3", 3) + both("XA", 7)
    jobs += both("T3", 4) + [("U", 0)] + both("T3", 5) + both("T3", 6) + both("T3", 7) + [("U", 1)]
    return jobs


JOBS = job_order()
NJ = len(JOBS)
HIDDEN_0 = [(0, 0), (1, 0), (0, 1), (1, 1), (2, 0), (2, 1), (3, 0), (3, 1)]
CHAINS = [(0, 0, 2), (0, 2, 2), (0, 4, 4), (1, 0, 4), (1, 4, 4), (2, 0, 4), (2, 4, 2), (2, 6, 2)]
W_ORDER = (2, 0, 1)
HI_KINDS = ("T1", "Q", "V", "PT", "O", "T3")


def nth(*job):
    return JOBS.index(job)


def nth_hi(*job):
    return sum(j[0] in HI_KINDS for j in JOBS[:nth(*job)])


def nth_chain(rnd, t):
    return next(n for n, (r, first, count) in enumerate(CHAINS) if r == rnd and first <= t < first + count)


def decoder_layer(nc, x_in, ctx_in, wqkv, bqk, bv, wo, bo, s1, z1, s2, z2, c1, c2, w1, w2, out):
    D = x_in.shape[2]
    NT = x_in.shape[0]
    NB = 2
    TB = NT // NB
    KD = D // P
    HD = wqkv.shape[3]
    DC = HD // P
    RANK = c1.shape[2]
    BLK = 64
    NG = c2.shape[0]
    GH = c2.shape[2]
    GJ = GH // P
    SB = TB * P
    SCALE = 1.0 / 16.0
    assert (D, NT, HD, GH, SB, HD ** 0.5) == (1024, 8, 256, BANK, BANK, 1 / SCALE)

    base = (nc.sbuf_base + 31) // 32 * 32

    def at(name, kb, shape, dt):
        t = nc.alloc_sbuf_tensor_at(name, shape, dt, offset=base + int(kb * KB))
        size = 2 if dt == BF16 else 4
        for d in shape[1:]:
            size *= d
        assert base + int(kb * KB) + size <= nc.sbuf_usable_end, name
        return t

    x = at("x", 0, [P, NT, D], F32)
    xT_hi = [at(f"xT_hi{b}", 32 + 32 * b, [P, KD, SB], F32R) for b in range(NB)]
    xT_lo = [at(f"xT_lo{b}", 48 + 32 * b, [P, KD, SB], F32R) for b in range(NB)]
    W_hi = at("W_hi", 96, [P, 3, KD, HD], F32R)
    W_lo = at("W_lo", 120, [P, 3, KD, HD], F32R)
    W_raw = at("W_raw", 168, [P, 3, KD, HD], F32)
    q_hi, q_lo, k_hi, k_lo, v_hi, v_lo = (
        [at(f"{n}{b}", 144 + 24 * b + 4 * i, [P, TB, HD] if n[0] == "v" else [P, DC, SB], F32R) for b in range(NB)]
        for i, n in enumerate(("q_hi", "q_lo", "k_hi", "k_lo", "v_hi", "v_lo")))
    xn = at("xn", 192, [P, 2, D], F32)
    ctx_raw = at("ctx_raw", 48, [P, 2, D], F32)
    ctx_slot = [ctx_raw[:, 0, :], ctx_raw[:, 1, :], xn[:, 0, :], xn[:, 1, :]]
    probs = at("probs", 56, [P, TB, SB], F32)
    q2 = [at("q2_0", 32, [P, KD, D], BF16), at("q2_1", 96, [P, KD, D], BF16)]
    pT_hi = at("pT_hi", 64, [P, TB, SB], F32R)
    pT_lo = at("pT_lo", 72, [P, TB, SB], F32R)
    oT_hi = at("oT_hi", 80, [P, DC, SB], F32R)
    oT_lo = at("oT_lo", 84, [P, DC, SB], F32R)
    Wo_raw = at("Wo_raw", 88, [P, DC, D], F32)
    Wo_hi = at("Wo_hi", 112, [P, DC, D], F32R)
    Wo_lo = at("Wo_lo", 120, [P, DC, D], F32R)
    corr = at("corr", 128, [P, NB, D], F32)
    q1 = at("q1", 136, [P, 4, D], BF16)
    q1T = at("q1T", 160, [P, 2, KD, P], BF16)
    xn3 = at("xn3", 112, [P, 2, D], F32)
    c1_raw = at("c1_raw", 120, [P, KD, RANK], F32)
    c1_hi = at("c1_hi", 121, [P, KD, 4, RANK], F32R)
    c1_lo = at("c1_lo", 123, [P, KD, 4, RANK], F32R)
    u_hi = at("u_hi", 125, [4 * RANK, SB], F32)
    u_lo = at("u_lo", 203, [4 * RANK, SB], F32)
    h_hi = at("h_hi", 96, [P, GJ, NT * P], F32R)
    h_lo = at("h_lo", 112, [P, GJ, NT * P], F32R)
    w2_lo = at("w2_lo", 128, [P, GJ, D], F32R)
    w1_hi = at("w1_hi", 144, [P, 2, KD, P], F32R)
    w1_lo = at("w1_lo", 152, [P, 2, KD, P], F32R)
    w2_hi = at("w2_hi", 160, [P, GJ, D], F32R)
    w_raw = at("w_raw", 176, [P, 2, D], F32)
    maskT = at("maskT", 184, [P, GJ, NT * P], BF16)
    u_stack = at("u_stack", 192, [4 * RANK, NT * P], F32R)
    c2_raw = at("c2_raw", 196, [4 * RANK, GH], F32)
    c2_stack = at("c2_stack", 198, [4 * RANK, GH], F32R)
    cand = at("cand", 200, [P, GH], BF16)
    pick = at("pick", 201, [P, GH], BF16)
    order = at("order", 202, [P, GH], BF16)
    bo_b = at("bo_b", 200, [P, D], F32)
    bv_b = at("bv_b", 204, [P, HD], F32)
    smalls = [205.0]

    def small(name, shape, dt):
        t = at(name, smalls[0], shape, dt)
        size = 2 if dt == BF16 else 4
        for d in shape[1:]:
            size *= d
        smalls[0] += (size + 31) // 32 * 32 / KB
        return t

    id_f = small("id_f", [P, P], F32)
    id_b = small("id_b", [P, P], BF16)
    ones_b = small("ones_b", [P, P], BF16)
    bqk_s = small("bqk_s", [P, 2 * DC], F32)
    stats = small("stats", [P, NT, 12], F32)
    mv = small("mv", [P, NT, 2], F32)
    veps = small("veps", [P, NT], F32)
    sdev = small("sdev", [P, NT], F32)
    rinv = small("rinv", [P, NT], F32)
    newt = small("newt", [P, NT], F32)
    rstd = small("rstd", [P, NT], F32)
    nmr = small("nmr", [P, NT], F32)
    qp = small("qp", [P, 4], F32)
    qd = small("qd", [P, 8], F32)
    inv1, inv2, s12, d1, d2, cs, rb_mul, rb_add = (qd[:, i:i + 1] for i in range(8))
    smax = small("smax", [P, NT], F32)
    nbias = small("nbias", [P, NT], F32)
    qmul = small("qmul", [P, NT], F32)
    qadd = small("qadd", [P, NT], F32)
    psum_row = small("psum_row", [P, NT], F32)
    pinv = small("pinv", [P, NT], F32)
    rowbias = small("rowbias", [P, NT], F32)
    mslot = small("mslot", [4 * RANK, 2], F32)
    bmax = small("bmax", [P, GH // BLK], F32)
    cmax = small("cmax", [P, GH // BLK], BF16)

    with ExitStack() as ctx:
        bank = [ctx.enter_context(nc.psum_tensor(f"bank{i}", [P, BANK], F32)) for i in range(8)]
        score_bank = bank[6]
        rowsum = bank[6][:, 0:NT]
        q1T_bank = bank[7][:, :].bitcast(BF16)
        maskT_bank = bank[7][:, 0:BANK // 2].bitcast(BF16)

        def sem(name):
            return ctx.enter_context(nc.semaphore(name))

        x_loaded = [sem(f"x_loaded{t}") for t in range(NT)]
        W_loaded = [[sem(f"W_loaded{i}_{h}") for h in range(2)] for i in range(3)]
        bias_loaded = sem("bias_loaded")
        qp_loaded = sem("qp_loaded")
        ctx_loaded = [sem(f"ctx_loaded{i}") for i in range(4)]
        Wo_loaded = sem("Wo_loaded")
        c1_loaded = sem("c1_loaded")
        c2_loaded = sem("c2_loaded")
        w_loaded = [sem(f"w_loaded{i}") for i in range(2)]
        stored = sem("stored")
        ident_zeroed = sem("ident_zeroed")
        ident_ready = sem("ident_ready")
        id_b_ready = sem("id_b_ready")
        order_ready = sem("order_ready")
        qp_ready = sem("qp_ready")
        mm_done = sem("mm_done")
        hi_done = sem("hi_done")
        bank_free = sem("bank_free")
        vec = sem("vec")
        mv_done = sem("mv_done")
        veps_ready = sem("veps_ready")
        sdev_ready = sem("sdev_ready")
        rstd_ready = sem("rstd_ready")
        normed = sem("normed")
        vbias_added = sem("vbias_added")
        W_hi_done = sem("W_hi_done")
        W_lo_done = sem("W_lo_done")
        bo_added = sem("bo_added")
        nbias_ready = sem("nbias_ready")
        exp_done = sem("exp_done")
        Wo_hi_done = sem("Wo_hi_done")
        Wo_lo_done = sem("Wo_lo_done")
        ctx_scaled = sem("ctx_scaled")
        ctx_rounded = sem("ctx_rounded")
        q2_done = sem("q2_done")
        q1_rounded = sem("q1_rounded")
        q1_done = sem("q1_done")
        q1T_done = sem("q1T_done")
        q1T_copied = sem("q1T_copied")
        rowsum_done = sem("rowsum_done")
        rowbias_ready = sem("rowbias_ready")
        xa_scaled = sem("xa_scaled")
        corr_added = sem("corr_added")
        c1_done = sem("c1_done")
        w_hi_done = sem("w_hi_done")
        w_lo_done = sem("w_lo_done")
        c2_done = sem("c2_done")
        score_done = sem("score_done")
        score_read = sem("score_read")
        pick_ready = sem("pick_ready")
        maskT_done = sem("maskT_done")
        maskT_copied = sem("maskT_copied")
        relu_masked = sem("relu_masked")
        h_hi_done = sem("h_hi_done")

        def job_bank(*job):
            return bank[nth(*job) % RING]

        PER = 2 * GJ + 2 * NT
        WSEQ = [("w1", 0), ("w1", 1), ("w2", 0), ("w2", 1), ("w1", 2), ("w2", 2), ("w1", 3), ("w2", 3)]
        NW = len(WSEQ)
        UNIT_BANK = [(0, 1, 4, 5, 2, 3)[u % 6] for u in range(2 * NT)]

        def hidden_nth(g, j, half):
            return g * PER + (NJ + hidden_pos(g, j, half))

        def unit_nth(g, u):
            return g * PER + (NJ + 2 * GJ + u)

        def hidden_pos(g, j, half):
            return HIDDEN_0.index((j, half)) if isinstance(g, int) and g == 0 else 2 * j + half

        def prev_unit_on(b):
            return max(u for u in range(2 * NT) if UNIT_BANK[u] == b)

        block = ctx.enter_context(nc.Block())

        @block.sync
        def _(sp):
            def load_x(*tiles):
                for t in tiles:
                    sp.dma_start(x[:, t, :], x_in[t]).then_inc(x_loaded[t], 16)

            def load_W(i):
                for h in range(2):
                    k = slice(h * KD // 2, (h + 1) * KD // 2)
                    sp.dma_start(W_raw[:, i, k, :], wqkv[i][:, k, :]).then_inc(W_loaded[i][h], 16)

            load_x(0, 1)
            load_W(W_ORDER[0])
            load_x(2, 3)
            for dst, src in ((bqk_s[:, :], bqk), (bv_b[:, :], bv.partition_broadcast(P)),
                             (bo_b[:, :], bo.partition_broadcast(P))):
                sp.dma_start(dst, src).then_inc(bias_loaded, 16)
            load_W(W_ORDER[1])
            load_x(4, 5)
            load_W(W_ORDER[2])
            load_x(6, 7)
            for i, src in enumerate((s1, z1, s2, z2)):
                sp.dma_start(qp[:, i:i + 1], src.partition_broadcast(P)).then_inc(qp_loaded, 16)
            sp.wait_ge(mm_done, nth("T1", 7, 1) + 1)
            for i in range(NB * KD):
                if i >= 4:
                    sp.wait_ge(q2_done, i - 3)
                sp.dma_start(ctx_slot[i % 4], ctx_in[i]).then_inc(ctx_loaded[i % 4], 16)

            def load_w(which, j, g, slot):
                src = w1 if which == "w1" else w2
                sp.dma_start(w_raw[:, slot, :], src[g * GJ + j]).then_inc(w_loaded[slot], 16)

            def load_c2(g):
                for i in range(4):
                    sp.dma_start(c2_raw[RANK * i:RANK * (i + 1), :], c2[g]).then_inc(c2_loaded, 16)

            sp.wait_ge(mm_done, nth("O", 1, 1) + 1)
            load_w(*WSEQ[0], 0, 0)
            load_w(*WSEQ[1], 0, 1)
            sp.wait_ge(mm_done, nth("WO", 7, 1) + 1)
            sp.dma_start(c1_raw[:, :, :], c1).then_inc(c1_loaded, 16)
            sp.wait_ge(q1_done, NT)
            load_c2(0)

            def group(g, last):
                if not last:
                    sp.wait_ge(c2_done, g + 1)
                    load_c2(g + 1)
                for i in range(NW - 2 if last else NW):
                    sp.wait_ge(w_lo_done, g * NW + (i + 1))
                    which, j = WSEQ[(i + 2) % NW]
                    load_w(which, j, g + 1 if i + 2 >= NW else g, i % 2)

            with sp.Fori(0, NG - 1) as g:
                group(g, False)
            group(NG - 1, True)
            for t in range(NT):
                sp.wait_ge(bank_free, unit_nth(NG - 1, 2 * t + 1) + 1)
                sp.dma_start(out[t], x[:, t, :]).then_inc(stored, 16)
            sp.wait_ge(stored, 16 * NT)

        @block.gpsimd
        def _(pool):
            nc.gpsimd.memset(id_f[:, :], 0.0).then_inc(ident_zeroed, 1)
            pool.wait_ge(ident_zeroed, 1)
            nc.gpsimd.affine_select(out=id_f[:, :], in_=id_f[:, :], compare_op=ALU.not_equal, fill=1.0,
                                    base=0, pattern=[[-1, P]], channel_multiplier=1).then_inc(ident_ready, 1)
            for n, i in enumerate(W_ORDER):
                for h in range(2):
                    pool.wait_ge(W_hi_done, 2 * n + h + 1)
                    k = slice(h * KD // 2, (h + 1) * KD // 2)
                    nc.gpsimd.tensor_tensor(W_lo[:, i, k, :], W_raw[:, i, k, :], W_hi[:, i, k, :].bitcast(F32),
                                            ALU.subtract).then_inc(W_lo_done, 1)
            pool.wait_ge(bias_loaded, 48)
            for t in range(NT):
                pool.wait_ge(normed, t + 1)
                nc.gpsimd.tensor_tensor(x[:, t, :], x[:, t, :], bo_b[:, :], ALU.add).then_inc(bo_added, 1)
            for i in range(NB * KD):
                pool.wait_ge(ctx_rounded, i + 1)
                if i == KD:
                    pool.wait_ge(mm_done, nth("Q", 1, 3) + 1)
                nc.gpsimd.tensor_scalar(q2[i // KD][:, i % KD, :], ctx_slot[i % 4], -(ROUND + CENTRE), 1.0,
                                        ALU.add, ALU.mult).then_inc(q2_done, 1)
            def centre_q1(t):
                pool.wait_ge(q1_rounded, t + 1)
                if t == 0:
                    pool.wait_ge(mm_done, nth("V", 1, 1) + 1)
                if t >= 4:
                    pool.wait_ge(q1T_done, t - 3)
                nc.gpsimd.tensor_scalar(q1[:, t % 4, :], xn[:, t % 2, :], -(ROUND + CENTRE), 1.0,
                                        ALU.add, ALU.mult).then_inc(q1_done, 1)

            def add_corr(t):
                pool.wait_ge(normed, NT + t + 1)
                pool.wait_ge(bank_free, nth("CB", t // TB, 1) + 1)
                nc.gpsimd.tensor_tensor(x[:, t, :], x[:, t, :], corr[:, t // TB, :], ALU.add).then_inc(corr_added, 1)

            for b in range(NB):
                for t in range(TB):
                    centre_q1(b * TB + t)
                for t in range(TB):
                    add_corr(b * TB + t)
            nc.gpsimd.iota(order[:, :].rearrange("p (b w) -> p b w", w=BLK), pattern=[[0, GH // BLK], [-1, BLK]],
                           base=BLK, channel_multiplier=0,
                           allow_small_or_imprecise_dtypes=True).then_inc(order_ready, 1)

            def cut_w(g, i):
                which, j = WSEQ[i % NW]
                pool.wait_ge(w_hi_done, g * NW + (i + 1))
                hi, lo = (w1_hi[:, j % 2], w1_lo[:, j % 2]) if which == "w1" else (w2_hi[:, j], w2_lo[:, j])
                raw = w_raw[:, i % 2, :]
                if which == "w1":
                    raw = raw.rearrange("p (k m) -> p k m", k=KD)
                nc.gpsimd.tensor_tensor(lo, raw, hi.bitcast(F32), ALU.subtract).then_inc(w_lo_done, 1)

            cut_w(0, 0)
            cut_w(0, 1)
            for i in range(2, NW):
                cut_w(0, i)
            with pool.Fori(1, NG) as g:
                for i in range(NW):
                    cut_w(g, i)

        @block.scalar
        def _(act):
            def roots(rnd, t):
                n = nth_chain(rnd, t)
                s = slice(t, t + CHAINS[n][2])
                act.wait_ge(veps_ready, n + 1)
                nc.scalar.activation(sdev[:, s], veps[:, s], ACT.Sqrt).then_inc(sdev_ready, 1)

            def norm(rnd, t):
                act.wait_ge(rstd_ready, nth_chain(rnd, t) + 1)
                if rnd == 0 and t >= 2:
                    act.wait_ge(mm_done, nth("T1", t - 2, 1) + 1)
                if rnd == 1 and t < 2:
                    act.wait_ge(q2_done, 2 * KD - 1 + t)
                if rnd == 1 and t >= 2:
                    act.wait_ge(q1_done, t - 1)
                if rnd == 2 and t >= 2:
                    act.wait_ge(mm_done, nth("T3", t - 2, 1) + 1)
                dst = (xn3 if rnd == 2 else xn)[:, t % 2, :]
                mul, add = (qmul, qadd) if rnd == 1 else (rstd, nmr)
                nc.scalar.activation(dst, x[:, t, :], ACT.Identity, bias=add[:, t:t + 1],
                                     scale=mul[:, t:t + 1]).then_inc(normed, 1)

            def hi_T(rnd, t, h):
                job = ("T1" if rnd == 0 else "T3", t, h)
                act.wait_ge(mm_done, nth(*job) + 1)
                nc.scalar.activation(
                    xT_hi[t // TB][:, 4 * h:4 * h + 4, (t % TB) * P:(t % TB + 1) * P],
                    job_bank(*job)[:, :].rearrange("p (k m) -> p k m", k=4), ACT.Copy).then_inc(hi_done, 1)

            def hi_W(i, h):
                act.wait_ge(W_loaded[i][h], 16)
                k = slice(h * KD // 2, (h + 1) * KD // 2)
                nc.scalar.activation(W_hi[:, i, k, :], W_raw[:, i, k, :], ACT.Copy).then_inc(W_hi_done, 1)

            def hi_Q(b, c):
                act.wait_ge(mm_done, nth("Q", b, c) + 1)
                if b == 0 and c == 0:
                    act.wait_ge(bias_loaded, 48)
                if b == 1 and c == 0:
                    act.wait_ge(W_lo_done, 6)
                dst = (q_hi if c < DC else k_hi)[b]
                nc.scalar.activation(dst[:, c % DC, :], job_bank("Q", b, c)[:, :], ACT.Identity,
                                     bias=bqk_s[:, c:c + 1], scale=1.0).then_inc(hi_done, 1)

            def hi_V(b, i):
                act.wait_ge(vbias_added, 2 * b + i + 1)
                nc.scalar.activation(v_hi[b][:, 2 * i:2 * i + 2, :],
                                     job_bank("V", b, i)[:, :].rearrange("p (t d) -> p t d", t=2),
                                     ACT.Copy).then_inc(hi_done, 1)

            def exp(b, i):
                n = b * TB + i
                act.wait_ge(nbias_ready, n + 1)
                if b == 0 and i == 0:
                    act.wait_ge(mm_done, nth("V", 0, 1) + 1)
                if b == 1:
                    act.wait_ge(mm_done, nth("PT", 0, i) + 1)
                nc.scalar.activation(probs[:, i, :], job_bank("S", b, i)[:, :], ACT.Exp, bias=nbias[:, n:n + 1],
                                     scale=SCALE, accum_out=psum_row[:, n:n + 1]).then_inc(exp_done, 1)

            def hi_PT(b, i):
                act.wait_ge(mm_done, nth("PT", b, i) + 1)
                nc.scalar.activation(pT_hi[:, :, i * P:(i + 1) * P],
                                     job_bank("PT", b, i)[:, :].rearrange("p (k m) -> p k m", k=TB),
                                     ACT.Copy).then_inc(hi_done, 1)

            def hi_O(b, c):
                act.wait_ge(mm_done, nth("O", b, c) + 1)
                nc.scalar.activation(oT_hi[:, c, :], job_bank("O", b, c)[:, :], ACT.Copy).then_inc(hi_done, 1)

            def scale_ctx(i):
                act.wait_ge(ctx_loaded[i % 4], 16 * (i // 4 + 1))
                nc.scalar.activation(ctx_slot[i % 4], ctx_slot[i % 4], ACT.Copy,
                                     scale=inv2).then_inc(ctx_scaled, 1)

            def copy_q1T(t):
                act.wait_ge(q1T_done, t + 1)
                if t >= 2:
                    act.wait_ge(mm_done, nth("XA", t - 2, 1) + 1)
                nc.scalar.activation(q1T[:, t % 2, :, :], q1T_bank.rearrange("p (k m) -> p k m", k=KD),
                                     ACT.Copy).then_inc(q1T_copied, 1)

            def scale_xa(t):
                act.wait_ge(rowbias_ready, t + 1)
                for n in range(2):
                    act.wait_ge(mm_done, nth("XA", t, n) + 1)
                    pb = job_bank("XA", t, n)
                    nc.scalar.activation(pb[:, :], pb[:, :], ACT.Identity, bias=rowbias[:, t:t + 1],
                                         scale=s12).then_inc(xa_scaled, 1)

            def hi_w(g, i):
                which, j = WSEQ[i % NW]
                act.wait_ge(w_loaded[i % 2], g * (16 * NW // 2) + 16 * (i // 2 + 1))
                if which == "w1":
                    gg, jj = (g + i // NW, j - 2) if j >= 2 else (g + i // NW - 1, j + 2)
                    if isinstance(gg, int) and gg < 0:
                        act.wait_ge(mm_done, nth("O", 0, 1) + 1)
                    else:
                        act.wait_ge(mm_done, hidden_nth(gg, jj, 1) + 1)
                    dst = w1_hi[:, j % 2]
                else:
                    act.wait_ge(mm_done, hidden_nth(g, 0, 0))
                    dst = w2_hi[:, j]
                raw = w_raw[:, i % 2, :]
                if which == "w1":
                    raw = raw.rearrange("p (k m) -> p k m", k=KD)
                nc.scalar.activation(dst, raw, ACT.Copy).then_inc(w_hi_done, 1)

            def both(f, *a):
                f(*a, 0)
                f(*a, 1)

            roots(0, 0)
            hi_W(W_ORDER[0], 0)
            norm(0, 0)
            norm(0, 1)
            hi_W(W_ORDER[0], 1)
            both(hi_T, 0, 0)
            both(hi_T, 0, 1)
            roots(0, 2)
            norm(0, 2)
            norm(0, 3)
            both(hi_W, W_ORDER[1])
            hi_V(0, 0)
            both(hi_T, 0, 2)
            both(hi_T, 0, 3)
            both(hi_W, W_ORDER[2])
            hi_V(0, 1)
            roots(0, 4)
            norm(0, 4)
            norm(0, 5)
            hi_Q(0, 0)
            hi_Q(0, 1)
            both(hi_T, 0, 4)
            norm(0, 6)
            hi_Q(0, 2)
            both(hi_T, 0, 5)
            norm(0, 7)
            hi_Q(0, 3)
            both(hi_T, 0, 6)
            both(hi_T, 0, 7)
            for i in range(TB):
                exp(0, i)
            act.wait_ge(qp_ready, 1)
            for i in range(4):
                scale_ctx(i)
            for c in range(4):
                hi_Q(1, c)
                scale_ctx(2 * c + 4)
                scale_ctx(2 * c + 5)
            hi_V(1, 0)
            scale_ctx(12)
            scale_ctx(13)
            hi_V(1, 1)
            act.wait_ge(mm_done, nth("V", 1, 1) + 1)
            act.dma_start(Wo_raw[:, :, :], wo).then_inc(Wo_loaded, 16)
            for i in range(TB):
                hi_PT(0, i)
            act.wait_ge(Wo_loaded, 16)
            nc.scalar.activation(Wo_hi[:, :, :], Wo_raw[:, :, :], ACT.Copy).then_inc(Wo_hi_done, 1)
            for i in range(TB):
                exp(1, i)
            scale_ctx(14)
            scale_ctx(15)
            hi_O(0, 0)
            hi_O(0, 1)
            for i in range(TB):
                hi_PT(1, i)
            roots(1, 0)
            norm(1, 0)
            norm(1, 1)
            hi_O(1, 0)
            hi_O(1, 1)
            norm(1, 2)
            norm(1, 3)
            copy_q1T(0)
            copy_q1T(1)
            roots(1, 4)
            norm(1, 4)
            norm(1, 5)
            scale_xa(0)
            copy_q1T(2)
            norm(1, 6)
            scale_xa(1)
            norm(1, 7)
            copy_q1T(3)
            scale_xa(2)
            copy_q1T(4)
            scale_xa(3)
            copy_q1T(5)
            roots(2, 0)
            scale_xa(4)
            norm(2, 0)
            norm(2, 1)
            copy_q1T(6)
            scale_xa(5)
            both(hi_T, 2, 0)
            both(hi_T, 2, 1)
            norm(2, 2)
            copy_q1T(7)
            norm(2, 3)
            roots(2, 4)
            scale_xa(6)
            both(hi_T, 2, 2)
            both(hi_T, 2, 3)
            norm(2, 4)
            scale_xa(7)
            norm(2, 5)
            hi_w(0, 0)
            roots(2, 6)

            def copy_maskT(g, t):
                act.wait_ge(maskT_done, g * NT + (t + 1))
                if not (isinstance(g, int) and g == 0):
                    act.wait_ge(relu_masked, g * 2 * GJ)
                nc.scalar.activation(maskT[:, :, t * P:(t + 1) * P],
                                     maskT_bank.rearrange("p (j m) -> p j m", j=GJ),
                                     ACT.Copy).then_inc(maskT_copied, 1)

            def hi_h(g, j, half):
                act.wait_ge(relu_masked, g * 2 * GJ + (hidden_pos(g, j, half) + 1))
                nc.scalar.activation(h_hi[:, j, half * SB:(half + 1) * SB], bank[2 * (j % 2) + half][:, :],
                                     ACT.Copy).then_inc(h_hi_done, 1)

            both(hi_T, 2, 4)
            norm(2, 6)
            norm(2, 7)
            both(hi_T, 2, 5)
            hi_w(0, 1)
            both(hi_T, 2, 6)
            both(hi_T, 2, 7)
            copy_maskT(0, 0)
            hi_w(0, 2)
            hi_w(0, 3)
            copy_maskT(0, 1)
            copy_maskT(0, 2)
            copy_maskT(0, 3)
            hi_h(0, 0, 0)
            hi_h(0, 1, 0)
            hi_w(0, 4)
            copy_maskT(0, 4)
            copy_maskT(0, 5)
            hi_w(0, 5)
            hi_w(0, 6)
            copy_maskT(0, 6)
            copy_maskT(0, 7)
            hi_h(0, 0, 1)
            hi_h(0, 1, 1)
            both(hi_h, 0, 2)
            hi_w(0, 7)
            both(hi_h, 0, 3)
            with act.Fori(0, NG - 1) as g:
                for t in range(NT - 1):
                    copy_maskT(g + 1, t)
                    if t == 2:
                        hi_w(g, NW)
                    if t == 4:
                        hi_w(g, NW + 1)
                hi_w(g + 1, 2)
                hi_w(g + 1, 3)
                copy_maskT(g + 1, NT - 1)
                both(hi_h, g + 1, 0)
                hi_w(g + 1, 4)
                hi_w(g + 1, 5)
                both(hi_h, g + 1, 1)
                hi_w(g + 1, 6)
                hi_w(g + 1, 7)
                both(hi_h, g + 1, 2)
                both(hi_h, g + 1, 3)

        @block.vector
        def _(dve):
            chained = [0]

            def link(ins, off=0):
                chained[0] += 1
                ins.then_inc(vec, 1)
                dve.wait_ge(vec, chained[0] + off)

            def free(ins):
                ins.then_inc(bank_free, 1)

            def stats_of(t, *job):
                if job:
                    dve.wait_ge(bank_free, nth(*job) + 1)
                nc.vector.bn_stats(stats[:, t, 0:6], x[:, t, 0:BANK])
                link(nc.vector.bn_stats(stats[:, t, 6:12], x[:, t, BANK:D]))
                nc.vector.bn_aggr(mv[:, t, :], stats[:, t, :]).then_inc(mv_done, 1)

            def add_eps(rnd, t):
                n = nth_chain(rnd, t)
                s = slice(t, t + CHAINS[n][2])
                dve.wait_ge(mv_done, rnd * NT + s.stop)
                nc.vector.tensor_scalar(veps[:, s], mv[:, s, 1], EPS, None, ALU.add).then_inc(veps_ready, 1)

            def norm_scale(rnd, t):
                n = nth_chain(rnd, t)
                s = slice(t, t + CHAINS[n][2])
                dve.wait_ge(sdev_ready, n + 1)
                link(nc.vector.reciprocal(rinv[:, s], sdev[:, s]))
                link(nc.vector.tensor_tensor(newt[:, s], veps[:, s], rinv[:, s], ALU.mult))
                link(nc.vector.tensor_tensor(newt[:, s], newt[:, s], rinv[:, s], ALU.mult))
                link(nc.vector.tensor_scalar(newt[:, s], newt[:, s], -0.5, 1.5, ALU.mult, ALU.add))
                link(nc.vector.tensor_tensor(rstd[:, s], newt[:, s], rinv[:, s], ALU.mult))
                ins = nc.vector.scalar_tensor_tensor(nmr[:, s], mv[:, s, 0], -1.0, rstd[:, s], ALU.mult, ALU.mult)
                if rnd == 1:
                    link(ins)
                    nc.vector.tensor_scalar(qmul[:, s], rstd[:, s], inv1, None, ALU.mult)
                    ins = nc.vector.tensor_scalar(qadd[:, s], nmr[:, s], inv1, None, ALU.mult)
                ins.then_inc(rstd_ready, 1)

            def lo_T(rnd, t):
                for h in range(2):
                    job = ("T1" if rnd == 0 else "T3", t, h)
                    dve.wait_ge(hi_done, nth_hi(*job) + 1)
                    k, m = slice(4 * h, 4 * h + 4), slice((t % TB) * P, (t % TB + 1) * P)
                    free(nc.vector.tensor_tensor(
                        xT_lo[t // TB][:, k, m], job_bank(*job)[:, :].rearrange("p (k m) -> p k m", k=4),
                        xT_hi[t // TB][:, k, m].bitcast(F32), ALU.subtract))

            def lo_Q(b, c):
                dve.wait_ge(hi_done, nth_hi("Q", b, c) + 1)
                hi, lo = (q_hi, q_lo) if c < DC else (k_hi, k_lo)
                free(nc.vector.scalar_tensor_tensor(
                    lo[b][:, c % DC, :], job_bank("Q", b, c)[:, :], bqk_s[:, c:c + 1],
                    hi[b][:, c % DC, :].bitcast(F32), ALU.add, ALU.subtract))

            def lo_V(b, i):
                pv = job_bank("V", b, i)[:, :].rearrange("p (t d) -> p t d", t=2)
                dve.wait_ge(mm_done, nth("V", b, i) + 1)
                nc.vector.tensor_tensor(
                    pv, pv, bv_b[:, :].rearrange("p (o d) -> p o d", o=1).to_broadcast([P, 2, HD]),
                    ALU.add).then_inc(vbias_added, 1)
                dve.wait_ge(hi_done, nth_hi("V", b, i) + 1)
                free(nc.vector.tensor_tensor(v_lo[b][:, 2 * i:2 * i + 2, :], pv,
                                             v_hi[b][:, 2 * i:2 * i + 2, :].bitcast(F32), ALU.subtract))

            def maxima(b):
                for i in range(TB):
                    n = b * TB + i
                    dve.wait_ge(mm_done, nth("S", b, i) + 1)
                    link(nc.vector.reduce_max(smax[:, n:n + 1], job_bank("S", b, i)[:, :], AX.X))
                    nc.vector.tensor_scalar(nbias[:, n:n + 1], smax[:, n:n + 1], -SCALE, None,
                                            ALU.mult).then_inc(nbias_ready, 1)

            def inverse_sums(b):
                for i in range(TB):
                    n = b * TB + i
                    dve.wait_ge(exp_done, n + 1)
                    free(nc.vector.reciprocal(pinv[:, n:n + 1], psum_row[:, n:n + 1]))

            def lo_PT(b, i):
                dve.wait_ge(hi_done, nth_hi("PT", b, i) + 1)
                m = slice(i * P, (i + 1) * P)
                free(nc.vector.tensor_tensor(pT_lo[:, :, m],
                                             job_bank("PT", b, i)[:, :].rearrange("p (k m) -> p k m", k=TB),
                                             pT_hi[:, :, m].bitcast(F32), ALU.subtract))

            def lo_O(b, c):
                dve.wait_ge(hi_done, nth_hi("O", b, c) + 1)
                free(nc.vector.tensor_tensor(oT_lo[:, c, :], job_bank("O", b, c)[:, :],
                                             oT_hi[:, c, :].bitcast(F32), ALU.subtract))

            def add_WO(t):
                dve.wait_ge(bo_added, t + 1)
                for n in range(2):
                    dve.wait_ge(mm_done, nth("WO", t, n) + 1)
                    c = slice(n * BANK, (n + 1) * BANK)
                    free(nc.vector.scalar_tensor_tensor(x[:, t, c], job_bank("WO", t, n)[:, :], pinv[:, t:t + 1],
                                                        x[:, t, c], ALU.mult, ALU.add))

            def round_ctx(i):
                r = ctx_slot[i % 4]
                dve.wait_ge(ctx_scaled, i + 1)
                link(nc.vector.tensor_scalar(r, r, qp[:, 3:4], ROUND, ALU.add, ALU.add))
                nc.vector.tensor_scalar(r, r, ROUND, ROUND + QMAX, ALU.max, ALU.min).then_inc(ctx_rounded, 1)

            def round_q1(t):
                r = xn[:, t % 2, :]
                dve.wait_ge(normed, NT + t + 1)
                link(nc.vector.tensor_scalar(r, r, qp[:, 1:2], ROUND, ALU.add, ALU.add))
                nc.vector.tensor_scalar(r, r, ROUND, ROUND + QMAX, ALU.max, ALU.min).then_inc(q1_rounded, 1)

            def copy_CB(b):
                for n in range(2):
                    dve.wait_ge(mm_done, nth("CB", b, n) + 1)
                    free(nc.vector.tensor_scalar(corr[:, b, n * BANK:(n + 1) * BANK], job_bank("CB", b, n)[:, :],
                                                 cs, None, ALU.mult))

            def row_bias(t):
                dve.wait_ge(rowsum_done, t + 1)
                nc.vector.tensor_scalar(rowbias[:, t:t + 1], rowsum[:, t:t + 1], rb_mul, rb_add, ALU.mult,
                                        ALU.add).then_inc(rowbias_ready, 1)

            def add_XA(t):
                dve.wait_ge(corr_added, t + 1)
                for n in range(2):
                    c = slice(n * BANK, (n + 1) * BANK)
                    dve.wait_ge(xa_scaled, 2 * t + n + 1)
                    free(nc.vector.tensor_tensor(x[:, t, c], job_bank("XA", t, n)[:, :], x[:, t, c], ALU.add))

            def stack_u(b):
                pu = job_bank("U", b)[0:4 * RANK, :]
                dve.wait_ge(mm_done, nth("U", b) + 1)
                link(nc.vector.tensor_copy(u_hi[:, :].bitcast(F32R), pu))
                link(nc.vector.tensor_tensor(u_lo[:, :], pu, u_hi[:, :], ALU.subtract))
                link(nc.vector.tensor_scalar(u_hi[:, :], u_hi[:, :], mslot[:, 0:1], None, ALU.mult))
                free(nc.vector.scalar_tensor_tensor(u_stack[:, b * SB:(b + 1) * SB], u_lo[:, :], mslot[:, 1:2],
                                                    u_hi[:, :], ALU.mult, ALU.add))

            def cut_c2(g, off=0):
                dve.wait_ge(c2_loaded, g * 64 + 64)
                half = slice(2 * RANK, 4 * RANK)
                link(nc.vector.tensor_copy(c2_stack[:, :], c2_raw[:, :]), off)
                nc.vector.tensor_tensor(c2_stack[half, :], c2_raw[half, :], c2_stack[half, :].bitcast(F32),
                                        ALU.subtract).then_inc(c2_done, 1)

            def pick_first(g, t, off=0):
                sc = score_bank[:, :].rearrange("p (b w) -> p b w", w=BLK)
                cd = cand[:, :].rearrange("p (b w) -> p b w", w=BLK)
                pk = pick[:, :].rearrange("p (b w) -> p b w", w=BLK)
                wide = [P, GH // BLK, BLK]
                dve.wait_ge(score_done, g * NT + (t + 1))
                link(nc.vector.tensor_reduce(bmax[:, :], sc, AX.X, ALU.max), off)
                ins = nc.vector.tensor_tensor(
                    cd, sc, bmax[:, :].rearrange("p (b o) -> p b o", o=1).to_broadcast(wide), ALU.is_equal)
                ins.then_inc(score_read, 1)
                dve.wait_ge(score_read, g * NT + (t + 1))
                link(nc.vector.tensor_tensor(cand[:, :], cand[:, :], order[:, :], ALU.mult), off)
                link(nc.vector.tensor_reduce(cmax[:, :], cd, AX.X, ALU.max), off)
                if isinstance(g, int) and g == 0:
                    if t > 0:
                        dve.wait_ge(maskT_done, t)
                else:
                    dve.wait_ge(maskT_done, g * NT + t)
                nc.vector.tensor_tensor(pk, cd, cmax[:, :].rearrange("p (b o) -> p b o", o=1).to_broadcast(wide),
                                        ALU.is_equal).then_inc(pick_ready, 1)

            def relu_mask(g, j, half):
                pb = bank[2 * (j % 2) + half]
                dve.wait_ge(mm_done, hidden_nth(g, j, half) + 1)
                dve.wait_ge(maskT_copied, g * NT + TB * (half + 1))
                nc.vector.scalar_tensor_tensor(pb[:, :], pb[:, :], 0.0, maskT[:, j, half * SB:(half + 1) * SB],
                                               ALU.max, ALU.mult).then_inc(relu_masked, 1)

            def lo_h(g, j, half):
                dve.wait_ge(h_hi_done, g * 2 * GJ + (hidden_pos(g, j, half) + 1))
                s = slice(half * SB, (half + 1) * SB)
                free(nc.vector.tensor_tensor(h_lo[:, j, s], bank[2 * (j % 2) + half][:, :],
                                             h_hi[:, j, s].bitcast(F32), ALU.subtract))

            def add_unit(g, u):
                t, n = divmod(u, 2)
                c = slice(n * BANK, (n + 1) * BANK)
                dve.wait_ge(mm_done, unit_nth(g, u) + 1)
                free(nc.vector.tensor_tensor(x[:, t, c], bank[UNIT_BANK[u]][:, :], x[:, t, c], ALU.add))

            nc.vector.memset(ones_b[:, :], 1.0)

            def first_stats(*tiles):
                for t in tiles:
                    dve.wait_ge(x_loaded[t], 16)
                    stats_of(t)

            first_stats(0, 1)
            add_eps(0, 0)
            norm_scale(0, 0)
            first_stats(2, 3)
            add_eps(0, 2)
            lo_T(0, 0)
            norm_scale(0, 2)
            lo_T(0, 1)
            dve.wait_ge(bias_loaded, 48)
            lo_V(0, 0)
            lo_T(0, 2)
            lo_T(0, 3)
            first_stats(4, 5, 6, 7)
            add_eps(0, 4)
            lo_V(0, 1)
            norm_scale(0, 4)
            lo_Q(0, 0)
            lo_Q(0, 1)
            lo_T(0, 4)
            lo_Q(0, 2)
            lo_T(0, 5)
            lo_Q(0, 3)
            lo_T(0, 6)
            lo_T(0, 7)
            dve.wait_ge(qp_loaded, 64)
            nc.vector.reciprocal(inv1, qp[:, 0:1])
            nc.vector.reciprocal(inv2, qp[:, 2:3])
            nc.vector.tensor_tensor(s12, qp[:, 0:1], qp[:, 2:3], ALU.mult)
            nc.vector.tensor_scalar(d1, qp[:, 1:2], -1.0, CENTRE, ALU.mult, ALU.add)
            link(nc.vector.tensor_scalar(d2, qp[:, 3:4], -1.0, CENTRE, ALU.mult, ALU.add))
            nc.vector.tensor_tensor(cs, s12, d1, ALU.mult)
            link(nc.vector.tensor_tensor(rb_mul, s12, d2, ALU.mult))
            nc.vector.scalar_tensor_tensor(rb_add, rb_mul, float(D), d1, ALU.mult, ALU.mult).then_inc(qp_ready, 1)
            maxima(0)
            inverse_sums(0)
            dve.wait_ge(ident_ready, 1)
            nc.vector.tensor_copy(id_b[:, :], id_f[:, :]).then_inc(id_b_ready, 1)
            slots = id_f[0:4 * RANK, 0:4 * RANK].rearrange("p (a s c) -> p s a c", a=2, s=2)
            for s in range(2):
                link(nc.vector.tensor_reduce(mslot[:, s:s + 1], slots[:, s], AX.XY, ALU.add))
            for i in range(4):
                round_ctx(i)
            for c in range(4):
                lo_Q(1, c)
                round_ctx(2 * c + 4)
                round_ctx(2 * c + 5)
            lo_V(1, 0)
            round_ctx(12)
            round_ctx(13)
            lo_V(1, 1)
            for i in range(TB):
                lo_PT(0, i)
            maxima(1)
            dve.wait_ge(Wo_hi_done, 1)
            nc.vector.tensor_tensor(Wo_lo[:, :, :], Wo_raw[:, :, :], Wo_hi[:, :, :].bitcast(F32),
                                    ALU.subtract).then_inc(Wo_lo_done, 1)
            inverse_sums(1)
            lo_O(0, 0)
            lo_O(0, 1)
            for i in range(TB):
                lo_PT(1, i)
            round_ctx(14)
            round_ctx(15)
            for t in range(TB):
                add_WO(t)
                stats_of(t, "WO", t, 1)
            add_eps(1, 0)
            norm_scale(1, 0)
            lo_O(1, 0)
            lo_O(1, 1)
            copy_CB(0)
            round_q1(0)
            round_q1(1)
            round_q1(2)
            round_q1(3)
            for t in range(TB, NT):
                add_WO(t)
                stats_of(t, "WO", t, 1)
            add_eps(1, 4)
            copy_CB(1)
            norm_scale(1, 4)
            round_q1(4)
            row_bias(0)
            round_q1(5)
            add_XA(0)
            stats_of(0, "XA", 0, 1)
            row_bias(1)
            round_q1(6)
            add_XA(1)
            stats_of(1, "XA", 1, 1)
            round_q1(7)
            row_bias(2)
            add_XA(2)
            stats_of(2, "XA", 2, 1)
            dve.wait_ge(c1_loaded, 16)
            wide = c1_raw[:, :, :].rearrange("p k (o r) -> p k o r", o=1).to_broadcast([P, KD, 4, RANK])
            link(nc.vector.tensor_copy(c1_hi[:, :, :, :], wide))
            nc.vector.tensor_tensor(c1_lo[:, :, :, :], wide, c1_hi[:, :, :, :].bitcast(F32),
                                    ALU.subtract).then_inc(c1_done, 1)
            row_bias(3)
            add_XA(3)
            stats_of(3, "XA", 3, 1)
            add_eps(2, 0)
            row_bias(4)
            norm_scale(2, 0)
            add_XA(4)
            stats_of(4, "XA", 4, 1)
            row_bias(5)
            add_XA(5)
            stats_of(5, "XA", 5, 1)
            add_eps(2, 4)
            lo_T(2, 0)
            lo_T(2, 1)
            norm_scale(2, 4)
            row_bias(6)
            add_XA(6)
            stats_of(6, "XA", 6, 1)
            lo_T(2, 2)
            row_bias(7)
            lo_T(2, 3)
            add_XA(7)
            stats_of(7, "XA", 7, 1)
            add_eps(2, 6)
            norm_scale(2, 6)
            lo_T(2, 4)
            cut_c2(0)
            stack_u(0)
            lo_T(2, 5)
            lo_T(2, 6)
            lo_T(2, 7)
            dve.wait_ge(order_ready, 1)
            pick_first(0, 0)
            pick_first(0, 1)
            pick_first(0, 2)
            stack_u(1)
            pick_first(0, 3)
            pick_first(0, 4)
            relu_mask(0, 0, 0)
            relu_mask(0, 1, 0)
            lo_h(0, 0, 0)
            lo_h(0, 1, 0)
            for t in range(TB + 1, NT):
                pick_first(0, t)
            relu_mask(0, 0, 1)
            relu_mask(0, 1, 1)
            lo_h(0, 0, 1)
            lo_h(0, 1, 1)
            for j in range(2, GJ):
                for half in range(2):
                    relu_mask(0, j, half)
                for half in range(2):
                    lo_h(0, j, half)

            before = chained[0]
            links = 1 + 3 * NT
            with dve.Fori(0, NG - 1) as g:
                off = g * links
                dve.wait_ge(score_done, g * NT + NT)
                cut_c2(g + 1, off)
                pick_first(g + 1, 0, off)
                for u in range(4):
                    add_unit(g, u)
                for t in range(1, NT - 1):
                    pick_first(g + 1, t, off)
                    add_unit(g, 2 * t + 2)
                    add_unit(g, 2 * t + 3)
                pick_first(g + 1, NT - 1, off)
                for j in range(GJ):
                    for half in range(2):
                        relu_mask(g + 1, j, half)
                    for half in range(2):
                        lo_h(g + 1, j, half)
            assert chained[0] - before == links
            for u in range(2 * NT):
                add_unit(NG - 1, u)

        @block.tensor
        def _(pe):
            def take_bank(*job):
                n = nth(*job)
                if n >= RING:
                    pe.wait_ge(bank_free, n - RING + 1)

            def made(*job):
                pe.wait_ge(bank_free, nth(*job) + 1)

            def split_mm(dst, pairs, between=lambda n: None):
                for n, ((ah, al), (bh, bl)) in enumerate(pairs):
                    between(n)
                    nc.tensor.matmul(dst, ah, bh, start=n == 0, stop=False)
                    nc.tensor.matmul(dst, ah, bl, start=False, stop=False)
                    last = nc.tensor.matmul(dst, al, bh, start=False, stop=n == len(pairs) - 1)
                return last

            def transpose_norm(rnd, t):
                pe.wait_ge(normed, rnd * NT + t + 1)
                for h in range(2):
                    job = ("T1" if rnd == 0 else "T3", t, h)
                    take_bank(*job)
                    for k in range(4):
                        src = (xn3 if rnd == 2 else xn)[:, t % 2, (4 * h + k) * P:(4 * h + k + 1) * P]
                        last = nc.tensor.transpose(job_bank(*job)[:, k * P:(k + 1) * P], src, id_f[:, :])
                    last.then_inc(mm_done, 1)

            def project_qk(b, c):
                take_bank("Q", b, c)
                if b == 0:
                    pe.wait_ge(W_lo_done, 2 * W_ORDER.index(c // DC) + 2)
                m = slice((c % DC) * P, (c % DC + 1) * P)
                split_mm(job_bank("Q", b, c)[:, :],
                         [((W_hi[:, c // DC, k, m], W_lo[:, c // DC, k, m]), (xT_hi[b][:, k, :], xT_lo[b][:, k, :]))
                          for k in range(KD)]).then_inc(mm_done, 1)

            def project_v(b, i):
                take_bank("V", b, i)
                def second_half(n):
                    if n == KD // 2:
                        pe.wait_ge(W_lo_done, 2)

                for s in range(2):
                    if b == 0:
                        pe.wait_ge(W_lo_done, 1)
                        made("T1", 2 * i + s, 1)
                    m = slice((2 * i + s) * P, (2 * i + s + 1) * P)
                    last = split_mm(job_bank("V", b, i)[:, s * HD:(s + 1) * HD],
                                    [((xT_hi[b][:, k, m], xT_lo[b][:, k, m]), (W_hi[:, 2, k, :], W_lo[:, 2, k, :]))
                                     for k in range(KD)], second_half)
                last.then_inc(mm_done, 1)

            def scores(b, i):
                take_bank("S", b, i)
                if i == 0:
                    made("Q", b, 3)
                m = slice(i * P, (i + 1) * P)
                split_mm(job_bank("S", b, i)[:, :],
                         [((q_hi[b][:, c, m], q_lo[b][:, c, m]), (k_hi[b][:, c, :], k_lo[b][:, c, :]))
                          for c in range(DC)]).then_inc(mm_done, 1)

            def transpose_probs(b, i):
                take_bank("PT", b, i)
                pe.wait_ge(exp_done, b * TB + i + 1)
                for k in range(TB):
                    last = nc.tensor.transpose(job_bank("PT", b, i)[:, k * P:(k + 1) * P],
                                               probs[:, i, k * P:(k + 1) * P], id_f[:, :])
                last.then_inc(mm_done, 1)

            def mix_values(b, c):
                take_bank("O", b, c)
                if c == 0:
                    made("PT", b, TB - 1)
                m = slice(c * P, (c + 1) * P)
                split_mm(job_bank("O", b, c)[:, :],
                         [((v_hi[b][:, k, m], v_lo[b][:, k, m]), (pT_hi[:, k, :], pT_lo[:, k, :]))
                          for k in range(TB)]).then_inc(mm_done, 1)

            def project_out(t):
                if t == 0:
                    pe.wait_ge(Wo_lo_done, 1)
                if t % TB == 0:
                    made("O", t // TB, 1)
                m = slice((t % TB) * P, (t % TB + 1) * P)
                for n in range(2):
                    take_bank("WO", t, n)
                    c = slice(n * BANK, (n + 1) * BANK)
                    split_mm(job_bank("WO", t, n)[:, :],
                             [((oT_hi[:, d, m], oT_lo[:, d, m]), (Wo_hi[:, d, c], Wo_lo[:, d, c]))
                              for d in range(DC)]).then_inc(mm_done, 1)

            def column_sums(b):
                pe.wait_ge(q2_done, KD * (b + 1))
                for n in range(2):
                    take_bank("CB", b, n)
                    for k in range(KD):
                        last = nc.tensor.matmul(job_bank("CB", b, n)[:, :], ones_b[:, :],
                                                q2[b][:, k, n * BANK:(n + 1) * BANK], start=k == 0, stop=k == KD - 1)
                    last.then_inc(mm_done, 1)

            def transpose_q1(t):
                pe.wait_ge(q1_done, t + 1)
                if t > 0:
                    pe.wait_ge(q1T_copied, t)
                for k in range(KD):
                    last = nc.tensor.transpose(q1T_bank[:, k * P:(k + 1) * P], q1[:, t % 4, k * P:(k + 1) * P],
                                               id_b[:, :])
                last.then_inc(q1T_done, 1)

            def quantised_product(t):
                pe.wait_ge(q1T_copied, t + 1)
                for n in range(2):
                    if n == 1:
                        if t > 0:
                            pe.wait_ge(rowbias_ready, t)
                        for k in range(KD):
                            last = nc.tensor.matmul(rowsum[:, t:t + 1], q1T[:, t % 2, k, :], ones_b[:, 0:1],
                                                    start=k == 0, stop=k == KD - 1)
                        last.then_inc(rowsum_done, 1)
                    take_bank("XA", t, n)
                    for k in range(KD):
                        last = nc.tensor.matmul(job_bank("XA", t, n)[:, :], q1T[:, t % 2, k, :],
                                                q2[t // TB][:, k, n * BANK:(n + 1) * BANK],
                                                start=k == 0, stop=k == KD - 1)
                    last.then_inc(mm_done, 1)

            def rank_projection(b, between=lambda n: None):
                take_bank("U", b)
                made("T3", TB * b + 3, 1)
                if b == 0:
                    pe.wait_ge(c1_done, 1)
                split_mm(job_bank("U", b)[0:4 * RANK, :],
                         [((c1_hi[:, k].rearrange("p s r -> p (s r)"), c1_lo[:, k].rearrange("p s r -> p (s r)")),
                           (xT_hi[b][:, k, :], xT_lo[b][:, k, :])) for k in range(KD)], between).then_inc(mm_done, 1)

            def score_tile(g, t):
                if t == 0:
                    pe.wait_ge(c2_done, g + 1)
                if isinstance(g, int) and g == 0:
                    if t == 0:
                        made("U", 0)
                    else:
                        pe.wait_ge(score_read, t)
                    if t == TB:
                        made("U", 1)
                else:
                    pe.wait_ge(score_read, g * NT + t)
                nc.tensor.matmul(score_bank[:, :], u_stack[:, t * P:(t + 1) * P], c2_stack[:, :],
                                 start=True, stop=True).then_inc(score_done, 1)

            def transpose_pick(g, t):
                pe.wait_ge(pick_ready, g * NT + (t + 1))
                if isinstance(g, int) and g == 0:
                    if t > 0:
                        pe.wait_ge(maskT_copied, t)
                else:
                    pe.wait_ge(maskT_copied, g * NT + t)
                for j in range(GJ):
                    last = nc.tensor.transpose(maskT_bank[:, j * P:(j + 1) * P], pick[:, j * P:(j + 1) * P], id_b[:, :])
                last.then_inc(maskT_done, 1)

            def hidden(g, j, half, between=lambda n: None):
                b = 2 * (j % 2) + half
                pe.wait_ge(w_lo_done, g * NW + (WSEQ.index(("w1", j)) + 1))
                if j >= 2:
                    pe.wait_ge(bank_free, hidden_nth(g, j - 2, half) + 1)
                elif isinstance(g, int) and g == 0:
                    pe.wait_ge(bank_free, 1 + max(n for n in range(NJ) if n % RING == b))
                else:
                    pe.wait_ge(bank_free, unit_nth(g, prev_unit_on(b)) + (1 - PER))
                pairs = [((w1_hi[:, j % 2, k, :], w1_lo[:, j % 2, k, :]), (xT_hi[half][:, k, :], xT_lo[half][:, k, :]))
                         for k in range(KD)]
                split_mm(bank[b][:, :], pairs, between).then_inc(mm_done, 1)

            def unit_part(u, js):
                t, n = divmod(u, 2)
                m, c = slice(t * P, (t + 1) * P), slice(n * BANK, (n + 1) * BANK)
                dst = bank[UNIT_BANK[u]][:, :]
                for j in js:
                    nc.tensor.matmul(dst, h_hi[:, j, m], w2_hi[:, j, c], start=j == 0, stop=False)
                    nc.tensor.matmul(dst, h_hi[:, j, m], w2_lo[:, j, c], start=False, stop=False)
                    last = nc.tensor.matmul(dst, h_lo[:, j, m], w2_hi[:, j, c], start=False, stop=j == GJ - 1)
                return last

            def take_unit_bank(g, u):
                if u >= 6:
                    pe.wait_ge(bank_free, unit_nth(g, u - 6) + 1)
                elif UNIT_BANK[u] < 4:
                    b = UNIT_BANK[u]
                    pe.wait_ge(bank_free, hidden_nth(g, GJ - 2 + b // 2, b % 2) + 1)

            def outputs(g, last_group):
                pe.wait_ge(w_lo_done, g * NW + (WSEQ.index(("w2", 2)) + 1))
                for u in range(4):
                    take_unit_bank(g, u)
                    for j in range(GJ - 1):
                        if u == 0:
                            pe.wait_ge(bank_free, hidden_nth(g, max(j, 1), 1) + 1)
                        unit_part(u, [j])
                    if u == 1 and not last_group:
                        score_tile(g + 1, 0)
                pe.wait_ge(w_lo_done, g * NW + NW)
                pe.wait_ge(bank_free, hidden_nth(g, GJ - 1, 1) + 1)
                for u in range(4):
                    unit_part(u, [GJ - 1]).then_inc(mm_done, 1)
                for u in range(4, 2 * NT):
                    if u % 2 == 0 and not last_group:
                        score_tile(g + 1, u // 2 - 1)
                        transpose_pick(g + 1, u // 2 - 2)
                    take_unit_bank(g, u)
                    unit_part(u, range(GJ)).then_inc(mm_done, 1)
                if not last_group:
                    score_tile(g + 1, NT - 1)
                    transpose_pick(g + 1, NT - 2)

            pe.wait_ge(ident_ready, 1)
            transpose_norm(0, 0)
            transpose_norm(0, 1)
            project_v(0, 0)
            transpose_norm(0, 2)
            transpose_norm(0, 3)
            project_v(0, 1)
            project_qk(0, 0)
            project_qk(0, 1)
            transpose_norm(0, 4)
            project_qk(0, 2)
            transpose_norm(0, 5)
            project_qk(0, 3)
            transpose_norm(0, 6)
            transpose_norm(0, 7)
            for i in range(TB):
                scores(0, i)
            made("T1", NT - 1, 1)
            for c in range(4):
                project_qk(1, c)
            project_v(1, 0)
            project_v(1, 1)
            for i in range(TB):
                transpose_probs(0, i)
            for i in range(TB):
                scores(1, i)
            mix_values(0, 0)
            mix_values(0, 1)
            for i in range(TB):
                transpose_probs(1, i)
            for t in range(TB):
                project_out(t)
            mix_values(1, 0)
            mix_values(1, 1)
            column_sums(0)
            for t in range(TB, NT):
                project_out(t)
            pe.wait_ge(id_b_ready, 1)
            transpose_q1(0)
            column_sums(1)
            transpose_q1(1)
            for t in range(5):
                quantised_product(t)
                transpose_q1(t + 2)
            quantised_product(5)
            transpose_norm(2, 0)
            transpose_norm(2, 1)
            transpose_q1(7)
            quantised_product(6)
            transpose_norm(2, 2)
            transpose_norm(2, 3)
            quantised_product(7)
            transpose_norm(2, 4)
            rank_projection(0)
            transpose_norm(2, 5)
            transpose_norm(2, 6)
            transpose_norm(2, 7)
            score_tile(0, 0)

            def masks_in(steps):
                def between(n):
                    if n in steps:
                        picked, scored = steps[n]
                        if picked is not None:
                            transpose_pick(0, picked)
                        if scored is not None:
                            score_tile(0, scored)
                return between

            rank_projection(1, masks_in({3: (None, 1), 7: (0, 2)}))
            hidden(0, 0, 0, masks_in({4: (1, 3)}))
            hidden(0, 1, 0, masks_in({4: (2, 4)}))
            hidden(0, 0, 1, masks_in({1: (3, 5)}))
            hidden(0, 1, 1, masks_in({2: (4, 6), 7: (5, 7)}))
            hidden(0, 2, 0, masks_in({3: (6, None), 7: (7, None)}))
            hidden(0, 2, 1)
            hidden(0, 3, 0)
            hidden(0, 3, 1)
            with pe.Fori(0, NG - 1) as g:
                outputs(g, False)
                for j in range(GJ):
                    for half in range(2):
                        hidden(g + 1, j, half)
                        if (j, half) == (0, 0):
                            transpose_pick(g + 1, NT - 1)
            outputs(NG - 1, True)


def kernel(x, ctx_4096, L0_attn_Wqkv, L0_attn_bqkv, L0_attn_Wo, L0_attn_bo, L0_xattn_x1_scale, L0_xattn_x1_zp,
           L0_xattn_x2_scale, L0_xattn_x2_zp, L0_ffn_c1_w, L0_ffn_c2_w, L0_ffn_w1, L0_ffn_w2t):
    import numpy as np
    import concourse.bacc as bacc
    from concourse.bass_utils import run_bass_kernel_spmd

    x, ctx = np.asarray(x), np.asarray(ctx_4096)
    wqkv, bqkv = np.asarray(L0_attn_Wqkv), np.asarray(L0_attn_bqkv)
    B, S, D = x.shape
    HD = D // 4
    nt, kd, ni = B * S // P, D // P, L0_ffn_w1.shape[0] // P
    c1, c2, w1, w2 = (np.asarray(a) for a in (L0_ffn_c1_w, L0_ffn_c2_w, L0_ffn_w1, L0_ffn_w2t))
    rank = c1.shape[0]
    laid = {
        "x_in": x.reshape(nt, P, D),
        "ctx_in": ctx.reshape(B * kd, P, D),
        "wqkv": wqkv.reshape(kd, P, 3, HD).transpose(2, 1, 0, 3),
        "bqk": bqkv[:2 * HD].reshape(2 * HD // P, P).T,
        "bv": bqkv[2 * HD:],
        "wo": np.asarray(L0_attn_Wo).reshape(HD // P, P, D).transpose(1, 0, 2),
        "bo": np.asarray(L0_attn_bo),
        "s1": np.asarray(L0_xattn_x1_scale), "z1": np.asarray(L0_xattn_x1_zp),
        "s2": np.asarray(L0_xattn_x2_scale), "z2": np.asarray(L0_xattn_x2_zp),
        "c1": c1.T.reshape(kd, P, rank).transpose(1, 0, 2),
        "c2": c2.reshape(-1, BANK, rank).transpose(0, 2, 1),
        "w1": w1.reshape(ni, P, kd, P).transpose(0, 3, 2, 1).reshape(ni, P, D),
        "w2": w2.reshape(ni, P, D),
    }
    arrays = {n: np.ascontiguousarray(a) for n, a in laid.items()}
    nc = bacc.Bacc("TRN2", target_bir_lowering=False, num_devices=1)
    args = [nc.dram_tensor(n, a.shape, mybir.dt.from_np(a.dtype), kind="ExternalInput").ap() for n, a in arrays.items()]
    out = nc.dram_tensor("out", (nt, P, D), F32, kind="ExternalOutput").ap()
    decoder_layer(nc, *args, out)
    r = run_bass_kernel_spmd(nc, [arrays], core_ids=[0])
    return r.results[0]["out"].reshape(B, S, D)
```

```python
from contextlib import ExitStack

import concourse.bass as bass
from concourse import mybir

P = 128
F32 = mybir.dt.float32
F32R = mybir.dt.float32r
BF16 = mybir.dt.bfloat16
ALU = mybir.AluOpType
ACT = mybir.ActivationFunctionType
AX = mybir.AxisListType

KB = 1024
BANK = 512
U1_BANK = 5
RING = 6
EPS = 1e-5
ROUND = 12582912.0
QMAX = 255.0
CENTRE = 128.0


def job_order():
    both = lambda kind, a: [(kind, a, 0), (kind, a, 1)]
    jobs = both("T1", 0) + both("T1", 1) + both("T1", 2) + [("V", 0, 0)] + both("T1", 3) + [("V", 0, 1)]
    jobs += [("Q", 0, 0), ("Q", 0, 1)] + both("T1", 4) + [("Q", 0, 2)] + both("T1", 5)
    jobs += [("Q", 0, 3)] + both("T1", 6) + both("T1", 7)
    jobs += [("S", 0, i) for i in range(4)]
    jobs += [("Q", 1, c) for c in range(4)] + both("V", 1)
    jobs += [("PT", 0, i) for i in range(4)] + [("S", 1, i) for i in range(4)] + both("O", 0)
    jobs += [("PT", 1, i) for i in range(4)]
    for t in range(4):
        jobs += both("WO", t)
    jobs += both("O", 1) + both("CB", 0)
    for t in range(4, 8):
        jobs += both("WO", t)
    jobs += both("CB", 1)
    for t in range(7):
        jobs += both("XA", t)
    jobs += both("T3", 0) + both("T3", 1) + both("XA", 7)
    for t in range(2, 6):
        jobs += both("T3", t)
    jobs += [("U", 0)] + both("T3", 6) + both("T3", 7)
    return jobs


JOBS = job_order()
NJ = len(JOBS)
HIDDEN_0 = [(0, 0), (1, 0), (0, 1), (1, 1), (2, 0), (3, 0), (2, 1), (3, 1)]
HIDDEN = [(0, 0), (0, 1), (1, 0), (1, 1), (2, 0), (3, 0), (2, 1), (3, 1)]
CHAINS = [(0, 0, 2), (0, 2, 2), (0, 4, 4), (1, 0, 4), (1, 4, 2), (1, 6, 2), (2, 0, 4), (2, 4, 2), (2, 6, 2)]
W_ORDER = (2, 0, 1)
HI_KINDS = ("T1", "Q", "V", "PT", "O", "T3")


def nth(*job):
    return JOBS.index(job)


def last_in(b):
    return max(n for n in range(NJ) if n % RING == b)


def nth_hi(*job):
    return sum(j[0] in HI_KINDS for j in JOBS[:nth(*job)])


def nth_chain(rnd, t):
    return next(n for n, (r, first, count) in enumerate(CHAINS) if r == rnd and first <= t < first + count)


def decoder_layer(nc, x_in, ctx_in, wqkv, bqk, bv, wo, bo, s1, z1, s2, z2, c1, c2, w1, w2, out):
    D = x_in.shape[2]
    NT = x_in.shape[0]
    NB = 2
    TB = NT // NB
    KD = D // P
    HD = wqkv.shape[3]
    DC = HD // P
    RANK = c1.shape[2]
    SLOTS = P // RANK
    BLK = 64
    NG = c2.shape[0]
    GH = c2.shape[2]
    GJ = GH // P
    SB = TB * P
    SCALE = 1.0 / 16.0
    assert (D, NT, HD, GH, SB, HD ** 0.5) == (1024, 8, 256, BANK, BANK, 1 / SCALE)

    base = (nc.sbuf_base + 31) // 32 * 32

    def at(name, kb, shape, dt):
        t = nc.alloc_sbuf_tensor_at(name, shape, dt, offset=base + int(kb * KB))
        size = 2 if dt == BF16 else 4
        for d in shape[1:]:
            size *= d
        assert base + int(kb * KB) + size <= nc.sbuf_usable_end, name
        return t

    x = at("x", 0, [P, NT, D], F32)
    xT_hi = [at(f"xT_hi{b}", 32 + 32 * b, [P, KD, SB], F32R) for b in range(NB)]
    xT_lo = [at(f"xT_lo{b}", 48 + 32 * b, [P, KD, SB], F32R) for b in range(NB)]
    W_hi = at("W_hi", 96, [P, 3, KD, HD], F32R)
    W_lo = at("W_lo", 120, [P, 3, KD, HD], F32R)
    W_raw = at("W_raw", 168, [P, 3, KD, HD], F32)
    q_hi, q_lo, k_hi, k_lo, v_hi, v_lo = (
        [at(f"{n}{b}", 144 + 24 * b + 4 * i, [P, TB, HD] if n[0] == "v" else [P, DC, SB], F32R) for b in range(NB)]
        for i, n in enumerate(("q_hi", "q_lo", "k_hi", "k_lo", "v_hi", "v_lo")))
    xn = at("xn", 192, [P, 2, D], F32)
    ctx_raw = at("ctx_raw", 48, [P, 2, D], F32)
    ctx_slot = [ctx_raw[:, 0, :], ctx_raw[:, 1, :], xn[:, 0, :], xn[:, 1, :]]
    probs = at("probs", 56, [P, TB, SB], F32)
    q2 = [at("q2_0", 32, [P, KD, D], BF16), at("q2_1", 96, [P, KD, D], BF16)]
    pT_hi = at("pT_hi", 64, [P, TB, SB], F32R)
    pT_lo = at("pT_lo", 72, [P, TB, SB], F32R)
    oT_hi = at("oT_hi", 80, [P, DC, SB], F32R)
    oT_lo = at("oT_lo", 84, [P, DC, SB], F32R)
    Wo_raw = at("Wo_raw", 88, [P, DC, D], F32)
    Wo_hi = at("Wo_hi", 112, [P, DC, D], F32R)
    Wo_lo = at("Wo_lo", 120, [P, DC, D], F32R)
    pairs = at("pairs", 136, [P, KD // 2, D], BF16)
    q2_sum = at("q2_sum", 88, [P, NB, D], F32R)
    ones_r = at("ones_r", 204, [P, P], F32R)
    corr = at("corr", 128, [P, NB, D], F32)
    q1 = at("q1", 136, [P, 4, D], BF16)
    q1T = at("q1T", 160, [P, 2, KD, P], BF16)
    xn3 = [at(f"xn3_{i}", kb, [P, D], F32) for i, kb in enumerate((112, 116, 184, 188))]
    c1_raw = at("c1_raw", 120, [P, KD, RANK], F32)
    c1_cut = at("c1_cut", 121, [P, KD, SLOTS, RANK], F32R)
    u_hi = at("u_hi", 125, [P, SB], F32)
    u_lo = at("u_lo", 203, [P, SB], F32)
    h_hi = at("h_hi", 96, [P, GJ, NT * P], F32R)
    h_lo = at("h_lo", 112, [P, GJ, NT * P], F32R)
    w2_lo = at("w2_lo", 128, [P, GJ, D], F32R)
    w1_hi = at("w1_hi", 144, [P, 2, KD, P], F32R)
    w1_lo = at("w1_lo", 152, [P, 2, KD, P], F32R)
    w2_hi = at("w2_hi", 160, [P, GJ, D], F32R)
    w_raw = at("w_raw", 176, [P, 2, D], F32)
    maskT = at("maskT", 184, [P, GJ, NT * P], BF16)
    u_stack = at("u_stack", 192, [P, NT * P], F32R)
    c2_raw = at("c2_raw", 196, [P, GH], F32)
    c2_stack = at("c2_stack", 198, [P, GH], F32R)
    cand = at("cand", 200, [P, GH], BF16)
    pick = at("pick", 201, [P, GH], BF16)
    order = at("order", 202, [P, GH], BF16)
    bo_b = at("bo_b", 200, [P, D], F32)
    bv_b = at("bv_b", 204, [P, HD], F32)
    smalls = [205.0]

    def small(name, shape, dt):
        t = at(name, smalls[0], shape, dt)
        size = 2 if dt == BF16 else 4
        for d in shape[1:]:
            size *= d
        smalls[0] += (size + 31) // 32 * 32 / KB
        return t

    id_f = small("id_f", [P, P], F32)
    id_b = small("id_b", [P, P], BF16)
    bqk_s = small("bqk_s", [P, 2 * DC], F32)
    uncentre = small("uncentre", [P, 1], F32)
    stats = small("stats", [P, NT, 12], F32)
    mv = small("mv", [P, NT, 2], F32)
    eps = small("eps", [P, 1], F32)
    eps_root = small("eps_root", [P, 1], F32)
    sdev = small("sdev", [P, NT], F32)
    rinv = small("rinv", [P, NT], F32)
    newt = small("newt", [P, NT], F32)
    rstd = small("rstd", [P, NT], F32)
    nmr = small("nmr", [P, NT], F32)
    qp = small("qp", [P, 4], F32)
    qd = small("qd", [P, 8], F32)
    inv1, inv2, s12, d1, d2, cs, rb_mul, rb_add = (qd[:, i:i + 1] for i in range(8))
    smax = small("smax", [P, NT], F32)
    nbias = small("nbias", [P, NT], F32)
    qmul = small("qmul", [P, NT], F32)
    qadd = small("qadd", [P, NT], F32)
    psum_row = small("psum_row", [P, NT], F32)
    q1_sum = small("q1_sum", [P, NT], F32)
    pinv = small("pinv", [P, NT], F32)
    rowbias = small("rowbias", [P, NT], F32)
    mslot = small("mslot", [P, 2], F32)
    bmax = small("bmax", [P, GH // BLK], F32)
    cmax = small("cmax", [P, GH // BLK], BF16)

    with ExitStack() as ctx:
        bank = [ctx.enter_context(nc.psum_tensor(f"bank{i}", [P, BANK], F32)) for i in range(8)]
        score_bank = bank[6]
        u_bank = [bank[nth("U", 0) % RING], bank[U1_BANK]]
        q1T_bank = bank[7][:, :].bitcast(BF16)
        maskT_bank = bank[7][:, 0:BANK // 2].bitcast(BF16)

        def sem(name):
            return ctx.enter_context(nc.semaphore(name))

        x_loaded = [sem(f"x_loaded{t}") for t in range(NT)]
        W_loaded = [[sem(f"W_loaded{i}_{h}") for h in range(2)] for i in range(3)]
        bias_loaded = sem("bias_loaded")
        qp_loaded = sem("qp_loaded")
        ctx_loaded = [sem(f"ctx_loaded{i}") for i in range(4)]
        Wo_loaded = sem("Wo_loaded")
        c1_loaded = sem("c1_loaded")
        c2_loaded = sem("c2_loaded")
        w_loaded = [sem(f"w_loaded{i}") for i in range(2)]
        stored = sem("stored")
        ident_zeroed = sem("ident_zeroed")
        ident_ready = sem("ident_ready")
        id_b_ready = sem("id_b_ready")
        order_ready = sem("order_ready")
        qp_ready = sem("qp_ready")
        mm_done = sem("mm_done")
        hi_done = sem("hi_done")
        bank_free = sem("bank_free")
        vec = sem("vec")
        mv_done = sem("mv_done")
        eps_ready = sem("eps_ready")
        sdev_ready = sem("sdev_ready")
        rstd_ready = sem("rstd_ready")
        normed = sem("normed")
        vbias_added = sem("vbias_added")
        W_hi_done = sem("W_hi_done")
        W_lo_done = sem("W_lo_done")
        bo_added = sem("bo_added")
        nbias_ready = sem("nbias_ready")
        exp_done = sem("exp_done")
        Wo_hi_done = sem("Wo_hi_done")
        Wo_lo_done = sem("Wo_lo_done")
        ctx_scaled = sem("ctx_scaled")
        ctx_rounded = sem("ctx_rounded")
        q2_done = sem("q2_done")
        q1_rounded = sem("q1_rounded")
        q1_done = sem("q1_done")
        q1T_done = sem("q1T_done")
        q1T_copied = sem("q1T_copied")
        uncentre_ready = sem("uncentre_ready")
        ones_r_ready = sem("ones_r_ready")
        pairs_added = sem("pairs_added")
        summing = sem("summing")
        q2_summed = sem("q2_summed")
        rowbias_ready = sem("rowbias_ready")
        corr_added = sem("corr_added")
        c1_done = sem("c1_done")
        u1_done = sem("u1_done")
        u_stacked = sem("u_stacked")
        w_hi_done = sem("w_hi_done")
        w_lo_done = sem("w_lo_done")
        c2_done = sem("c2_done")
        score_done = sem("score_done")
        score_read = sem("score_read")
        pick_ready = sem("pick_ready")
        maskT_done = sem("maskT_done")
        maskT_copied = sem("maskT_copied")
        relu_masked = sem("relu_masked")
        h_hi_done = sem("h_hi_done")

        def job_bank(*job):
            return bank[nth(*job) % RING]

        PER = 2 * GJ + 2 * NT
        WSEQ = [("w1", 0), ("w1", 1), ("w2", 0), ("w2", 1), ("w1", 2), ("w2", 2), ("w1", 3), ("w2", 3)]
        NW = len(WSEQ)
        UNIT_BANK = [(0, 1, 4, 5, 2, 3)[u % 6] for u in range(2 * NT)]

        def hidden_nth(g, j, half):
            return g * PER + (NJ + hidden_pos(g, j, half))

        def unit_nth(g, u):
            return g * PER + (NJ + 2 * GJ + u)

        def hidden_pos(g, j, half):
            return (HIDDEN_0 if isinstance(g, int) and g == 0 else HIDDEN).index((j, half))

        def prev_unit_on(b):
            return max(u for u in range(2 * NT) if UNIT_BANK[u] == b)

        block = ctx.enter_context(nc.Block())

        @block.sync
        def _(sp):
            def load_x(*tiles):
                for t in tiles:
                    sp.dma_start(x[:, t, :], x_in[t]).then_inc(x_loaded[t], 16)

            def load_W(i):
                for h in range(2):
                    k = slice(h * KD // 2, (h + 1) * KD // 2)
                    sp.dma_start(W_raw[:, i, k, :], wqkv[i][:, k, :]).then_inc(W_loaded[i][h], 16)

            load_x(0, 1)
            load_W(W_ORDER[0])
            load_x(2, 3)
            for dst, src in ((bqk_s[:, :], bqk), (bv_b[:, :], bv.partition_broadcast(P)),
                             (bo_b[:, :], bo.partition_broadcast(P))):
                sp.dma_start(dst, src).then_inc(bias_loaded, 16)
            load_W(W_ORDER[1])
            load_x(4, 5)
            load_W(W_ORDER[2])
            load_x(6, 7)
            for i, src in enumerate((s1, z1, s2, z2)):
                sp.dma_start(qp[:, i:i + 1], src.partition_broadcast(P)).then_inc(qp_loaded, 16)
            sp.wait_ge(mm_done, nth("T1", 7, 1) + 1)
            for i in range(NB * KD):
                if i >= 4:
                    sp.wait_ge(q2_done, i - 3)
                sp.dma_start(ctx_slot[i % 4], ctx_in[i]).then_inc(ctx_loaded[i % 4], 16)

            def load_w(which, j, g, slot):
                src = w1 if which == "w1" else w2
                sp.dma_start(w_raw[:, slot, :], src[g * GJ + j]).then_inc(w_loaded[slot], 16)

            def load_c2(g):
                for i in range(SLOTS):
                    sp.dma_start(c2_raw[RANK * i:RANK * (i + 1), :], c2[g]).then_inc(c2_loaded, 16)

            sp.wait_ge(mm_done, nth("O", 1, 1) + 1)
            load_w(*WSEQ[0], 0, 0)
            load_w(*WSEQ[1], 0, 1)
            sp.wait_ge(mm_done, nth("WO", 7, 1) + 1)
            sp.dma_start(c1_raw[:, :, :], c1).then_inc(c1_loaded, 16)
            sp.wait_ge(q1_done, NT)
            load_c2(0)

            def group(g, last):
                if not last:
                    sp.wait_ge(c2_done, g + 1)
                    load_c2(g + 1)
                for i in range(NW - 2 if last else NW):
                    sp.wait_ge(w_lo_done, g * NW + (i + 1))
                    which, j = WSEQ[(i + 2) % NW]
                    load_w(which, j, g + 1 if i + 2 >= NW else g, i % 2)

            with sp.Fori(0, NG - 1) as g:
                group(g, False)
            group(NG - 1, True)
            for t in range(NT - 1):
                sp.wait_ge(bank_free, unit_nth(NG - 1, 2 * t + 1) + 1)
                sp.dma_start(out[t], x[:, t, :]).then_inc(stored, 16)
            for n in range(2):
                c = slice(n * BANK, (n + 1) * BANK)
                sp.wait_ge(bank_free, unit_nth(NG - 1, 2 * (NT - 1) + n) + 1)
                sp.dma_start(out[NT - 1][:, c], x[:, NT - 1, c]).then_inc(stored, 16)
            sp.wait_ge(stored, 16 * (NT + 1))

        @block.gpsimd
        def _(pool):
            nc.gpsimd.memset(id_f[:, :], 0.0).then_inc(ident_zeroed, 1)
            pool.wait_ge(ident_zeroed, 1)
            nc.gpsimd.affine_select(out=id_f[:, :], in_=id_f[:, :], compare_op=ALU.not_equal, fill=1.0,
                                    base=0, pattern=[[-1, P]], channel_multiplier=1).then_inc(ident_ready, 1)
            for n, i in enumerate(W_ORDER):
                for h in range(2):
                    pool.wait_ge(W_hi_done, 2 * n + h + 1)
                    k = slice(h * KD // 2, (h + 1) * KD // 2)
                    nc.gpsimd.tensor_tensor(W_lo[:, i, k, :], W_raw[:, i, k, :], W_hi[:, i, k, :].bitcast(F32),
                                            ALU.subtract).then_inc(W_lo_done, 1)
            pool.wait_ge(bias_loaded, 48)
            for t in range(NT):
                pool.wait_ge(normed, t + 1)
                nc.gpsimd.tensor_tensor(x[:, t, :], x[:, t, :], bo_b[:, :], ALU.add).then_inc(bo_added, 1)

            SUMS = (KD // 2 - 2) + (KD - 2)

            def sum_q2(b):
                s = q2_sum[:, b, :]
                if b == 0:
                    pool.wait_ge(pairs_added, 1)
                    tiles = [pairs[:, i, :] for i in range(KD // 2)]
                else:
                    pool.wait_ge(q2_done, 2 * KD)
                    tiles = [q2[b][:, i, :] for i in range(KD)]
                add = tiles[0]
                for i in range(1, len(tiles)):
                    if i == len(tiles) - 1:
                        nc.gpsimd.tensor_tensor(s, add, tiles[i], ALU.add).then_inc(q2_summed, 1)
                    else:
                        nc.gpsimd.tensor_tensor(s, add, tiles[i], ALU.add).then_inc(summing, 1)
                        pool.wait_ge(summing, i + (KD // 2 - 2 if b else 0))
                        add = s.bitcast(F32)

            for i in range(NB * KD):
                pool.wait_ge(ctx_rounded, i + 1)
                if i == KD:
                    pool.wait_ge(mm_done, nth("Q", 1, 3) + 1)
                nc.gpsimd.tensor_scalar(q2[i // KD][:, i % KD, :], ctx_slot[i % 4], -(ROUND + CENTRE), 1.0,
                                        ALU.add, ALU.mult).then_inc(q2_done, 1)
                if i == NB * KD - 3:
                    sum_q2(0)
            sum_q2(1)

            def add_corr(t):
                pool.wait_ge(normed, NT + t + 1)
                pool.wait_ge(bank_free, nth("CB", t // TB, 1) + 1)
                nc.gpsimd.tensor_tensor(x[:, t, :], x[:, t, :], corr[:, t // TB, :], ALU.add).then_inc(summing, 1)
                pool.wait_ge(summing, SUMS + t + 1)
                pool.wait_ge(rowbias_ready, t + 1)
                nc.gpsimd.tensor_scalar(x[:, t, :], x[:, t, :], rowbias[:, t:t + 1], 1.0, ALU.add,
                                        ALU.mult).then_inc(corr_added, 1)

            for t in range(NT):
                add_corr(t)
            nc.gpsimd.iota(order[:, :].rearrange("p (b w) -> p b w", w=BLK), pattern=[[0, GH // BLK], [-1, BLK]],
                           base=BLK, channel_multiplier=0,
                           allow_small_or_imprecise_dtypes=True).then_inc(order_ready, 1)

            def cut_w(g, i):
                which, j = WSEQ[i % NW]
                pool.wait_ge(w_hi_done, g * NW + (i + 1))
                hi, lo = (w1_hi[:, j % 2], w1_lo[:, j % 2]) if which == "w1" else (w2_hi[:, j], w2_lo[:, j])
                raw = w_raw[:, i % 2, :]
                if which == "w1":
                    raw = raw.rearrange("p (k m) -> p k m", k=KD)
                nc.gpsimd.tensor_tensor(lo, raw, hi.bitcast(F32), ALU.subtract).then_inc(w_lo_done, 1)

            cut_w(0, 0)
            cut_w(0, 1)
            for i in range(2, NW):
                cut_w(0, i)
            with pool.Fori(1, NG) as g:
                for i in range(NW):
                    cut_w(g, i)

        @block.scalar
        def _(act):
            def roots(rnd, t):
                n = nth_chain(rnd, t)
                s = slice(t, t + CHAINS[n][2])
                act.wait_ge(mv_done, rnd * NT + s.stop)
                nc.scalar.activation(sdev[:, s], mv[:, s, 1], ACT.Sqrt, bias=eps[:, 0:1],
                                     scale=1.0).then_inc(sdev_ready, 1)

            def norm(rnd, t):
                act.wait_ge(rstd_ready, nth_chain(rnd, t) + 1)
                if rnd == 0 and t >= 2:
                    act.wait_ge(mm_done, nth("T1", t - 2, 1) + 1)
                if rnd == 1 and t < 2:
                    act.wait_ge(q2_done, 2 * KD - 1 + t)
                if rnd == 1 and t >= 2:
                    act.wait_ge(q1_done, t - 1)
                if rnd == 2 and t >= 4:
                    act.wait_ge(mm_done, nth("T3", t - 4, 1) + 1)
                dst = xn3[t % 4][:, :] if rnd == 2 else xn[:, t % 2, :]
                mul, add = (qmul, qadd) if rnd == 1 else (rstd, nmr)
                func = ACT.Relu if rnd == 1 else ACT.Identity
                nc.scalar.activation(dst, x[:, t, :], func, bias=add[:, t:t + 1],
                                     scale=mul[:, t:t + 1]).then_inc(normed, 1)

            def hi_T(rnd, t, h):
                job = ("T1" if rnd == 0 else "T3", t, h)
                act.wait_ge(mm_done, nth(*job) + 1)
                nc.scalar.activation(
                    xT_hi[t // TB][:, 4 * h:4 * h + 4, (t % TB) * P:(t % TB + 1) * P],
                    job_bank(*job)[:, :].rearrange("p (k m) -> p k m", k=4), ACT.Copy).then_inc(hi_done, 1)

            def hi_W(i, h):
                act.wait_ge(W_loaded[i][h], 16)
                k = slice(h * KD // 2, (h + 1) * KD // 2)
                nc.scalar.activation(W_hi[:, i, k, :], W_raw[:, i, k, :], ACT.Copy).then_inc(W_hi_done, 1)

            def hi_Q(b, c):
                act.wait_ge(mm_done, nth("Q", b, c) + 1)
                if b == 0 and c == 0:
                    act.wait_ge(bias_loaded, 48)
                if b == 1 and c == 0:
                    act.wait_ge(W_lo_done, 6)
                dst = (q_hi if c < DC else k_hi)[b]
                nc.scalar.activation(dst[:, c % DC, :], job_bank("Q", b, c)[:, :], ACT.Identity,
                                     bias=bqk_s[:, c:c + 1], scale=1.0).then_inc(hi_done, 1)

            def hi_V(b, i):
                act.wait_ge(vbias_added, 2 * b + i + 1)
                nc.scalar.activation(v_hi[b][:, 2 * i:2 * i + 2, :],
                                     job_bank("V", b, i)[:, :].rearrange("p (t d) -> p t d", t=2),
                                     ACT.Copy).then_inc(hi_done, 1)

            def exp(b, i):
                n = b * TB + i
                act.wait_ge(nbias_ready, n + 1)
                if b == 0 and i == 0:
                    act.wait_ge(mm_done, nth("V", 0, 1) + 1)
                if b == 1:
                    act.wait_ge(mm_done, nth("PT", 0, i) + 1)
                nc.scalar.activation(probs[:, i, :], job_bank("S", b, i)[:, :], ACT.Exp, bias=nbias[:, n:n + 1],
                                     scale=SCALE, accum_out=psum_row[:, n:n + 1]).then_inc(exp_done, 1)

            def hi_PT(b, i):
                act.wait_ge(mm_done, nth("PT", b, i) + 1)
                nc.scalar.activation(pT_hi[:, :, i * P:(i + 1) * P],
                                     job_bank("PT", b, i)[:, :].rearrange("p (k m) -> p k m", k=TB),
                                     ACT.Copy).then_inc(hi_done, 1)

            def hi_O(b, c):
                act.wait_ge(mm_done, nth("O", b, c) + 1)
                nc.scalar.activation(oT_hi[:, c, :], job_bank("O", b, c)[:, :], ACT.Copy).then_inc(hi_done, 1)

            def scale_ctx(i):
                act.wait_ge(ctx_loaded[i % 4], 16 * (i // 4 + 1))
                nc.scalar.activation(ctx_slot[i % 4], ctx_slot[i % 4], ACT.Relu, bias=qp[:, 3:4],
                                     scale=inv2).then_inc(ctx_scaled, 1)

            def copy_q1T(t):
                act.wait_ge(q1T_done, t + 1)
                if t >= 2:
                    act.wait_ge(mm_done, nth("XA", t - 2, 1) + 1)
                nc.scalar.activation(q1T[:, t % 2, :, :], q1T_bank.rearrange("p (k m) -> p k m", k=KD),
                                     ACT.Copy).then_inc(q1T_copied, 1)

            def centre_q1(t):
                act.wait_ge(q1_rounded, t + 1)
                if t == 0:
                    act.wait_ge(uncentre_ready, 1)
                    act.wait_ge(q2_summed, 1)
                if t >= 4:
                    act.wait_ge(q1T_done, t - 3)
                nc.scalar.activation(q1[:, t % 4, :], xn[:, t % 2, :], ACT.Identity, bias=uncentre[:, 0:1], scale=1.0,
                                     accum_out=q1_sum[:, t:t + 1]).then_inc(q1_done, 1)

            def hi_w(g, i):
                which, j = WSEQ[i % NW]
                act.wait_ge(w_loaded[i % 2], g * (16 * NW // 2) + 16 * (i // 2 + 1))
                if which == "w1":
                    gg, jj = (g + i // NW, j - 2) if j >= 2 else (g + i // NW - 1, j + 2)
                    if isinstance(gg, int) and gg < 0:
                        act.wait_ge(mm_done, nth("O", 0, 1) + 1)
                    else:
                        act.wait_ge(mm_done, hidden_nth(gg, jj, 1) + 1)
                    dst = w1_hi[:, j % 2]
                else:
                    act.wait_ge(mm_done, hidden_nth(g, 0, 0))
                    dst = w2_hi[:, j]
                raw = w_raw[:, i % 2, :]
                if which == "w1":
                    raw = raw.rearrange("p (k m) -> p k m", k=KD)
                nc.scalar.activation(dst, raw, ACT.Copy).then_inc(w_hi_done, 1)

            def copy_maskT(g, t):
                act.wait_ge(maskT_done, g * NT + (t + 1))
                if not (isinstance(g, int) and g == 0):
                    act.wait_ge(relu_masked, g * 2 * GJ)
                nc.scalar.activation(maskT[:, :, t * P:(t + 1) * P],
                                     maskT_bank.rearrange("p (j m) -> p j m", j=GJ),
                                     ACT.Copy).then_inc(maskT_copied, 1)

            def hi_h(g, j, half):
                act.wait_ge(relu_masked, g * 2 * GJ + (hidden_pos(g, j, half) + 1))
                nc.scalar.activation(h_hi[:, j, half * SB:(half + 1) * SB], bank[2 * (j % 2) + half][:, :],
                                     ACT.Copy).then_inc(h_hi_done, 1)

            def both(f, *a):
                f(*a, 0)
                f(*a, 1)

            act.wait_ge(eps_ready, 1)
            nc.scalar.activation(eps_root[:, :], eps[:, 0:1], ACT.Sqrt)

            roots(0, 0)
            hi_W(W_ORDER[0], 0)
            norm(0, 0)
            norm(0, 1)
            hi_W(W_ORDER[0], 1)
            both(hi_T, 0, 0)
            both(hi_T, 0, 1)
            roots(0, 2)
            norm(0, 2)
            norm(0, 3)
            both(hi_T, 0, 2)
            both(hi_W, W_ORDER[1])
            hi_V(0, 0)
            both(hi_T, 0, 3)
            both(hi_W, W_ORDER[2])
            hi_V(0, 1)
            roots(0, 4)
            norm(0, 4)
            norm(0, 5)
            hi_Q(0, 0)
            hi_Q(0, 1)
            both(hi_T, 0, 4)
            norm(0, 6)
            hi_Q(0, 2)
            both(hi_T, 0, 5)
            norm(0, 7)
            hi_Q(0, 3)
            both(hi_T, 0, 6)
            both(hi_T, 0, 7)
            for i in range(TB):
                exp(0, i)
            act.wait_ge(qp_ready, 1)
            for i in range(4):
                scale_ctx(i)
            for c in range(4):
                hi_Q(1, c)
                scale_ctx(2 * c + 4)
                scale_ctx(2 * c + 5)
            hi_V(1, 0)
            scale_ctx(12)
            scale_ctx(13)
            hi_V(1, 1)
            act.wait_ge(mm_done, nth("V", 1, 1) + 1)
            act.dma_start(Wo_raw[:, :, :], wo).then_inc(Wo_loaded, 16)
            for i in range(TB):
                hi_PT(0, i)
            act.wait_ge(Wo_loaded, 16)
            nc.scalar.activation(Wo_hi[:, :, :], Wo_raw[:, :, :], ACT.Copy).then_inc(Wo_hi_done, 1)
            for i in range(TB):
                exp(1, i)
            hi_O(0, 0)
            scale_ctx(14)
            hi_O(0, 1)
            scale_ctx(15)
            for i in range(TB):
                hi_PT(1, i)
            hi_O(1, 0)
            hi_O(1, 1)
            roots(1, 0)
            norm(1, 0)
            norm(1, 1)
            centre_q1(0)
            norm(1, 2)
            centre_q1(1)
            copy_q1T(0)
            norm(1, 3)
            centre_q1(2)
            copy_q1T(1)
            centre_q1(3)
            roots(1, 4)
            copy_q1T(2)
            norm(1, 4)
            norm(1, 5)
            centre_q1(4)
            roots(1, 6)
            copy_q1T(3)
            centre_q1(5)
            norm(1, 6)
            norm(1, 7)
            copy_q1T(4)
            centre_q1(6)
            copy_q1T(5)
            centre_q1(7)
            copy_q1T(6)
            roots(2, 0)
            norm(2, 0)
            norm(2, 1)
            norm(2, 2)
            copy_q1T(7)
            roots(2, 4)
            both(hi_T, 2, 0)
            both(hi_T, 2, 1)
            norm(2, 3)
            norm(2, 4)
            norm(2, 5)
            hi_w(0, 0)
            both(hi_T, 2, 2)
            both(hi_T, 2, 3)
            both(hi_T, 2, 4)
            both(hi_T, 2, 5)
            roots(2, 6)
            norm(2, 6)
            norm(2, 7)
            both(hi_T, 2, 6)
            both(hi_T, 2, 7)
            hi_w(0, 1)
            for t in range(3):
                copy_maskT(0, t)
            hi_w(0, 2)
            hi_w(0, 3)
            copy_maskT(0, 3)
            hi_h(0, 0, 0)
            hi_h(0, 1, 0)
            hi_w(0, 4)
            hi_w(0, 5)
            copy_maskT(0, 4)
            hi_w(0, 6)
            copy_maskT(0, 5)
            copy_maskT(0, 6)
            copy_maskT(0, 7)
            for n, (j, half) in enumerate(HIDDEN_0[2:]):
                hi_h(0, j, half)
                if n == 2:
                    hi_w(0, 7)
            with act.Fori(0, NG - 1) as g:
                for t in range(NT - 1):
                    copy_maskT(g + 1, t)
                    if t == 2:
                        hi_w(g, NW)
                    if t == 4:
                        hi_w(g, NW + 1)
                hi_w(g + 1, 2)
                hi_w(g + 1, 3)
                copy_maskT(g + 1, NT - 1)
                both(hi_h, g + 1, 0)
                hi_w(g + 1, 4)
                hi_w(g + 1, 5)
                both(hi_h, g + 1, 1)
                hi_w(g + 1, 6)
                hi_w(g + 1, 7)
                for j, half in HIDDEN[4:]:
                    hi_h(g + 1, j, half)

        @block.vector
        def _(dve):
            chained = [0]

            def link(ins, off=0):
                chained[0] += 1
                ins.then_inc(vec, 1)
                dve.wait_ge(vec, chained[0] + off)

            def free(ins):
                ins.then_inc(bank_free, 1)

            def stats_of(t, kind=None):
                for n in range(2):
                    if kind:
                        dve.wait_ge(bank_free, nth(kind, t, n) + 1)
                    ins = nc.vector.bn_stats(stats[:, t, 6 * n:6 * n + 6], x[:, t, n * BANK:(n + 1) * BANK])
                link(ins)
                nc.vector.bn_aggr(mv[:, t, :], stats[:, t, :]).then_inc(mv_done, 1)

            def norm_scale(rnd, t):
                n = nth_chain(rnd, t)
                s = slice(t, t + CHAINS[n][2])
                mean, var = mv[:, s, 0], mv[:, s, 1]
                dve.wait_ge(sdev_ready, n + 1)
                link(nc.vector.reciprocal(rinv[:, s], sdev[:, s]))
                link(nc.vector.scalar_tensor_tensor(newt[:, s], rinv[:, s], -0.5, rinv[:, s], ALU.mult, ALU.mult))
                link(nc.vector.scalar_tensor_tensor(newt[:, s], var, EPS, newt[:, s], ALU.add, ALU.mult))
                link(nc.vector.scalar_tensor_tensor(rstd[:, s], newt[:, s], 1.5, rinv[:, s], ALU.add, ALU.mult))
                ins = nc.vector.scalar_tensor_tensor(nmr[:, s], mean, -1.0, rstd[:, s], ALU.mult, ALU.mult)
                if rnd == 1:
                    link(ins)
                    nc.vector.tensor_scalar(qmul[:, s], rstd[:, s], inv1, None, ALU.mult)
                    ins = nc.vector.tensor_scalar(qadd[:, s], nmr[:, s], inv1, qp[:, 1:2], ALU.mult, ALU.add)
                ins.then_inc(rstd_ready, 1)

            def lo_T(rnd, t):
                for h in range(2):
                    job = ("T1" if rnd == 0 else "T3", t, h)
                    dve.wait_ge(hi_done, nth_hi(*job) + 1)
                    k, m = slice(4 * h, 4 * h + 4), slice((t % TB) * P, (t % TB + 1) * P)
                    free(nc.vector.tensor_tensor(
                        xT_lo[t // TB][:, k, m], job_bank(*job)[:, :].rearrange("p (k m) -> p k m", k=4),
                        xT_hi[t // TB][:, k, m].bitcast(F32), ALU.subtract))

            def lo_Q(b, c):
                dve.wait_ge(hi_done, nth_hi("Q", b, c) + 1)
                hi, lo = (q_hi, q_lo) if c < DC else (k_hi, k_lo)
                free(nc.vector.scalar_tensor_tensor(
                    lo[b][:, c % DC, :], job_bank("Q", b, c)[:, :], bqk_s[:, c:c + 1],
                    hi[b][:, c % DC, :].bitcast(F32), ALU.add, ALU.subtract))

            def lo_V(b, i):
                pv = job_bank("V", b, i)[:, :].rearrange("p (t d) -> p t d", t=2)
                dve.wait_ge(mm_done, nth("V", b, i) + 1)
                nc.vector.tensor_tensor(
                    pv, pv, bv_b[:, :].rearrange("p (o d) -> p o d", o=1).to_broadcast([P, 2, HD]),
                    ALU.add).then_inc(vbias_added, 1)
                dve.wait_ge(hi_done, nth_hi("V", b, i) + 1)
                free(nc.vector.tensor_tensor(v_lo[b][:, 2 * i:2 * i + 2, :], pv,
                                             v_hi[b][:, 2 * i:2 * i + 2, :].bitcast(F32), ALU.subtract))

            def maxima(b):
                for i in range(TB):
                    n = b * TB + i
                    dve.wait_ge(mm_done, nth("S", b, i) + 1)
                    link(nc.vector.reduce_max(smax[:, n:n + 1], job_bank("S", b, i)[:, :], AX.X))
                    nc.vector.tensor_scalar(nbias[:, n:n + 1], smax[:, n:n + 1], -SCALE, None,
                                            ALU.mult).then_inc(nbias_ready, 1)

            def inverse_sums(b):
                for i in range(TB):
                    n = b * TB + i
                    dve.wait_ge(exp_done, n + 1)
                    free(nc.vector.reciprocal(pinv[:, n:n + 1], psum_row[:, n:n + 1]))

            def lo_PT(b, i):
                dve.wait_ge(hi_done, nth_hi("PT", b, i) + 1)
                m = slice(i * P, (i + 1) * P)
                free(nc.vector.tensor_tensor(pT_lo[:, :, m],
                                             job_bank("PT", b, i)[:, :].rearrange("p (k m) -> p k m", k=TB),
                                             pT_hi[:, :, m].bitcast(F32), ALU.subtract))

            def lo_O(b, c):
                dve.wait_ge(hi_done, nth_hi("O", b, c) + 1)
                free(nc.vector.tensor_tensor(oT_lo[:, c, :], job_bank("O", b, c)[:, :],
                                             oT_hi[:, c, :].bitcast(F32), ALU.subtract))

            def add_WO(t):
                dve.wait_ge(bo_added, t + 1)
                for n in range(2):
                    dve.wait_ge(mm_done, nth("WO", t, n) + 1)
                    c = slice(n * BANK, (n + 1) * BANK)
                    free(nc.vector.scalar_tensor_tensor(x[:, t, c], job_bank("WO", t, n)[:, :], pinv[:, t:t + 1],
                                                        x[:, t, c], ALU.mult, ALU.add))

            def round_ctx(i):
                r = ctx_slot[i % 4]
                dve.wait_ge(ctx_scaled, i + 1)
                nc.vector.tensor_scalar(r, r, QMAX, ROUND, ALU.min, ALU.add).then_inc(ctx_rounded, 1)

            def round_q1(t):
                r = xn[:, t % 2, :]
                dve.wait_ge(normed, NT + t + 1)
                nc.vector.tensor_scalar(r, r, QMAX, ROUND, ALU.min, ALU.add).then_inc(q1_rounded, 1)

            def copy_CB(b):
                for n in range(2):
                    dve.wait_ge(mm_done, nth("CB", b, n) + 1)
                    free(nc.vector.tensor_scalar(corr[:, b, n * BANK:(n + 1) * BANK], job_bank("CB", b, n)[:, :],
                                                 cs, None, ALU.mult))

            def row_bias(t):
                dve.wait_ge(q1_done, t + 1)
                nc.vector.tensor_scalar(rowbias[:, t:t + 1], q1_sum[:, t:t + 1], rb_mul, rb_add, ALU.mult,
                                        ALU.add).then_inc(rowbias_ready, 1)

            def add_XA(t):
                dve.wait_ge(corr_added, t + 1)
                for n in range(2):
                    c = slice(n * BANK, (n + 1) * BANK)
                    dve.wait_ge(mm_done, nth("XA", t, n) + 1)
                    free(nc.vector.scalar_tensor_tensor(x[:, t, c], job_bank("XA", t, n)[:, :], s12, x[:, t, c],
                                                        ALU.mult, ALU.add))

            def cut_u(b):
                if b == 0:
                    dve.wait_ge(mm_done, nth("U", 0) + 1)
                else:
                    dve.wait_ge(u1_done, 1)
                link(nc.vector.tensor_copy(u_hi[:, :].bitcast(F32R), u_bank[b][:, :]))
                ins = nc.vector.tensor_tensor(u_lo[:, :], u_bank[b][:, :], u_hi[:, :], ALU.subtract)
                if b == 0:
                    free(ins)
                    dve.wait_ge(bank_free, nth("U", 0) + 1)
                else:
                    link(ins)

            def stack_u(b):
                link(nc.vector.tensor_scalar(u_hi[:, :], u_hi[:, :], mslot[:, 0:1], None, ALU.mult))
                nc.vector.scalar_tensor_tensor(u_stack[:, b * SB:(b + 1) * SB], u_lo[:, :], mslot[:, 1:2],
                                               u_hi[:, :], ALU.mult, ALU.add).then_inc(u_stacked, 1)

            def cut_c2(g, off=0):
                dve.wait_ge(c2_loaded, g * (16 * SLOTS) + 16 * SLOTS)
                half = slice(P // 2, P)
                link(nc.vector.tensor_copy(c2_stack[:, :], c2_raw[:, :]), off)
                nc.vector.tensor_tensor(c2_stack[half, :], c2_raw[half, :], c2_stack[half, :].bitcast(F32),
                                        ALU.subtract).then_inc(c2_done, 1)

            def pick_first(g, t, off=0):
                sc = score_bank[:, :].rearrange("p (b w) -> p b w", w=BLK)
                cd = cand[:, :].rearrange("p (b w) -> p b w", w=BLK)
                pk = pick[:, :].rearrange("p (b w) -> p b w", w=BLK)
                wide = [P, GH // BLK, BLK]
                dve.wait_ge(score_done, g * NT + (t + 1))
                link(nc.vector.tensor_reduce(bmax[:, :], sc, AX.X, ALU.max), off)
                ins = nc.vector.tensor_tensor(
                    cd, sc, bmax[:, :].rearrange("p (b o) -> p b o", o=1).to_broadcast(wide), ALU.is_equal)
                ins.then_inc(score_read, 1)
                dve.wait_ge(score_read, g * NT + (t + 1))
                link(nc.vector.tensor_tensor(cand[:, :], cand[:, :], order[:, :], ALU.mult), off)
                link(nc.vector.tensor_reduce(cmax[:, :], cd, AX.X, ALU.max), off)
                if isinstance(g, int) and g == 0:
                    if t > 0:
                        dve.wait_ge(maskT_done, t)
                else:
                    dve.wait_ge(maskT_done, g * NT + t)
                nc.vector.tensor_tensor(pk, cd, cmax[:, :].rearrange("p (b o) -> p b o", o=1).to_broadcast(wide),
                                        ALU.is_equal).then_inc(pick_ready, 1)

            def relu_mask(g, j, half):
                pb = bank[2 * (j % 2) + half]
                dve.wait_ge(mm_done, hidden_nth(g, j, half) + 1)
                dve.wait_ge(maskT_copied, g * NT + TB * (half + 1))
                nc.vector.scalar_tensor_tensor(pb[:, :], pb[:, :], 0.0, maskT[:, j, half * SB:(half + 1) * SB],
                                               ALU.max, ALU.mult).then_inc(relu_masked, 1)

            def lo_h(g, j, half):
                dve.wait_ge(h_hi_done, g * 2 * GJ + (hidden_pos(g, j, half) + 1))
                s = slice(half * SB, (half + 1) * SB)
                free(nc.vector.tensor_tensor(h_lo[:, j, s], bank[2 * (j % 2) + half][:, :],
                                             h_hi[:, j, s].bitcast(F32), ALU.subtract))

            def add_unit(g, u):
                t, n = divmod(u, 2)
                c = slice(n * BANK, (n + 1) * BANK)
                dve.wait_ge(mm_done, unit_nth(g, u) + 1)
                free(nc.vector.tensor_tensor(x[:, t, c], bank[UNIT_BANK[u]][:, :], x[:, t, c], ALU.add))

            nc.vector.memset(eps[:, :], EPS).then_inc(eps_ready, 1)
            nc.vector.memset(uncentre[:, :], -(ROUND + CENTRE)).then_inc(uncentre_ready, 1)

            def first_stats(*tiles):
                for t in tiles:
                    dve.wait_ge(x_loaded[t], 16)
                    stats_of(t)

            first_stats(0, 1)
            norm_scale(0, 0)
            first_stats(2, 3)
            lo_T(0, 0)
            norm_scale(0, 2)
            lo_T(0, 1)
            dve.wait_ge(bias_loaded, 48)
            lo_T(0, 2)
            lo_V(0, 0)
            lo_T(0, 3)
            first_stats(4, 5, 6, 7)
            lo_V(0, 1)
            norm_scale(0, 4)
            lo_Q(0, 0)
            lo_Q(0, 1)
            lo_T(0, 4)
            lo_Q(0, 2)
            lo_T(0, 5)
            lo_Q(0, 3)
            lo_T(0, 6)
            lo_T(0, 7)
            dve.wait_ge(qp_loaded, 64)
            nc.vector.reciprocal(inv1, qp[:, 0:1])
            nc.vector.reciprocal(inv2, qp[:, 2:3])
            nc.vector.tensor_tensor(s12, qp[:, 0:1], qp[:, 2:3], ALU.mult)
            nc.vector.tensor_scalar(d1, qp[:, 1:2], -1.0, CENTRE, ALU.mult, ALU.add)
            link(nc.vector.tensor_scalar(d2, qp[:, 3:4], -1.0, CENTRE, ALU.mult, ALU.add))
            nc.vector.tensor_tensor(cs, s12, d1, ALU.mult)
            link(nc.vector.tensor_tensor(rb_mul, s12, d2, ALU.mult))
            nc.vector.scalar_tensor_tensor(rb_add, rb_mul, float(D), d1, ALU.mult, ALU.mult).then_inc(qp_ready, 1)
            maxima(0)
            inverse_sums(0)
            dve.wait_ge(ident_ready, 1)
            nc.vector.tensor_copy(id_b[:, :], id_f[:, :]).then_inc(id_b_ready, 1)
            slots = id_f[:, :].rearrange("p (a s c) -> p s a c", a=SLOTS // 2, s=2)
            for s in range(2):
                link(nc.vector.tensor_reduce(mslot[:, s:s + 1], slots[:, s], AX.XY, ALU.add))
            for i in range(4):
                round_ctx(i)
            for c in range(4):
                lo_Q(1, c)
                round_ctx(2 * c + 4)
                round_ctx(2 * c + 5)
            lo_V(1, 0)
            round_ctx(12)
            round_ctx(13)
            lo_V(1, 1)
            nc.vector.tensor_scalar(ones_r[:, :], id_f[:, :], 0.0, 1.0, ALU.mult, ALU.add).then_inc(ones_r_ready, 1)
            for i in range(TB):
                lo_PT(0, i)
            maxima(1)
            dve.wait_ge(Wo_hi_done, 1)
            nc.vector.tensor_tensor(Wo_lo[:, :, :], Wo_raw[:, :, :], Wo_hi[:, :, :].bitcast(F32),
                                    ALU.subtract).then_inc(Wo_lo_done, 1)
            dve.wait_ge(q2_done, KD)
            nc.vector.tensor_tensor(pairs[:, :, :], q2[0][:, 0:KD // 2, :], q2[0][:, KD // 2:KD, :],
                                    ALU.add).then_inc(pairs_added, 1)
            inverse_sums(1)
            lo_O(0, 0)
            lo_O(0, 1)
            for i in range(TB):
                lo_PT(1, i)
            round_ctx(14)
            round_ctx(15)
            for t in range(TB):
                add_WO(t)
                if t == TB - 1:
                    lo_O(1, 0)
                    lo_O(1, 1)
                stats_of(t, "WO")
            copy_CB(0)
            norm_scale(1, 0)
            add_WO(4)
            round_q1(0)
            stats_of(4, "WO")
            round_q1(1)
            add_WO(5)
            add_WO(6)
            round_q1(2)
            row_bias(0)
            stats_of(5, "WO")
            round_q1(3)
            row_bias(1)
            add_WO(7)
            copy_CB(1)
            norm_scale(1, 4)
            stats_of(6, "WO")
            row_bias(2)
            row_bias(3)
            round_q1(4)
            stats_of(7, "WO")
            row_bias(4)
            round_q1(5)
            norm_scale(1, 6)
            add_XA(0)
            add_XA(1)
            row_bias(5)
            round_q1(6)
            stats_of(0, "XA")
            row_bias(6)
            add_XA(2)
            round_q1(7)
            stats_of(1, "XA")
            stats_of(2, "XA")
            row_bias(7)
            dve.wait_ge(c1_loaded, 16)
            wide = c1_raw[:, :, :].rearrange("p k (o r) -> p k o r", o=1)
            link(nc.vector.tensor_copy(c1_cut[:, :, :, :], wide.to_broadcast([P, KD, SLOTS, RANK])))
            add_XA(3)
            stats_of(3, "XA")
            for i in range(2, SLOTS, 4):
                nc.vector.tensor_tensor(c1_cut[:, :, i:i + 2, :], wide.to_broadcast([P, KD, 2, RANK]),
                                        c1_cut[:, :, i:i + 2, :].bitcast(F32), ALU.subtract).then_inc(c1_done, 1)
            add_XA(4)
            norm_scale(2, 0)
            stats_of(4, "XA")
            add_XA(5)
            stats_of(5, "XA")
            add_XA(6)
            norm_scale(2, 4)
            stats_of(6, "XA")
            lo_T(2, 0)
            lo_T(2, 1)
            add_XA(7)
            lo_T(2, 2)
            lo_T(2, 3)
            stats_of(7, "XA")
            lo_T(2, 4)
            norm_scale(2, 6)
            lo_T(2, 5)
            cut_u(0)
            cut_c2(0)
            stack_u(0)
            lo_T(2, 6)
            lo_T(2, 7)
            dve.wait_ge(order_ready, 1)
            for t in range(TB):
                pick_first(0, t)
            cut_u(1)
            stack_u(1)
            for f in relu_mask, lo_h:
                for j, half in HIDDEN_0[:2]:
                    f(0, j, half)
            for t in range(TB, NT):
                pick_first(0, t)
            for f in relu_mask, lo_h:
                for j, half in HIDDEN_0[2:4]:
                    f(0, j, half)
            for j, half in HIDDEN_0[4:]:
                relu_mask(0, j, half)
                lo_h(0, j, half)

            before = chained[0]
            links = 1 + 3 * NT
            with dve.Fori(0, NG - 1) as g:
                off = g * links
                dve.wait_ge(score_done, g * NT + NT)
                cut_c2(g + 1, off)
                pick_first(g + 1, 0, off)
                for u in range(4):
                    add_unit(g, u)
                for t in range(1, NT - 1):
                    pick_first(g + 1, t, off)
                    add_unit(g, 2 * t + 2)
                    add_unit(g, 2 * t + 3)
                pick_first(g + 1, NT - 1, off)
                for j, half in HIDDEN:
                    relu_mask(g + 1, j, half)
                    lo_h(g + 1, j, half)
            assert chained[0] - before == links
            for u in range(2 * NT):
                add_unit(NG - 1, u)

        @block.tensor
        def _(pe):
            def take_bank(*job):
                n = nth(*job)
                if n >= RING:
                    pe.wait_ge(bank_free, n - RING + 1)

            def made(*job):
                pe.wait_ge(bank_free, nth(*job) + 1)

            def split_mm(dst, pairs, between=lambda n: None):
                for n, ((ah, al), (bh, bl)) in enumerate(pairs):
                    between(n)
                    nc.tensor.matmul(dst, ah, bh, start=n == 0, stop=False)
                    nc.tensor.matmul(dst, ah, bl, start=False, stop=False)
                    last = nc.tensor.matmul(dst, al, bh, start=False, stop=n == len(pairs) - 1)
                return last

            def transpose_norm(rnd, t):
                pe.wait_ge(normed, rnd * NT + t + 1)
                for h in range(2):
                    job = ("T1" if rnd == 0 else "T3", t, h)
                    take_bank(*job)
                    for k in range(4):
                        c = slice((4 * h + k) * P, (4 * h + k + 1) * P)
                        src = xn3[t % 4][:, c] if rnd == 2 else xn[:, t % 2, c]
                        last = nc.tensor.transpose(job_bank(*job)[:, k * P:(k + 1) * P], src, id_f[:, :])
                    last.then_inc(mm_done, 1)

            def project_qk(b, c):
                take_bank("Q", b, c)
                if b == 0:
                    pe.wait_ge(W_lo_done, 2 * W_ORDER.index(c // DC) + 2)
                m = slice((c % DC) * P, (c % DC + 1) * P)
                split_mm(job_bank("Q", b, c)[:, :],
                         [((W_hi[:, c // DC, k, m], W_lo[:, c // DC, k, m]), (xT_hi[b][:, k, :], xT_lo[b][:, k, :]))
                          for k in range(KD)]).then_inc(mm_done, 1)

            def project_v(b, i, halfway=lambda: None):
                take_bank("V", b, i)
                def second_half(n):
                    if n == KD // 2:
                        pe.wait_ge(W_lo_done, 2)

                for s in range(2):
                    if s == 1:
                        halfway()
                    if b == 0:
                        pe.wait_ge(W_lo_done, 1)
                        made("T1", 2 * i + s, 1)
                    m = slice((2 * i + s) * P, (2 * i + s + 1) * P)
                    last = split_mm(job_bank("V", b, i)[:, s * HD:(s + 1) * HD],
                                    [((xT_hi[b][:, k, m], xT_lo[b][:, k, m]), (W_hi[:, 2, k, :], W_lo[:, 2, k, :]))
                                     for k in range(KD)], second_half)
                last.then_inc(mm_done, 1)

            def scores(b, i):
                take_bank("S", b, i)
                if i == 0:
                    made("Q", b, 3)
                m = slice(i * P, (i + 1) * P)
                split_mm(job_bank("S", b, i)[:, :],
                         [((q_hi[b][:, c, m], q_lo[b][:, c, m]), (k_hi[b][:, c, :], k_lo[b][:, c, :]))
                          for c in range(DC)]).then_inc(mm_done, 1)

            def transpose_probs(b, i):
                take_bank("PT", b, i)
                pe.wait_ge(exp_done, b * TB + i + 1)
                for k in range(TB):
                    last = nc.tensor.transpose(job_bank("PT", b, i)[:, k * P:(k + 1) * P],
                                               probs[:, i, k * P:(k + 1) * P], id_f[:, :])
                last.then_inc(mm_done, 1)

            def mix_values(b, c):
                take_bank("O", b, c)
                if c == 0:
                    made("PT", b, TB - 1)
                m = slice(c * P, (c + 1) * P)
                split_mm(job_bank("O", b, c)[:, :],
                         [((v_hi[b][:, k, m], v_lo[b][:, k, m]), (pT_hi[:, k, :], pT_lo[:, k, :]))
                          for k in range(TB)]).then_inc(mm_done, 1)

            def project_out(t):
                if t == 0:
                    pe.wait_ge(Wo_lo_done, 1)
                if t % TB == 0:
                    made("O", t // TB, 1)
                m = slice((t % TB) * P, (t % TB + 1) * P)
                for n in range(2):
                    take_bank("WO", t, n)
                    c = slice(n * BANK, (n + 1) * BANK)
                    split_mm(job_bank("WO", t, n)[:, :],
                             [((oT_hi[:, d, m], oT_lo[:, d, m]), (Wo_hi[:, d, c], Wo_lo[:, d, c]))
                              for d in range(DC)]).then_inc(mm_done, 1)

            def column_sums(b):
                pe.wait_ge(ones_r_ready, 1)
                pe.wait_ge(q2_summed, b + 1)
                for n in range(2):
                    take_bank("CB", b, n)
                    nc.tensor.matmul(job_bank("CB", b, n)[:, :], ones_r[:, :], q2_sum[:, b, n * BANK:(n + 1) * BANK],
                                     start=True, stop=True).then_inc(mm_done, 1)

            def transpose_q1(t):
                pe.wait_ge(q1_done, t + 1)
                if t > 0:
                    pe.wait_ge(q1T_copied, t)
                for k in range(KD):
                    last = nc.tensor.transpose(q1T_bank[:, k * P:(k + 1) * P], q1[:, t % 4, k * P:(k + 1) * P],
                                               id_b[:, :])
                last.then_inc(q1T_done, 1)

            def quantised_product(t, halfway=lambda: None):
                pe.wait_ge(q1T_copied, t + 1)
                if t == 0:
                    pe.wait_ge(q2_done, KD)
                if t == TB:
                    pe.wait_ge(q2_done, 2 * KD)
                for n in range(2):
                    if n == 1:
                        halfway()
                    take_bank("XA", t, n)
                    for k in range(KD):
                        last = nc.tensor.matmul(job_bank("XA", t, n)[:, :], q1T[:, t % 2, k, :],
                                                q2[t // TB][:, k, n * BANK:(n + 1) * BANK],
                                                start=k == 0, stop=k == KD - 1)
                    last.then_inc(mm_done, 1)

            def rank_projection(b, between=lambda n: None):
                if b == 0:
                    take_bank("U", 0)
                else:
                    pe.wait_ge(bank_free, last_in(U1_BANK) + 1)
                made("T3", TB * b + 3, 1)
                if b == 0:
                    pe.wait_ge(c1_done, SLOTS // 4)
                for k in range(KD):
                    between(k)
                    for part in (xT_hi, xT_lo):
                        last = nc.tensor.matmul(u_bank[b][:, :], c1_cut[:, k].rearrange("p s r -> p (s r)"),
                                                part[b][:, k, :], start=k == 0 and part is xT_hi,
                                                stop=k == KD - 1 and part is xT_lo)
                last.then_inc(u1_done if b else mm_done, 1)

            def score_tile(g, t):
                if t == 0:
                    pe.wait_ge(c2_done, g + 1)
                if isinstance(g, int) and g == 0:
                    if t == 0:
                        pe.wait_ge(u_stacked, 1)
                    else:
                        pe.wait_ge(score_read, t)
                    if t == TB:
                        pe.wait_ge(u_stacked, 2)
                else:
                    pe.wait_ge(score_read, g * NT + t)
                nc.tensor.matmul(score_bank[:, :], u_stack[:, t * P:(t + 1) * P], c2_stack[:, :],
                                 start=True, stop=True).then_inc(score_done, 1)

            def transpose_pick(g, t):
                pe.wait_ge(pick_ready, g * NT + (t + 1))
                if isinstance(g, int) and g == 0:
                    if t > 0:
                        pe.wait_ge(maskT_copied, t)
                else:
                    pe.wait_ge(maskT_copied, g * NT + t)
                for j in range(GJ):
                    last = nc.tensor.transpose(maskT_bank[:, j * P:(j + 1) * P], pick[:, j * P:(j + 1) * P], id_b[:, :])
                last.then_inc(maskT_done, 1)

            def hidden(g, j, half, between=lambda n: None):
                b = 2 * (j % 2) + half
                pe.wait_ge(w_lo_done, g * NW + (WSEQ.index(("w1", j)) + 1))
                if j >= 2:
                    pe.wait_ge(bank_free, hidden_nth(g, j - 2, half) + 1)
                elif isinstance(g, int) and g == 0:
                    pe.wait_ge(bank_free, last_in(b) + 1)
                else:
                    pe.wait_ge(bank_free, unit_nth(g, prev_unit_on(b)) + (1 - PER))
                pairs = [((w1_hi[:, j % 2, k, :], w1_lo[:, j % 2, k, :]), (xT_hi[half][:, k, :], xT_lo[half][:, k, :]))
                         for k in range(KD)]
                split_mm(bank[b][:, :], pairs, between).then_inc(mm_done, 1)

            def unit_part(u, js):
                t, n = divmod(u, 2)
                m, c = slice(t * P, (t + 1) * P), slice(n * BANK, (n + 1) * BANK)
                dst = bank[UNIT_BANK[u]][:, :]
                for j in js:
                    nc.tensor.matmul(dst, h_hi[:, j, m], w2_hi[:, j, c], start=j == 0, stop=False)
                    nc.tensor.matmul(dst, h_hi[:, j, m], w2_lo[:, j, c], start=False, stop=False)
                    last = nc.tensor.matmul(dst, h_lo[:, j, m], w2_hi[:, j, c], start=False, stop=j == GJ - 1)
                return last

            def take_unit_bank(g, u):
                if u >= 6:
                    pe.wait_ge(bank_free, unit_nth(g, u - 6) + 1)
                elif UNIT_BANK[u] < 4:
                    b = UNIT_BANK[u]
                    pe.wait_ge(bank_free, hidden_nth(g, GJ - 2 + b // 2, b % 2) + 1)

            def outputs(g, last_group):
                pe.wait_ge(w_lo_done, g * NW + (WSEQ.index(("w2", 2)) + 1))
                for u in range(4):
                    take_unit_bank(g, u)
                    for j in range(GJ - 1):
                        if u == 0:
                            pe.wait_ge(bank_free, hidden_nth(g, max(j, 1), 1) + 1)
                        unit_part(u, [j])
                    if u == 1 and not last_group:
                        score_tile(g + 1, 0)
                pe.wait_ge(w_lo_done, g * NW + NW)
                pe.wait_ge(bank_free, hidden_nth(g, GJ - 1, 1) + 1)
                for u in range(4):
                    unit_part(u, [GJ - 1]).then_inc(mm_done, 1)
                for u in range(4, 2 * NT):
                    if u % 2 == 0 and not last_group:
                        score_tile(g + 1, u // 2 - 1)
                        transpose_pick(g + 1, u // 2 - 2)
                    take_unit_bank(g, u)
                    unit_part(u, range(GJ)).then_inc(mm_done, 1)
                if not last_group:
                    score_tile(g + 1, NT - 1)
                    transpose_pick(g + 1, NT - 2)

            pe.wait_ge(ident_ready, 1)
            transpose_norm(0, 0)
            transpose_norm(0, 1)
            project_v(0, 0, lambda: transpose_norm(0, 2))
            transpose_norm(0, 3)
            project_v(0, 1)
            project_qk(0, 0)
            project_qk(0, 1)
            transpose_norm(0, 4)
            project_qk(0, 2)
            transpose_norm(0, 5)
            project_qk(0, 3)
            transpose_norm(0, 6)
            transpose_norm(0, 7)
            for i in range(TB):
                scores(0, i)
            made("T1", NT - 1, 1)
            for c in range(4):
                project_qk(1, c)
            project_v(1, 0)
            project_v(1, 1)
            for i in range(TB):
                transpose_probs(0, i)
            for i in range(TB):
                scores(1, i)
            mix_values(0, 0)
            mix_values(0, 1)
            for i in range(TB):
                transpose_probs(1, i)
            for t in range(TB):
                project_out(t)
            mix_values(1, 0)
            mix_values(1, 1)
            column_sums(0)
            project_out(4)
            project_out(5)
            project_out(6)
            pe.wait_ge(id_b_ready, 1)
            transpose_q1(0)
            project_out(7)
            transpose_q1(1)
            column_sums(1)
            for t in range(6):
                quantised_product(t, lambda: transpose_q1(t + 2))
            quantised_product(6)
            transpose_norm(2, 0)
            transpose_norm(2, 1)
            quantised_product(7)
            for t in range(2, 6):
                transpose_norm(2, t)
            rank_projection(0)
            transpose_norm(2, 6)
            transpose_norm(2, 7)

            def masks_in(steps):
                def between(n):
                    if n in steps:
                        picked, scored = steps[n]
                        if picked is not None:
                            transpose_pick(0, picked)
                        if scored is not None:
                            score_tile(0, scored)
                return between

            hidden(0, 0, 0, masks_in({4: (None, 0)}))
            hidden(0, 1, 0, masks_in({1: (None, 1), 5: (0, 2)}))
            rank_projection(1, masks_in({1: (1, 3), 5: (2, None)}))
            hidden(0, 0, 1, masks_in({3: (3, None)}))
            hidden(0, 1, 1, masks_in({0: (None, 4), 5: (None, 5)}))
            hidden(0, 2, 0, masks_in({1: (4, 6), 4: (5, 7)}))
            hidden(0, 3, 0, masks_in({1: (6, None), 3: (7, None)}))
            hidden(0, 2, 1)
            hidden(0, 3, 1)
            with pe.Fori(0, NG - 1) as g:
                outputs(g, False)
                for j, half in HIDDEN:
                    hidden(g + 1, j, half)
                    if (j, half) == (0, 0):
                        transpose_pick(g + 1, NT - 1)
            outputs(NG - 1, True)


def kernel(x, ctx_4096, L0_attn_Wqkv, L0_attn_bqkv, L0_attn_Wo, L0_attn_bo, L0_xattn_x1_scale, L0_xattn_x1_zp,
           L0_xattn_x2_scale, L0_xattn_x2_zp, L0_ffn_c1_w, L0_ffn_c2_w, L0_ffn_w1, L0_ffn_w2t):
    import numpy as np
    import concourse.bacc as bacc
    from concourse.bass_utils import run_bass_kernel_spmd

    x, ctx = np.asarray(x), np.asarray(ctx_4096)
    wqkv, bqkv = np.asarray(L0_attn_Wqkv), np.asarray(L0_attn_bqkv)
    B, S, D = x.shape
    HD = D // 4
    nt, kd, ni = B * S // P, D // P, L0_ffn_w1.shape[0] // P
    c1, c2, w1, w2 = (np.asarray(a) for a in (L0_ffn_c1_w, L0_ffn_c2_w, L0_ffn_w1, L0_ffn_w2t))
    rank = c1.shape[0]
    laid = {
        "x_in": x.reshape(nt, P, D),
        "ctx_in": ctx.reshape(B * kd, P, D),
        "wqkv": wqkv.reshape(kd, P, 3, HD).transpose(2, 1, 0, 3),
        "bqk": bqkv[:2 * HD].reshape(2 * HD // P, P).T,
        "bv": bqkv[2 * HD:],
        "wo": np.asarray(L0_attn_Wo).reshape(HD // P, P, D).transpose(1, 0, 2),
        "bo": np.asarray(L0_attn_bo),
        "s1": np.asarray(L0_xattn_x1_scale), "z1": np.asarray(L0_xattn_x1_zp),
        "s2": np.asarray(L0_xattn_x2_scale), "z2": np.asarray(L0_xattn_x2_zp),
        "c1": c1.T.reshape(kd, P, rank).transpose(1, 0, 2),
        "c2": c2.reshape(-1, BANK, rank).transpose(0, 2, 1),
        "w1": w1.reshape(ni, P, kd, P).transpose(0, 3, 2, 1).reshape(ni, P, D),
        "w2": w2.reshape(ni, P, D),
    }
    arrays = {n: np.ascontiguousarray(a) for n, a in laid.items()}
    nc = bacc.Bacc("TRN2", target_bir_lowering=False, num_devices=1)
    args = [nc.dram_tensor(n, a.shape, mybir.dt.from_np(a.dtype), kind="ExternalInput").ap() for n, a in arrays.items()]
    out = nc.dram_tensor("out", (nt, P, D), F32, kind="ExternalOutput").ap()
    decoder_layer(nc, *args, out)
    r = run_bass_kernel_spmd(nc, [arrays], core_ids=[0])
    return r.results[0]["out"].reshape(B, S, D)
```
